# Optimizing a Trainium2 kernel written in Bass

```python
import numpy as np
import jax
import jax.numpy as jnp

def _softmax(x, axis=-1):
    return jax.nn.softmax(x, axis=axis)

def _gelu(x):
    return jax.nn.gelu(x, approximate=True)

def _silu(x):
    return jax.nn.silu(x)

def _sigmoid(x):
    return jax.nn.sigmoid(x)

def _layernorm(x, axis=-1, eps=1e-05):
    m = jnp.mean(x, axis=axis, keepdims=True)
    v = jnp.var(x, axis=axis, keepdims=True)
    return (x - m) / jnp.sqrt(v + eps)

def _scatter_add(tgt, idx, src, axis=0):
    return tgt.at[idx].add(src)

def _segment_sum(src, seg, n):
    return jax.ops.segment_sum(src, seg, n)
kernel_name = 'mk_flamingo_gated_d2_seqx_r4_c57880'

def setup_inputs(seed: int=0):
    np.random.seed(seed)
    _w = jnp.asarray

    def _rec_inputs():
        import jax
        import jax.numpy as jnp
        _rk = jax.random.key(seed)
        x = -0.0002928 + 1 * jax.random.normal(jax.random.fold_in(_rk, 1), (8, 512, 256), jnp.float32)
        _lenS = 512 - jax.random.randint(jax.random.fold_in(_rk, 7), (8,), 0, max(1, 512 // 4) + 1, jnp.int32)
        _lenS2 = 512 - jax.random.randint(jax.random.fold_in(_rk, 8), (8,), 0, max(1, 512 // 4) + 1, jnp.int32)
        _ctx_1024P = jax.random.normal(jax.random.fold_in(_rk, 11), (8, 16, 256), jnp.float32)
        _ctx_1024c = jax.random.dirichlet(jax.random.fold_in(_rk, 511), 0.3 * jnp.ones((16,), jnp.float32), (8, 512))
        _ctx_1024t = jnp.einsum('bsk,bkd->bsd', _ctx_1024c, _ctx_1024P)
        _ctx_1024t = _ctx_1024t * jax.lax.rsqrt(jnp.mean(jnp.square(_ctx_1024t)) + 1e-12) * 0.953939
        ctx_1024 = -1.39393e-06 + 0.999914 * (_ctx_1024t + 0.3 * jax.random.normal(jax.random.fold_in(_rk, 611), (8, 512, 256), jnp.float32))
        _g = jax.random.normal(jax.random.fold_in(_rk, 9001), (2, 2), jnp.float32)
        _g = jnp.sign(_g) * jnp.maximum(jnp.abs(_g), 1.0) + (_g == 0) * 1.0
        g_xattn = _g[0]
        g_ffn = _g[1]
        return (x, ctx_1024, g_xattn, g_ffn)
    x, ctx_1024, g_xattn, g_ffn = _rec_inputs()

    def _L0_xattn_setup():
        import jax, jax.numpy as jnp
        import numpy as np
        EPS_BACKEND = 1e-06
        NORM_EPS = 1e-06
        NUM_HEADS = 4

        def _mlstm_forward(q, k, v, ig_kernel, ig_bias, fg_kernel, fg_bias, outnorm_weight):
            B, S, E = q.shape
            NH = ig_bias.shape[0]
            DH = E // NH
            gate_input = jnp.concatenate([q, k, v], axis=-1)
            igate = gate_input @ ig_kernel + ig_bias
            fgate = gate_input @ fg_kernel + fg_bias
            qh = q.reshape(B, S, NH, DH).transpose(0, 2, 1, 3)
            kh = k.reshape(B, S, NH, DH).transpose(0, 2, 1, 3)
            vh = v.reshape(B, S, NH, DH).transpose(0, 2, 1, 3)
            ig = igate.transpose(0, 2, 1)
            fg = fgate.transpose(0, 2, 1)
            log_fg = jax.nn.log_sigmoid(fg)
            cums = jnp.concatenate([jnp.zeros((B, NH, 1), log_fg.dtype), jnp.cumsum(log_fg, axis=-1)], axis=-1)
            fg_mat = cums[..., :, None] - cums[..., None, :]
            mask = jnp.tril(jnp.ones((S + 1, S + 1), bool))
            fg_mat = jnp.where(mask, fg_mat, -jnp.inf)[..., 1:, 1:]
            log_D = fg_mat + ig[..., None, :]
            max_log_D = jnp.max(log_D, axis=-1, keepdims=True)
            D = jnp.exp(log_D - max_log_D)
            qk = jnp.einsum('bnsd,bntd->bnst', qh, kh) / jnp.sqrt(jnp.float32(DH))
            C = qk * D
            normalizer = jnp.maximum(jnp.abs(C.sum(-1, keepdims=True)), jnp.exp(-max_log_D))
            h = jnp.einsum('bnst,bntd->bnsd', C / (normalizer + EPS_BACKEND), vh)
            h = h.transpose(0, 2, 1, 3)
            mean = h.mean(-1, keepdims=True)
            var = h.var(-1, keepdims=True)
            hn = (h - mean) * jax.lax.rsqrt(var + NORM_EPS) * outnorm_weight
            return hn.reshape(B, S, E)
        key = jax.random.key(seed)
        ks = jax.random.split(key, 8)
        B, S, E, NH = (2, 512, 256, NUM_HEADS)
        DH = E // NH
        q = jax.random.normal(ks[0], (B, S, E), jnp.float32)
        k = jax.random.normal(ks[1], (B, S, E), jnp.float32)
        v = jax.random.normal(ks[2], (B, S, E), jnp.float32)
        ig_kernel = jax.random.normal(ks[3], (3 * E, NH), jnp.float32) * 0.02
        fg_kernel = jax.random.normal(ks[4], (3 * E, NH), jnp.float32) * 0.02
        ig_bias = jax.random.normal(ks[5], (NH,), jnp.float32) * 0.1
        fg_bias = jnp.linspace(3.0, 6.0, NH, dtype=jnp.float32)
        outnorm_weight = jnp.ones((NH, DH), jnp.float32)
        return {'q': q, 'k': k, 'v': v, 'ig_kernel': ig_kernel, 'ig_bias': ig_bias, 'fg_kernel': fg_kernel, 'fg_bias': fg_bias, 'outnorm_weight': outnorm_weight}
    _L0_xattn_all = _L0_xattn_setup()
    _L0_xattn_in = {k: v for k, v in _L0_xattn_all.items() if k in ('ig_kernel', 'ig_bias', 'fg_kernel', 'fg_bias', 'outnorm_weight')}
    del _L0_xattn_all

    def _L0_ffn_setup():
        import math
        import jax, jax.numpy as jnp
        import numpy as np
        D_MODEL = 256
        NUM_EXPERTS = 8
        D_FF_EXPERT = max(64, int(D_MODEL * 4 * 0.25))
        THRESHOLD = 0.9
        CAP_FACTOR = 1.0
        INIT_STD = 0.02

        def _xmoe_route(probs):
            N, E = probs.shape
            order = jnp.argsort(-probs, axis=-1)
            p_sorted = jnp.take_along_axis(probs, order, axis=-1)
            csum = jnp.cumsum(p_sorted, axis=-1)
            reached = (csum >= THRESHOLD).at[:, -1].set(True)
            k_idx = jnp.argmax(reached, axis=-1)
            select_prefix = jnp.arange(E)[None, :] <= k_idx[:, None]
            rows = jnp.arange(N)[:, None]
            assign_mask = jnp.zeros((N, E), dtype=bool).at[rows, order].set(select_prefix)
            rank = jnp.arange(1, E + 1, dtype=probs.dtype)[None, :]
            R_sorted = jnp.where(select_prefix, p_sorted - rank, jnp.full_like(p_sorted, -1000000000.0))
            R = jnp.zeros((N, E), dtype=probs.dtype).at[rows, order].set(R_sorted)
            capacity = int(math.ceil(N / E) * CAP_FACTOR)
            C = min(capacity, N)
            tok_order = jnp.argsort(-R, axis=0)
            topC = tok_order[:C, :]
            keep = jnp.zeros((N, E), dtype=bool).at[topC, jnp.arange(E)[None, :]].set(True)
            final_mask = assign_mask & keep
            return jnp.where(final_mask, probs, jnp.zeros_like(probs))
        key = jax.random.key(seed)
        k_x, k_g, k_w1, k_w2 = jax.random.split(key, 4)
        B, T = (4, 512)
        x = jax.random.normal(k_x, (B, T, D_MODEL), dtype=jnp.float32)
        bound = 1.0 / math.sqrt(D_MODEL)
        gate_w = jax.random.uniform(k_g, (NUM_EXPERTS, D_MODEL), minval=-bound, maxval=bound, dtype=jnp.float32)
        w1 = INIT_STD * jax.random.normal(k_w1, (NUM_EXPERTS, D_FF_EXPERT, D_MODEL), dtype=jnp.float32)
        w2 = INIT_STD * jax.random.normal(k_w2, (NUM_EXPERTS, D_MODEL, D_FF_EXPERT), dtype=jnp.float32)
        return {'x': x, 'gate_w': gate_w, 'w1': w1, 'w2': w2}
    _L0_ffn_all = _L0_ffn_setup()
    _L0_ffn_in = {k: v for k, v in _L0_ffn_all.items() if k in ('gate_w', 'w1', 'w2')}
    del _L0_ffn_all

    def _L1_xattn_setup():
        import jax, jax.numpy as jnp
        import numpy as np
        B, L, D = (4, 1024, 256)
        key = jax.random.key(seed)
        k1, k2 = jax.random.split(key)
        Q = jax.random.normal(k1, (B, L, D), dtype=jnp.float32)
        K = jax.random.normal(k2, (B, L, D), dtype=jnp.float32)
        return {'Q': Q, 'K': K}
    _L1_xattn_all = _L1_xattn_setup()
    _L1_xattn_in = {k: v for k, v in _L1_xattn_all.items() if k in ()}
    del _L1_xattn_all

    def _L1_ffn_setup():
        import jax, jax.numpy as jnp
        import numpy as np
        DIM = 256
        DEPTH = 2
        HEADS = 8
        DIM_HEAD = 64
        WINDOW = 128
        INNER = HEADS * DIM_HEAD
        HID = int(DIM * 4 * 2 / 3)
        B, N = (2, 2048)
        QK_SCALE = 8.0

        def shift_token(t):
            t1, t2 = jnp.split(t, 2, axis=-1)
            t2 = jnp.pad(t2, ((0, 0), (1, 0), (0, 0)))[:, :-1]
            return jnp.concatenate([t1, t2], axis=-1)

        def l2norm(t):
            return t / jnp.clip(jnp.linalg.norm(t, axis=-1, keepdims=True), 1e-12)

        def rotate_half(x):
            x1, x2 = jnp.split(x, 2, axis=-1)
            return jnp.concatenate([-x2, x1], axis=-1)

        def rotary_xpos(q, k):
            n = q.shape[-2]
            half_idx = jnp.arange(0, DIM_HEAD, 2, dtype=jnp.float32)
            inv_freq = 1.0 / 10000.0 ** (half_idx / DIM_HEAD)
            t = jnp.arange(n, dtype=jnp.float32)
            freqs = t[:, None] * inv_freq[None, :]
            freqs = jnp.concatenate([freqs, freqs], axis=-1)
            base = (half_idx + 0.4 * DIM_HEAD) / (1.4 * DIM_HEAD)
            power = (t - n // 2) / float(WINDOW // 2)
            scale = base[None, :] ** power[:, None]
            scale = jnp.concatenate([scale, scale], axis=-1)
            cos, sin = (jnp.cos(freqs), jnp.sin(freqs))
            q = q * cos * scale + rotate_half(q) * sin * scale
            k = k * cos / scale + rotate_half(k) * sin / scale
            return (q, k)

        def local_attention(q, k, v):
            b, h, n, d = q.shape
            w = n // WINDOW
            bq = q.reshape(b, h, w, WINDOW, d) * QK_SCALE
            bk = k.reshape(b, h, w, WINDOW, d)
            bv = v.reshape(b, h, w, WINDOW, d)

            def look_around(t):
                p = jnp.pad(t, ((0, 0), (0, 0), (1, 0), (0, 0), (0, 0)))
                return jnp.concatenate([p[:, :, :w], p[:, :, 1:]], axis=3)
            bk, bv = (look_around(bk), look_around(bv))
            bt = jnp.arange(n).reshape(w, WINDOW)
            btp = jnp.pad(bt, ((1, 0), (0, 0)), constant_values=-1)
            btk = jnp.concatenate([btp[:w], btp[1:]], axis=1)
            sim = jnp.einsum('bhwid,bhwjd->bhwij', bq, bk)
            i = bt[:, :, None]
            j = btk[:, None, :]
            mask = (i < j) | (i > j + WINDOW) | (j == -1)
            sim = jnp.where(mask, -jnp.finfo(sim.dtype).max, sim)
            attn = jax.nn.softmax(sim, axis=-1)
            out = jnp.einsum('bhwij,bhwjd->bhwid', attn, bv)
            return out.reshape(b, h, n, d)

        def _layer(x, wqkv, qs, ksc, wo, lg, lb, w1, b1, w2, b2):
            b, n, _ = x.shape
            h = shift_token(x)
            qkv = h @ wqkv
            q, k, v = jnp.split(qkv, 3, axis=-1)
            to_heads = lambda t: t.reshape(b, n, HEADS, DIM_HEAD).transpose(0, 2, 1, 3)
            q, k, v = (to_heads(q), to_heads(k), to_heads(v))
            q = l2norm(q) * qs
            k = l2norm(k) * ksc
            q, k = rotary_xpos(q, k)
            o = local_attention(q, k, v)
            o = o.transpose(0, 2, 1, 3).reshape(b, n, INNER)
            x = x + o @ wo
            h = shift_token(x)
            mu = h.mean(-1, keepdims=True)
            var = h.var(-1, keepdims=True)
            h = (h - mu) / jnp.sqrt(var + 1e-05) * lg + lb
            h = h @ w1 + b1
            a, g = jnp.split(h, 2, axis=-1)
            h = a * jax.nn.gelu(g, approximate=False)
            x = x + h @ w2 + b2
            return x
        key = jax.random.key(seed)
        ks = jax.random.split(key, 6)
        return {'x': jax.random.normal(ks[0], (B, N, DIM), jnp.float32), 'wqkv': jax.random.normal(ks[1], (DEPTH, DIM, 3 * INNER), jnp.float32) * 0.02, 'q_scale': jnp.ones((DEPTH, DIM_HEAD), jnp.float32), 'k_scale': jnp.ones((DEPTH, DIM_HEAD), jnp.float32), 'wo': jax.random.normal(ks[2], (DEPTH, INNER, DIM), jnp.float32) * 0.02, 'ln_g': jnp.ones((DEPTH, DIM), jnp.float32), 'ln_b': jnp.zeros((DEPTH, DIM), jnp.float32), 'w1': jax.random.normal(ks[3], (DEPTH, DIM, 2 * HID), jnp.float32) * 0.02, 'b1': jnp.zeros((DEPTH, 2 * HID), jnp.float32), 'w2': jax.random.normal(ks[4], (DEPTH, HID, DIM), jnp.float32) * 0.02, 'b2': jnp.zeros((DEPTH, DIM), jnp.float32)}
    _L1_ffn_all = _L1_ffn_setup()
    _L1_ffn_in = {k: v for k, v in _L1_ffn_all.items() if k in ('wqkv', 'q_scale', 'k_scale', 'wo', 'ln_g', 'ln_b', 'w1', 'b1', 'w2', 'b2')}
    del _L1_ffn_all
    return {'x': x, 'ctx_1024': ctx_1024, 'g_xattn': g_xattn, 'g_ffn': g_ffn, 'L0_xattn_ig_kernel': _L0_xattn_in['ig_kernel'], 'L0_xattn_ig_bias': _L0_xattn_in['ig_bias'], 'L0_xattn_fg_kernel': _L0_xattn_in['fg_kernel'], 'L0_xattn_fg_bias': _L0_xattn_in['fg_bias'], 'L0_xattn_outnorm_weight': _L0_xattn_in['outnorm_weight'], 'L0_ffn_gate_w': _L0_ffn_in['gate_w'], 'L0_ffn_w1': _L0_ffn_in['w1'], 'L0_ffn_w2': _L0_ffn_in['w2'], 'L1_ffn_wqkv': _L1_ffn_in['wqkv'], 'L1_ffn_q_scale': _L1_ffn_in['q_scale'], 'L1_ffn_k_scale': _L1_ffn_in['k_scale'], 'L1_ffn_wo': _L1_ffn_in['wo'], 'L1_ffn_ln_g': _L1_ffn_in['ln_g'], 'L1_ffn_ln_b': _L1_ffn_in['ln_b'], 'L1_ffn_w1': _L1_ffn_in['w1'], 'L1_ffn_b1': _L1_ffn_in['b1'], 'L1_ffn_w2': _L1_ffn_in['w2'], 'L1_ffn_b2': _L1_ffn_in['b2']}

def reference(x, ctx_1024, g_xattn, g_ffn, L0_xattn_ig_kernel, L0_xattn_ig_bias, L0_xattn_fg_kernel, L0_xattn_fg_bias, L0_xattn_outnorm_weight, L0_ffn_gate_w, L0_ffn_w1, L0_ffn_w2, L1_ffn_wqkv, L1_ffn_q_scale, L1_ffn_k_scale, L1_ffn_wo, L1_ffn_ln_g, L1_ffn_ln_b, L1_ffn_w1, L1_ffn_b1, L1_ffn_w2, L1_ffn_b2):
    import jax
    import jax.numpy as jnp

    def _L0_xattn_ref(q, k, v, ig_kernel, ig_bias, fg_kernel, fg_bias, outnorm_weight):
        import jax, jax.numpy as jnp
        import numpy as np
        EPS_BACKEND = 1e-06
        NORM_EPS = 1e-06
        NUM_HEADS = 4

        def _mlstm_forward(q, k, v, ig_kernel, ig_bias, fg_kernel, fg_bias, outnorm_weight):
            B, S, E = q.shape
            NH = ig_bias.shape[0]
            DH = E // NH
            gate_input = jnp.concatenate([q, k, v], axis=-1)
            igate = gate_input @ ig_kernel + ig_bias
            fgate = gate_input @ fg_kernel + fg_bias
            qh = q.reshape(B, S, NH, DH).transpose(0, 2, 1, 3)
            kh = k.reshape(B, S, NH, DH).transpose(0, 2, 1, 3)
            vh = v.reshape(B, S, NH, DH).transpose(0, 2, 1, 3)
            ig = igate.transpose(0, 2, 1)
            fg = fgate.transpose(0, 2, 1)
            log_fg = jax.nn.log_sigmoid(fg)
            cums = jnp.concatenate([jnp.zeros((B, NH, 1), log_fg.dtype), jnp.cumsum(log_fg, axis=-1)], axis=-1)
            fg_mat = cums[..., :, None] - cums[..., None, :]
            mask = jnp.tril(jnp.ones((S + 1, S + 1), bool))
            fg_mat = jnp.where(mask, fg_mat, -jnp.inf)[..., 1:, 1:]
            log_D = fg_mat + ig[..., None, :]
            max_log_D = jnp.max(log_D, axis=-1, keepdims=True)
            D = jnp.exp(log_D - max_log_D)
            qk = jnp.einsum('bnsd,bntd->bnst', qh, kh) / jnp.sqrt(jnp.float32(DH))
            C = qk * D
            normalizer = jnp.maximum(jnp.abs(C.sum(-1, keepdims=True)), jnp.exp(-max_log_D))
            h = jnp.einsum('bnst,bntd->bnsd', C / (normalizer + EPS_BACKEND), vh)
            h = h.transpose(0, 2, 1, 3)
            mean = h.mean(-1, keepdims=True)
            var = h.var(-1, keepdims=True)
            hn = (h - mean) * jax.lax.rsqrt(var + NORM_EPS) * outnorm_weight
            return hn.reshape(B, S, E)
        return _mlstm_forward(q, k, v, ig_kernel, ig_bias, fg_kernel, fg_bias, outnorm_weight)

    def _L0_ffn_ref(x, gate_w, w1, w2):
        import math
        import jax, jax.numpy as jnp
        import numpy as np
        D_MODEL = 256
        NUM_EXPERTS = 8
        D_FF_EXPERT = max(64, int(D_MODEL * 4 * 0.25))
        THRESHOLD = 0.9
        CAP_FACTOR = 1.0
        INIT_STD = 0.02

        def _xmoe_route(probs):
            N, E = probs.shape
            order = jnp.argsort(-probs, axis=-1)
            p_sorted = jnp.take_along_axis(probs, order, axis=-1)
            csum = jnp.cumsum(p_sorted, axis=-1)
            reached = (csum >= THRESHOLD).at[:, -1].set(True)
            k_idx = jnp.argmax(reached, axis=-1)
            select_prefix = jnp.arange(E)[None, :] <= k_idx[:, None]
            rows = jnp.arange(N)[:, None]
            assign_mask = jnp.zeros((N, E), dtype=bool).at[rows, order].set(select_prefix)
            rank = jnp.arange(1, E + 1, dtype=probs.dtype)[None, :]
            R_sorted = jnp.where(select_prefix, p_sorted - rank, jnp.full_like(p_sorted, -1000000000.0))
            R = jnp.zeros((N, E), dtype=probs.dtype).at[rows, order].set(R_sorted)
            capacity = int(math.ceil(N / E) * CAP_FACTOR)
            C = min(capacity, N)
            tok_order = jnp.argsort(-R, axis=0)
            topC = tok_order[:C, :]
            keep = jnp.zeros((N, E), dtype=bool).at[topC, jnp.arange(E)[None, :]].set(True)
            final_mask = assign_mask & keep
            return jnp.where(final_mask, probs, jnp.zeros_like(probs))
        B, T, D = x.shape
        N = B * T
        xf = x.reshape(N, D)
        probs = jax.nn.softmax(xf @ gate_w.T, axis=-1)
        scores_sel = _xmoe_route(probs)
        h = jax.nn.gelu(jnp.einsum('nd,efd->enf', xf, w1), approximate=False)
        y_e = jnp.einsum('enf,edf->end', h, w2)
        y = jnp.einsum('ne,end->nd', scores_sel, y_e)
        return y.reshape(B, T, D)

    def _L1_xattn_ref(Q, K):
        import jax, jax.numpy as jnp
        import numpy as np
        B, L, D = (4, 1024, 256)
        scores = jnp.einsum('btd,bsd->bts', K, K)
        Lq = Q.shape[1]
        mask = jnp.tril(jnp.ones((Lq, Lq), dtype=scores.dtype))
        scores = scores * mask[None, :, :]
        Q_proj = jnp.einsum('bts,bsd->btd', scores, Q)
        return Q + Q_proj

    def _L1_ffn_ref(x, wqkv, q_scale, k_scale, wo, ln_g, ln_b, w1, b1, w2, b2):
        import jax, jax.numpy as jnp
        import numpy as np
        DIM = 256
        DEPTH = 2
        HEADS = 8
        DIM_HEAD = 64
        WINDOW = 128
        INNER = HEADS * DIM_HEAD
        HID = int(DIM * 4 * 2 / 3)
        B, N = (2, 2048)
        QK_SCALE = 8.0

        def shift_token(t):
            t1, t2 = jnp.split(t, 2, axis=-1)
            t2 = jnp.pad(t2, ((0, 0), (1, 0), (0, 0)))[:, :-1]
            return jnp.concatenate([t1, t2], axis=-1)

        def l2norm(t):
            return t / jnp.clip(jnp.linalg.norm(t, axis=-1, keepdims=True), 1e-12)

        def rotate_half(x):
            x1, x2 = jnp.split(x, 2, axis=-1)
            return jnp.concatenate([-x2, x1], axis=-1)

        def rotary_xpos(q, k):
            n = q.shape[-2]
            half_idx = jnp.arange(0, DIM_HEAD, 2, dtype=jnp.float32)
            inv_freq = 1.0 / 10000.0 ** (half_idx / DIM_HEAD)
            t = jnp.arange(n, dtype=jnp.float32)
            freqs = t[:, None] * inv_freq[None, :]
            freqs = jnp.concatenate([freqs, freqs], axis=-1)
            base = (half_idx + 0.4 * DIM_HEAD) / (1.4 * DIM_HEAD)
            power = (t - n // 2) / float(WINDOW // 2)
            scale = base[None, :] ** power[:, None]
            scale = jnp.concatenate([scale, scale], axis=-1)
            cos, sin = (jnp.cos(freqs), jnp.sin(freqs))
            q = q * cos * scale + rotate_half(q) * sin * scale
            k = k * cos / scale + rotate_half(k) * sin / scale
            return (q, k)

        def local_attention(q, k, v):
            b, h, n, d = q.shape
            w = n // WINDOW
            bq = q.reshape(b, h, w, WINDOW, d) * QK_SCALE
            bk = k.reshape(b, h, w, WINDOW, d)
            bv = v.reshape(b, h, w, WINDOW, d)

            def look_around(t):
                p = jnp.pad(t, ((0, 0), (0, 0), (1, 0), (0, 0), (0, 0)))
                return jnp.concatenate([p[:, :, :w], p[:, :, 1:]], axis=3)
            bk, bv = (look_around(bk), look_around(bv))
            bt = jnp.arange(n).reshape(w, WINDOW)
            btp = jnp.pad(bt, ((1, 0), (0, 0)), constant_values=-1)
            btk = jnp.concatenate([btp[:w], btp[1:]], axis=1)
            sim = jnp.einsum('bhwid,bhwjd->bhwij', bq, bk)
            i = bt[:, :, None]
            j = btk[:, None, :]
            mask = (i < j) | (i > j + WINDOW) | (j == -1)
            sim = jnp.where(mask, -jnp.finfo(sim.dtype).max, sim)
            attn = jax.nn.softmax(sim, axis=-1)
            out = jnp.einsum('bhwij,bhwjd->bhwid', attn, bv)
            return out.reshape(b, h, n, d)

        def _layer(x, wqkv, qs, ksc, wo, lg, lb, w1, b1, w2, b2):
            b, n, _ = x.shape
            h = shift_token(x)
            qkv = h @ wqkv
            q, k, v = jnp.split(qkv, 3, axis=-1)
            to_heads = lambda t: t.reshape(b, n, HEADS, DIM_HEAD).transpose(0, 2, 1, 3)
            q, k, v = (to_heads(q), to_heads(k), to_heads(v))
            q = l2norm(q) * qs
            k = l2norm(k) * ksc
            q, k = rotary_xpos(q, k)
            o = local_attention(q, k, v)
            o = o.transpose(0, 2, 1, 3).reshape(b, n, INNER)
            x = x + o @ wo
            h = shift_token(x)
            mu = h.mean(-1, keepdims=True)
            var = h.var(-1, keepdims=True)
            h = (h - mu) / jnp.sqrt(var + 1e-05) * lg + lb
            h = h @ w1 + b1
            a, g = jnp.split(h, 2, axis=-1)
            h = a * jax.nn.gelu(g, approximate=False)
            x = x + h @ w2 + b2
            return x
        for l in range(DEPTH):
            x = _layer(x, wqkv[l], q_scale[l], k_scale[l], wo[l], ln_g[l], ln_b[l], w1[l], b1[l], w2[l], b2[l])
        return x
    x = x + jnp.tanh(g_xattn[0]) * _L0_xattn_ref(_layernorm(x, axis=-1), ctx_1024, ctx_1024, L0_xattn_ig_kernel, L0_xattn_ig_bias, L0_xattn_fg_kernel, L0_xattn_fg_bias, L0_xattn_outnorm_weight)
    x = x + jnp.tanh(g_ffn[0]) * _L0_ffn_ref(_layernorm(x, axis=-1), L0_ffn_gate_w, L0_ffn_w1, L0_ffn_w2)
    x = x + jnp.tanh(g_xattn[1]) * _L1_xattn_ref(_layernorm(x, axis=-1), ctx_1024)
    x = x + jnp.tanh(g_ffn[1]) * _L1_ffn_ref(_layernorm(x, axis=-1), L1_ffn_wqkv, L1_ffn_q_scale, L1_ffn_k_scale, L1_ffn_wo, L1_ffn_ln_g, L1_ffn_ln_b, L1_ffn_w1, L1_ffn_b1, L1_ffn_w2, L1_ffn_b2)
    return x

_drawn_inputs = setup_inputs


def setup_inputs(seed=0):
    import zlib

    import numpy as np

    out = dict(_drawn_inputs(seed))
    spreads = {'g_ffn': (-1.0, 0.6),
     'L0_xattn_outnorm_weight': (1.0, 0.2),
     'L1_ffn_q_scale': (1.0, 0.6),
     'L1_ffn_k_scale': (1.0, 0.6),
     'L1_ffn_ln_g': (1.0, 0.6),
     'L1_ffn_ln_b': (0.0, 0.8),
     'L1_ffn_b1': (0.0, 0.8),
     'L1_ffn_b2': (0.0, 0.8)}
    factors = {'L0_xattn_ig_bias': 8.0,
     'L0_ffn_gate_w': 5.368,
     'L0_ffn_w1': 5.398,
     'L0_ffn_w2': 4.117,
     'L1_ffn_wqkv': 8.0,
     'L1_ffn_wo': 8.0,
     'L1_ffn_w1': 8.0,
     'L1_ffn_w2': 8.0}
    for name, (base, spread) in spreads.items():
        noise = np.random.default_rng([zlib.crc32(name.encode()), seed]).standard_normal(out[name].shape)
        drawn = base * np.exp(spread * noise) if base else spread * noise
        out[name] = jnp.asarray(drawn.astype(out[name].dtype))
    for name, factor in factors.items():
        out[name] = (out[name] * factor).astype(out[name].dtype)
    return out
```

```python
import concourse.bass as bass
from concourse import mybir
from contextlib import ExitStack
import numpy as np

FP = mybir.dt.float32
I32 = mybir.dt.int32
R32 = mybir.dt.float32r
ALU = mybir.AluOpType
ACT = mybir.ActivationFunctionType
AX = mybir.AxisListType.X

P = 128
B, S, D = 8, 512, 256
NT = S // P
KD = D // P
N = B * S
STREAMS = 2
PAIRS = B // STREAMS


class Sig:

    def __init__(self, sem, per, credit=0):
        self.sem, self.per, self.credit, self.n = sem, per, credit, 0

    def up(self, by=1):
        self.n += by
        return self.sem, by

    def at(self, turn, k):
        return self.sem, turn * self.per + (self.credit + k)

    def prev(self, turn, k):
        assert self.credit >= self.per and k > 0
        return self.sem, turn * self.per + (self.credit - self.per + k)

    def now(self, turn):
        return self.at(turn, self.n)

    def close(self):
        assert self.n == self.per, (self.sem.name, self.n, self.per)
        self.n = 0


class Ring:

    def __init__(self, banks, groups, full, emptied):
        self.banks, self.names = banks, [g for g, _ in groups]
        self.who = dict(groups)
        assert len(self.who) == len(groups)
        self.index = {g: i for i, g in enumerate(self.names)}
        count = {"V": 0, "S": 0}
        self.rank = {}
        for g, w in groups:
            count[w] += 1
            self.rank[g] = count[w]
        self.full = Sig(full, len(groups), len(groups))
        self.emptied = {w: Sig(emptied[w], count[w], count[w]) for w in "VS"}
        self.taken = 0

    def bank(self, name):
        return self.banks[self.index[name] % 8]

    def take(self, pe, turn, name):
        i = self.index[name]
        assert i == self.taken, (name, self.names[self.taken])
        self.taken += 1
        if i >= 8:
            last, back = self.names[i - 8], 0
        else:
            last, back = self.names[max(j for j in range(len(self.names)) if j % 8 == i)], 1
        sig = self.emptied[self.who[last]]
        pe.wait_ge(sig.sem, turn * sig.per + (sig.credit - back * sig.per + self.rank[last]))
        return self.bank(name)

    def ready(self, turn, name):
        return self.full.at(turn, self.index[name] + 1)

    def used(self, turn, name):
        return self.full.prev(turn, self.index[name] + 1)

    def out(self, name):
        sig = self.emptied[self.who[name]]
        assert sig.n == self.rank[name] - 1, name
        return sig.up()

    def moved(self, turn, name):
        return self.emptied[self.who[name]].at(turn, self.rank[name])

    def moved_before(self, turn, name):
        return self.emptied[self.who[name]].prev(turn, self.rank[name])

    def close_pe(self):
        assert self.taken == len(self.names)
        self.taken = 0
        self.full.close()


def plain(ap):
    return ap.bitcast(FP)


def split_matmul(nc, out, weights, data, start, stop):
    (wh, wl), (dh, dl) = weights, data
    nc.tensor.matmul(out, wh, dh, start=start, stop=False)
    nc.tensor.matmul(out, wh, dl, start=False, stop=False)
    return nc.tensor.matmul(out, wl, dh, start=False, stop=stop)


def turned(nc, out, data, ident):
    return nc.tensor.matmul(out, data, ident, start=True, stop=True)


def hold(engine, passed, sem, value):
    engine.wait_ge(sem, value)
    engine.sem_inc(passed, 1)


def credit(engine, *sigs):
    for sig in sigs:
        engine.sem_inc(sig.sem, sig.credit)
H = 4
DH = D // H


class Store:

    def __init__(self, nc, phase):
        self.nc, self.phase, self.stack, self.place = nc, phase, ExitStack(), {}

    def sb(self, name, shape, dt=FP):
        self.place[name] = -(-self.nc.sbuf_base // 32) * 32
        return self.stack.enter_context(self.nc.sbuf_tensor(f"{self.phase}_{name}", [P] + shape, dt))

    def rounded(self, name, shape):
        return self.nc.alloc_sbuf_tensor_at(f"{self.phase}_{name}_r", [P] + shape, R32, offset=self.place[name])

    def rows(self, name, shape, dt=FP):
        return self.stack.enter_context(self.nc.sbuf_tensor(f"{self.phase}_{name}", shape, dt))

    def banks(self):
        return [self.stack.enter_context(self.nc.psum_tensor(f"{self.phase}_bank{i}", [P, 512], FP)) for i in range(8)]

    def sem(self, name):
        return self.nc.alloc_semaphore(f"{self.phase}_{name}")


def tiles(ap):
    return ap.rearrange("(t p) d -> p t d", p=P)


def setup(nc, A, K):
    sem_zero, sem_ready = nc.alloc_semaphore("const_zero"), nc.alloc_semaphore("const_ready")
    K.ident = K.keep.sb("ident", [P])
    K.half = K.keep.sb("minus_half", [64])
    K.one = K.keep.sb("one", [1])
    K.v_passed, K.pool_passed, K.pe_passed, K.sp_passed = (nc.alloc_semaphore(f"{n}_waits") for n in ("vector", "pool", "tensor", "sync"))
    with nc.Block() as block:
        @block.gpsimd
        def _(pool):
            nc.gpsimd.memset(K.ident[:], 0.0).then_inc(sem_zero, 1)
            nc.gpsimd.memset(K.half[:], -0.5).then_inc(sem_ready, 1)
            nc.gpsimd.memset(K.one[:], 1.0).then_inc(sem_ready, 1)
            pool.wait_ge(sem_zero, 1)
            nc.gpsimd.affine_select(out=K.ident[:], in_=K.ident[:], compare_op=ALU.not_equal, fill=1.0,
                                    base=0, pattern=[[-1, P]], channel_multiplier=1).then_inc(sem_ready, 1)
            pool.wait_ge(sem_ready, 3)


def normalize_phase(nc, A, K):
    R = Store(nc, "nrm")
    with R.stack:
        X = [R.sb(f"x{s}", [NT, D]) for s in range(STREAMS)]
        C = [R.sb(f"ctx{s}", [NT, D]) for s in range(STREAMS)]
        XN = [R.sb(f"xn{s}", [NT, D]) for s in range(STREAMS)]
        XT = [R.sb(f"xT{s}", [KD, S]) for s in range(STREAMS)]
        CT = [R.sb(f"cT{s}", [KD, S]) for s in range(STREAMS)]
        halves = [R.sb(f"halves{s}", [NT, 6]) for s in range(STREAMS)]
        stats = [R.sb(f"stats{s}", [NT, 2]) for s in range(STREAMS)]
        vare = [R.sb(f"vare{s}", [NT]) for s in range(STREAMS)]
        rstd = [R.sb(f"rstd{s}", [NT]) for s in range(STREAMS)]
        kern = R.sb("kern", [3 * KD, 2, H])
        Wg = R.sb("Wg", [2 * KD, 2, H])
        bias = R.sb("bias", [2, H])
        groups = []
        for s in range(STREAMS):
            groups += [(("cT", s, k), "S") for k in range(KD)]
        for s in range(STREAMS):
            groups += [(("xT", s, k), "S") for k in range(KD)]
        for s in range(STREAMS):
            groups += [(("gate", s), "V")]
        ring = Ring(R.banks(), groups, R.sem("bank_full"), {"V": R.sem("emptied_V"), "S": R.sem("emptied_S")})
        w_in = R.sem("weights_in")
        x_in = [Sig(R.sem(f"x_in{s}"), 16) for s in range(STREAMS)]
        c_in = [Sig(R.sem(f"ctx_in{s}"), 16) for s in range(STREAMS)]
        stored = [Sig(R.sem(f"stored{s}"), 32, 32) for s in range(STREAMS)]
        step = Sig(R.sem("vector_step"), STREAMS * NT)
        stat = Sig(R.sem("stats_ready"), STREAMS * NT)
        normed = Sig(R.sem("x_normed"), STREAMS * NT, STREAMS * NT)
        pstep = Sig(R.sem("pool_step"), STREAMS)
        rs = Sig(R.sem("rstd_ready"), STREAMS)
        wg = R.sem("gate_weights")
        xb = A["x"].rearrange("b (t p) d -> b p t d", p=P)
        cb = A["ctx_1024"].rearrange("b (t p) d -> b p t d", p=P)
        with nc.Block() as block:
            @block.sync
            def _(sp):
                for i, name in enumerate(("ig", "fg")):
                    sp.dma_start(kern[:, :, i, :], A[f"L0_xattn_{name}_kernel"].rearrange("(k p) h -> p k h", p=P)).then_inc(w_in, 16)
                    sp.dma_start(bias[:, i, :], A[f"L0_xattn_{name}_bias"].partition_broadcast(P)).then_inc(w_in, 16)
                with sp.Fori(0, PAIRS) as t:
                    for s in range(STREAMS):
                        sp.wait_ge(*ring.used(t, ("cT", s, KD - 1)))
                        sp.dma_start(C[s][:], cb[t * STREAMS + s]).then_inc(c_in[s].sem, 16)
                        sp.wait_ge(*normed.prev(t, NT * (s + 1)))
                        sp.dma_start(X[s][:], xb[t * STREAMS + s]).then_inc(x_in[s].sem, 16)

            @block.vector
            def _(v):
                credit(v, normed, ring.emptied["V"])
                v.wait_ge(w_in, 64)
                nc.vector.tensor_copy(Wg[:, 0:KD], kern[:, 0:KD]).then_inc(wg, 1)
                nc.vector.tensor_tensor(Wg[:, KD:2 * KD], kern[:, KD:2 * KD], kern[:, 2 * KD:3 * KD], ALU.add).then_inc(wg, 1)
                with v.Fori(0, PAIRS) as t:
                    for s in range(STREAMS):
                        v.wait_ge(*x_in[s].at(t, 16))
                        for i in range(NT):
                            nc.vector.bn_stats(halves[s][:, i, :], X[s][:, i, :]).then_inc(*step.up())
                        hold(v, K.v_passed, *step.at(t, (s + 1) * NT))
                        for i in range(NT):
                            nc.vector.bn_aggr(stats[s][:, i, :], halves[s][:, i, :]).then_inc(*stat.up())
                    for s in range(STREAMS):
                        v.wait_ge(*rs.at(t, s + 1))
                        for i in range(NT):
                            nc.vector.tensor_scalar(XN[s][:, i, :], X[s][:, i, :], stats[s][:, i, 0:1], rstd[s][:, i:i + 1],
                                                    ALU.subtract, ALU.mult).then_inc(*normed.up())
                    for s in range(STREAMS):
                        v.wait_ge(*ring.ready(t, ("gate", s)))
                        psum = ring.bank(("gate", s))[:, 0:NT * 2 * H].rearrange("p (t g h) -> p g t h", t=NT, g=2)
                        nc.vector.tensor_tensor(K.gates[:, :, :, t * STREAMS + s, :], psum,
                                                bias[:].unsqueeze(2).broadcast_to([P, 2, NT, H]), ALU.add).then_inc(*ring.out(("gate", s)))
                    step.close(), stat.close(), normed.close(), ring.emptied["V"].close()

            @block.gpsimd
            def _(pool):
                with pool.Fori(0, PAIRS) as t:
                    for s in range(STREAMS):
                        hold(pool, K.pool_passed, *stat.at(t, (s + 1) * NT))
                        nc.gpsimd.tensor_scalar(vare[s][:], stats[s][:, :, 1], 1e-5, None, ALU.add).then_inc(*pstep.up())
                        pool.wait_ge(*pstep.now(t))
                        nc.gpsimd.tensor_tensor(rstd[s][:], vare[s][:], K.half[:, 0:NT], ALU.pow).then_inc(*rs.up())
                    pstep.close(), rs.close()

            @block.scalar
            def _(act):
                credit(act, ring.emptied["S"], *stored)
                with act.Fori(0, PAIRS) as t:
                    for name, T, scratch in (("cT", CT, K.ctxT_d), ("xT", XT, K.xnT_d)):
                        for s in range(STREAMS):
                            act.wait_ge(*stored[s].at(t, 0))
                            for k in range(KD):
                                act.wait_ge(*ring.ready(t, (name, s, k)))
                                nc.scalar.activation(T[s][:, k, :], ring.bank((name, s, k))[:], ACT.Copy).then_inc(*ring.out((name, s, k)))
                    for name, T, scratch in (("cT", CT, K.ctxT_d), ("xT", XT, K.xnT_d)):
                        for s in range(STREAMS):
                            act.wait_ge(*ring.moved(t, (name, s, KD - 1)))
                            act.dma_start(scratch[t * STREAMS + s], T[s][:]).then_inc(stored[s].sem, 16)
                    ring.emptied["S"].close()
                for s in range(STREAMS):
                    act.wait_ge(*stored[s].at(PAIRS, 0))

            @block.tensor
            def _(pe):
                pe.wait_ge(wg, 2)
                credit(pe, ring.full)
                with pe.Fori(0, PAIRS) as t:
                    for name, src, sig in (("cT", C, c_in), ("xT", XN, None)):
                        for s in range(STREAMS):
                            if sig:
                                pe.wait_ge(*sig[s].at(t, 16))
                            else:
                                pe.wait_ge(*normed.at(t, NT * (s + 1)))
                            for k in range(KD):
                                bank = ring.take(pe, t, (name, s, k))
                                for i in range(NT):
                                    mm = nc.tensor.transpose(bank[:, i * P:(i + 1) * P], src[s][:, i, k * P:(k + 1) * P], K.ident[:])
                                mm.then_inc(*ring.full.up())
                    for s in range(STREAMS):
                        pe.wait_ge(*ring.moved(t, ("xT", s, KD - 1)))
                        bank = ring.take(pe, t, ("gate", s))
                        for i in range(NT):
                            for k in range(2 * KD):
                                T = (XT if k < KD else CT)[s]
                                mm = nc.tensor.matmul(bank[:, i * 2 * H:(i + 1) * 2 * H], T[:, k % KD, i * P:(i + 1) * P],
                                                      Wg[:, k].rearrange("p g h -> p (g h)"), start=(k == 0), stop=(k == 2 * KD - 1))
                        mm.then_inc(*ring.full.up())
                    ring.close_pe()


def scan_phase(nc, A, K):
    R = Store(nc, "scan")
    BH = B * H
    with R.stack:
        row = lambda name: R.rows(name, [BH, S])
        f, nf, nabs, e, l, minf, lf, F, a, m, Fm, nl, ones = map(row, "f nf nabs e l minf lf F a m Fm nl ones".split())
        banks = R.banks()
        turned, step, sstep = R.sem("gates_turned"), Sig(R.sem("vector_step"), 0), Sig(R.sem("scalar_step"), 0)
        rows_ready, back, kept = R.sem("rows_ready"), R.sem("columns_turned"), R.sem("m_stored")
        with nc.Block() as block:
            @block.tensor
            def _(pe):
                for kind in range(2):
                    for i in range(NT):
                        mm = nc.tensor.transpose(banks[kind][0:BH, i * P:(i + 1) * P],
                                                 K.gates[:, kind, i].rearrange("p b h -> p (b h)"), K.ident[:])
                    mm.then_inc(turned, 1)
                pe.wait_ge(rows_ready, 1)
                for i in range(NT):
                    mm = nc.tensor.transpose(banks[2][:, i * BH:(i + 1) * BH], a[:, i * P:(i + 1) * P], K.ident[0:BH, 0:BH])
                mm.then_inc(back, 1)
                pe.wait_ge(rows_ready, 2)
                for i in range(NT):
                    mm = nc.tensor.transpose(banks[3][:, i * BH:(i + 1) * BH], nl[:, i * P:(i + 1) * P], K.ident[0:BH, 0:BH])
                mm.then_inc(back, 1)

            @block.vector
            def _(v):
                def then(ins):
                    ins.then_inc(*step.up())
                    v.wait_ge(*step.now(0))
                then(nc.vector.memset(ones[:], 1.0))
                v.wait_ge(turned, 2)
                then(nc.vector.tensor_copy(f[:], banks[1][0:BH, :]))
                then(nc.vector.tensor_scalar(nf[:], f[:], -1.0, None, ALU.mult))
                then(nc.vector.tensor_tensor(nabs[:], f[:], nf[:], ALU.min))
                then(nc.vector.tensor_scalar(minf[:], f[:], 0.0, None, ALU.min))
                v.wait_ge(*sstep.at(0, 2))
                then(nc.vector.tensor_tensor(lf[:], minf[:], l[:], ALU.subtract))
                then(nc.vector.tensor_tensor_scan(F[:], ones[:], lf[:], 0.0, ALU.mult, ALU.add))
                then(nc.vector.tensor_tensor(a[:], banks[0][0:BH, :], F[:], ALU.subtract))
                then(nc.vector.tensor_tensor_scan(m[:], a[:], a[:], -3.0e38, ALU.max, ALU.max))
                nc.vector.tensor_tensor(Fm[:], F[:], m[:], ALU.add).then_inc(rows_ready, 1)
                v.wait_ge(back, 1)
                nc.vector.tensor_copy(K.acol[:].rearrange("p t b h -> p (t b h)"), banks[2][:, 0:NT * BH]).then_inc(*step.up())
                v.wait_ge(back, 2)
                nc.vector.tensor_copy(K.nlcol[:].rearrange("p t b h -> p (t b h)"), banks[3][:, 0:NT * BH]).then_inc(*step.up())

            @block.scalar
            def _(act):
                act.wait_ge(*step.at(0, 4))
                nc.scalar.activation(e[:], nabs[:], ACT.Exp).then_inc(*sstep.up())
                act.wait_ge(*sstep.now(0))
                nc.scalar.activation(l[:], e[:], ACT.Ln, bias=K.one[0:BH, :]).then_inc(*sstep.up())
                act.wait_ge(rows_ready, 1)
                nc.scalar.activation(nl[:], Fm[:], ACT.Exp, scale=-1.0).then_inc(rows_ready, 1)

            @block.sync
            def _(sp):
                sp.wait_ge(rows_ready, 1)
                sp.dma_start(K.m_d[:, :], m[:]).then_inc(kept, 16)
                sp.wait_ge(kept, 16)


def mlstm_phase(nc, A, K):
    R = Store(nc, "mlstm")
    UNITS = [(h, s) for h in range(H) for s in range(STREAMS)]
    U, RB, LAG = len(UNITS), 4, 2
    W = DH + 1
    with R.stack:
        X = [R.sb(f"x{s}", [NT, D]) for s in range(STREAMS)]
        XT = [R.sb(f"xT{s}", [KD, S]) for s in range(STREAMS)]
        CT = [R.sb(f"cT{s}", [KD, S]) for s in range(STREAMS)]
        VE = [R.sb(f"v{s}", [NT, H, W]) for s in range(STREAMS)]
        MB = [R.sb(f"m{s}", [H, S]) for s in range(STREAMS)]
        DT = [R.sb(f"decay{i}", [NT, S]) for i in range(RB)]
        CM = [R.sb(f"weights{i}", [NT, S]) for i in range(RB)]
        HB = [R.sb(f"h{s}", [NT, H, W]) for s in range(STREAMS)]
        hh = [R.sb(f"hh{s}", [NT * H, DH]) for s in range(STREAMS)]
        sq = [R.sb(f"sq{s}", [NT * H, DH]) for s in range(STREAMS)]
        small = lambda name: [R.sb(f"{name}{s}", [NT * H]) for s in range(STREAMS)]
        den, rden, hsum, hmean, vsum, vare, rstd = map(small, "den rden hsum hmean vsum vare rstd".split())
        gb, tg, wb, wt = R.sb("g", [2]), R.sb("tanh_g", [2]), R.sb("w", [D]), R.sb("w_tanh", [D])
        groups = []
        for k in range(U + LAG):
            if k < U:
                groups += [(("qk", k, j), "V") for j in range(3)]
            if k >= LAG:
                groups += [(("pv", k - LAG), "S")]
        ring = Ring(R.banks(), groups, R.sem("bank_full"), {"V": R.sem("emptied_V"), "S": R.sem("emptied_S")})
        par_in = R.sem("params_in")
        names = ("xT", "cT", "v", "m", "x")
        loaded = {n: [Sig(R.sem(f"{n}_in{s}"), 16 * NT if n == "v" else 16) for s in range(STREAMS)] for n in names}
        stored = [Sig(R.sem(f"stored{s}"), 16, 16) for s in range(STREAMS)]
        ones = R.sem("ones_set")
        tgs, wts = R.sem("tanh_ready"), R.sem("w_ready")
        decay = Sig(R.sem("decay_ready"), U, U)
        masked = Sig(R.sem("decay_masked"), U)
        step = Sig(R.sem("vector_step"), STREAMS * 9)
        centred = Sig(R.sem("h_centred"), STREAMS)
        squared = Sig(R.sem("h_squared"), STREAMS)
        varsum = Sig(R.sem("variance_ready"), STREAMS)
        pstep = Sig(R.sem("pool_step"), STREAMS)
        rs = Sig(R.sem("rstd_ready"), STREAMS)
        x1 = Sig(R.sem("x1_ready"), STREAMS)
        xb = A["x"].rearrange("b (t p) d -> b p t d", p=P)
        vb = A["ctx_1024"].rearrange("b (t p) (h d) -> b t p h d", p=P, h=H)
        mb = K.m_d[:, :].rearrange("(b h) s -> b (h s)", h=H)
        ob = K.x2_d[0:N, :].rearrange("(b t p) d -> b p t d", p=P, t=NT)
        with nc.Block() as block:
            @block.sync
            def _(sp):
                sp.dma_start(gb[:, 0:1], A["g_xattn"][0:1].partition_broadcast(P)).then_inc(par_in, 16)
                sp.dma_start(wb[:], A["L0_xattn_outnorm_weight"].rearrange("h d -> (h d)").partition_broadcast(P)).then_inc(par_in, 16)
                sp.wait_ge(ones, STREAMS)
                last = ("pv", U - STREAMS), ("pv", U - 1)
                with sp.Fori(0, PAIRS) as t:
                    for s in range(STREAMS):
                        b = t * STREAMS + s
                        sp.wait_ge(*ring.used(t, ("qk", U - STREAMS + s, 2)))
                        sp.dma_start(XT[s][:], K.xnT_d[b]).then_inc(loaded["xT"][s].sem, 16)
                        sp.dma_start(CT[s][:], K.ctxT_d[b]).then_inc(loaded["cT"][s].sem, 16)
                        sp.wait_ge(*decay.prev(t, U - STREAMS + s + 1))
                        sp.dma_start(MB[s][:], mb[b].partition_broadcast(P)).then_inc(loaded["m"][s].sem, 16)
                        sp.wait_ge(*ring.used(t, ("pv", U - STREAMS + s)))
                        for i in range(NT):
                            sp.dma_start(VE[s][:, i, :, 0:DH], vb[b, i]).then_inc(loaded["v"][s].sem, 16)
                        sp.wait_ge(*stored[s].at(t, 0))
                        sp.dma_start(X[s][:], xb[b]).then_inc(loaded["x"][s].sem, 16)

            @block.scalar
            def _(act):
                act.wait_ge(par_in, 32)
                nc.scalar.activation(tg[:, 0:1], gb[:, 0:1], ACT.Tanh).then_inc(tgs, 1)
                credit(act, ring.emptied["S"], decay, *stored)
                with act.Fori(0, PAIRS) as t:
                    for k in range(U + LAG):
                        if k < U:
                            h, s = UNITS[k]
                            if h == 0:
                                act.wait_ge(*loaded["m"][s].at(t, 16))
                            act.wait_ge(*(ring.moved(t, ("qk", k - RB, 2)) if k >= RB else ring.moved_before(t, ("qk", U + k - RB, 2))))
                            for j in range(NT):
                                bcol = K.acol[:, j, t * STREAMS + s, h:h + 1]
                                e = nc.scalar.activation(DT[k % RB][:, j, 0:S - j * P], MB[s][:, h, j * P:S], ACT.Exp, bias=bcol, scale=-1.0)
                            e.then_inc(*decay.up())
                        if k >= LAG:
                            h, s = UNITS[k - LAG]
                            act.wait_ge(*ring.ready(t, ("pv", k - LAG)))
                            nc.scalar.activation(HB[s][:, :, h, :], ring.bank(("pv", k - LAG))[:, 0:NT * W].rearrange("p (t w) -> p t w", t=NT),
                                                 ACT.Copy).then_inc(*ring.out(("pv", k - LAG)))
                    for s in range(STREAMS):
                        act.wait_ge(*centred.at(t, s + 1))
                        nc.scalar.activation(sq[s][:], hh[s][:], ACT.Square).then_inc(*squared.up())
                    for s in range(STREAMS):
                        act.wait_ge(*x1.at(t, s + 1))
                        act.dma_start(ob[t * STREAMS + s], X[s][:]).then_inc(stored[s].sem, 16)
                    decay.close(), squared.close(), ring.emptied["S"].close()
                for s in range(STREAMS):
                    act.wait_ge(*stored[s].at(PAIRS, 0))

            @block.gpsimd
            def _(pool):
                for s in range(STREAMS):
                    nc.gpsimd.memset(VE[s][:, :, :, DH:W], 1.0).then_inc(ones, 1)
                with pool.Fori(0, PAIRS) as t:
                    for k in range(U):
                        hold(pool, K.pool_passed, *decay.at(t, k + 1))
                        diag = DT[k % RB][:, :, 0:P]
                        nc.gpsimd.affine_select(out=diag, in_=diag, compare_op=ALU.is_ge, fill=0.0, base=0,
                                                pattern=[[0, NT], [1, P]], channel_multiplier=-1).then_inc(*masked.up())
                    for s in range(STREAMS):
                        hold(pool, K.pool_passed, *varsum.at(t, s + 1))
                        nc.gpsimd.tensor_scalar(vare[s][:], vsum[s][:], 1.0 / DH, 1e-6, ALU.mult, ALU.add).then_inc(*pstep.up())
                        pool.wait_ge(*pstep.now(t))
                        nc.gpsimd.tensor_tensor(rstd[s][:], vare[s][:], K.half[:, 0:NT * H], ALU.pow).then_inc(*rs.up())
                    masked.close(), pstep.close(), rs.close()

            @block.vector
            def _(v):
                v.wait_ge(tgs, 1)
                nc.vector.tensor_scalar(wt[:], wb[:], tg[:, 0:1], None, ALU.mult).then_inc(wts, 1)
                v.wait_ge(wts, 1)
                credit(v, ring.emptied["V"])

                def then(t, ins):
                    ins.then_inc(*step.up())
                    v.wait_ge(*step.now(t))

                over = lambda x: x[:].unsqueeze(2).broadcast_to([P, NT * H, DH])
                with v.Fori(0, PAIRS) as t:
                    for k in range(U):
                        v.wait_ge(*masked.at(t, k + 1))
                        for g, js in enumerate(((0,), (1, 3), (2,))):
                            v.wait_ge(*ring.ready(t, ("qk", k, g)))
                            at = 0
                            for j in js:
                                n = S - j * P
                                ins = nc.vector.scalar_tensor_tensor(out=CM[k % RB][:, j, 0:n], in0=ring.bank(("qk", k, g))[:, at:at + n],
                                                                     scalar=float(DH) ** -0.5, in1=DT[k % RB][:, j, 0:n],
                                                                     op0=ALU.mult, op1=ALU.mult)
                                at += n
                            ins.then_inc(*ring.out(("qk", k, g)))
                    for s in range(STREAMS):
                        v.wait_ge(*ring.moved(t, ("pv", U - STREAMS + s)))
                        sums = HB[s][:, :, :, DH]
                        quad = lambda x: x[s][:].rearrange("p (t h) -> p t h", t=NT)
                        then(t, nc.vector.scalar_tensor_tensor(out=quad(den), in0=sums, scalar=-1.0, in1=sums, op0=ALU.mult, op1=ALU.max))
                        then(t, nc.vector.tensor_tensor(quad(den), quad(den), K.nlcol[:, :, t * STREAMS + s, :], ALU.max))
                        then(t, nc.vector.tensor_scalar(den[s][:], den[s][:], 1e-6, None, ALU.add))
                        then(t, nc.vector.reciprocal(rden[s][:], den[s][:]))
                        then(t, nc.vector.tensor_tensor(hh[s][:], HB[s][:, :, :, 0:DH].rearrange("p t h d -> p (t h) d"), over(rden[s]), ALU.mult))
                        then(t, nc.vector.tensor_reduce(hsum[s][:], hh[s][:], AX, ALU.add))
                        then(t, nc.vector.tensor_scalar(hmean[s][:], hsum[s][:], 1.0 / DH, None, ALU.mult))
                        nc.vector.tensor_tensor(hh[s][:], hh[s][:], over(hmean[s]), ALU.subtract).then_inc(*centred.up())
                    for s in range(STREAMS):
                        v.wait_ge(*squared.at(t, s + 1))
                        nc.vector.tensor_reduce(vsum[s][:], sq[s][:], AX, ALU.add).then_inc(*varsum.up())
                    for s in range(STREAMS):
                        v.wait_ge(*rs.at(t, s + 1))
                        v.wait_ge(*loaded["x"][s].at(t, 16))
                        nc.vector.tensor_tensor(sq[s][:], hh[s][:], over(rstd[s]), ALU.mult).then_inc(*step.up())
                        v.wait_ge(*step.now(t))
                        rows = sq[s][:].rearrange("p (t h) d -> p t (h d)", t=NT)
                        then(t, nc.vector.tensor_tensor(rows, rows, wt[:].unsqueeze(1).broadcast_to([P, NT, D]), ALU.mult))
                        nc.vector.tensor_tensor(X[s][:], X[s][:], rows, ALU.add).then_inc(*x1.up())
                    step.close(), centred.close(), varsum.close(), x1.close(), ring.emptied["V"].close()

            @block.tensor
            def _(pe):
                credit(pe, ring.full)
                pe.wait_ge(ones, STREAMS)
                with pe.Fori(0, PAIRS) as t:
                    for k in range(U + LAG):
                        if k < U:
                            h, s = UNITS[k]
                            if h == 0:
                                pe.wait_ge(*loaded["xT"][s].at(t, 16))
                                pe.wait_ge(*loaded["cT"][s].at(t, 16))
                            part, kd = slice(h % 2 * DH, h % 2 * DH + DH), h // 2
                            for g, js in enumerate(((0,), (1, 3), (2,))):
                                bank = ring.take(pe, t, ("qk", k, g))
                                at = 0
                                for j in js:
                                    n = S - j * P
                                    mm = nc.tensor.matmul(bank[:, at:at + n], CT[s][part, kd, j * P:(j + 1) * P], XT[s][part, kd, j * P:S],
                                                          start=True, stop=True)
                                    at += n
                                mm.then_inc(*ring.full.up())
                        if k >= LAG:
                            h, s = UNITS[k - LAG]
                            if h == 0:
                                pe.wait_ge(*loaded["v"][s].at(t, 16 * NT))
                            pe.wait_ge(*ring.moved(t, ("qk", k - LAG, 2)))
                            bank = ring.take(pe, t, ("pv", k - LAG))
                            for i in range(NT):
                                for j in range(i + 1):
                                    mm = nc.tensor.matmul(bank[:, i * W:(i + 1) * W], CM[(k - LAG) % RB][:, j, (i - j) * P:(i - j + 1) * P],
                                                          VE[s][:, j, h, :], start=(j == 0), stop=(j == i))
                            mm.then_inc(*ring.full.up())
                    ring.close_pe()
E_ = 8
F_ = 256
KF = F_ // P
CAP = N // E_
SLOTS = CAP // P
ROW = D + E_
COLS = N // P


def layernorm_stats(nc, v, t, K, src, halves, stats, step, stat):
    first = step.n
    for i in range(NT):
        nc.vector.bn_stats(halves[:, i, :], src[:, i, :]).then_inc(*step.up())
    hold(v, K.v_passed, *step.at(t, first + NT))
    for i in range(NT):
        nc.vector.bn_aggr(stats[:, i, :], halves[:, i, :]).then_inc(*stat.up())


def rstd_on_pool(nc, pool, t, K, stats, vare, rstd, eps, stat, pstep, rs):
    hold(pool, K.pool_passed, *stat.at(t, (rs.n + 1) * NT))
    nc.gpsimd.tensor_scalar(vare[:], stats[:, :, 1], eps, None, ALU.add).then_inc(*pstep.up())
    pool.wait_ge(*pstep.now(t))
    nc.gpsimd.tensor_tensor(rstd[:], vare[:], K.half[:, 0:NT], ALU.pow).then_inc(*rs.up())


def router_phase(nc, A, K):
    R = Store(nc, "router")
    with R.stack:
        two = range(STREAMS)
        X = [R.sb(f"x{s}", [NT, D]) for s in two]
        XG = [R.sb(f"row{s}", [NT, ROW]) for s in two]
        XT = [R.sb(f"xT{s}", [KD, S]) for s in two]
        halves = [R.sb(f"halves{s}", [NT, 6]) for s in two]
        stats = [R.sb(f"stats{s}", [NT, 2]) for s in two]
        vare, rstd = ([R.sb(f"{n}{s}", [NT]) for s in two] for n in ("vare", "rstd"))
        lg, zz, ex, rank, prec, sel, q = ([R.sb(f"{n}{s}", [NT, E_]) for s in two] for n in "lg zz ex rank prec sel q".split())
        mx, sm, rc = ([R.sb(f"{n}{s}", [NT]) for s in two] for n in "mx sm rc".split())
        gt, eq, bp = ([R.sb(f"{n}{s}", [NT, E_, E_]) for s in two] for n in "gt eq bp".split())
        gw = R.sb("gate_w", [KD, E_])
        tri = R.sb("earlier", [E_, E_])
        zero = R.sb("zero", [SLOTS, ROW])
        groups = [(("xT", s, k), "S") for s in two for k in range(KD)] + [(("logits", s), "V") for s in two]
        ring = Ring(R.banks(), groups, R.sem("bank_full"), {"V": R.sem("emptied_V"), "S": R.sem("emptied_S")})
        w_in, tri_ready, zeroed, dummies = R.sem("gate_in"), R.sem("tri_ready"), R.sem("zeroed"), R.sem("dummy_rows")
        x_in = [Sig(R.sem(f"x_in{s}"), 16) for s in two]
        stored = [Sig(R.sem(f"stored{s}"), 16, 16) for s in two]
        step = Sig(R.sem("vector_step"), STREAMS * (NT + 16))
        stat = Sig(R.sem("stats_ready"), STREAMS * NT)
        normed = Sig(R.sem("x_normed"), STREAMS * NT, STREAMS * NT)
        pstep = Sig(R.sem("pool_step"), STREAMS)
        rs = Sig(R.sem("rstd_ready"), STREAMS)
        shifted = Sig(R.sem("logits_shifted"), STREAMS)
        expd = Sig(R.sem("exp_ready"), STREAMS)
        rows_ready = Sig(R.sem("rows_ready"), STREAMS)
        xb = K.x2_d[0:N, :].rearrange("(b t p) d -> b p t d", p=P, t=NT)
        gb = K.xg_d[0:N, :].rearrange("(b t p) d -> b p t d", p=P, t=NT)
        with nc.Block() as block:
            @block.sync
            def _(sp):
                sp.dma_start(gw[:], A["gate_wT"].rearrange("(k p) e -> p k e", p=P)).then_inc(w_in, 16)
                with sp.Fori(0, PAIRS) as t:
                    for s in two:
                        sp.wait_ge(*normed.prev(t, NT * (s + 1)))
                        sp.dma_start(X[s][:], xb[t * STREAMS + s]).then_inc(x_in[s].sem, 16)
                sp.wait_ge(zeroed, 1)
                sp.dma_start(K.xg_d[N:N + CAP, :].rearrange("(t p) d -> p t d", p=P), zero[:]).then_inc(dummies, 16)
                sp.dma_start(K.x2_d[N:N + CAP, :].rearrange("(t p) d -> p t d", p=P), zero[:, :, 0:D]).then_inc(dummies, 16)
                sp.wait_ge(dummies, 32)

            @block.gpsimd
            def _(pool):
                nc.gpsimd.memset(zero[:], 0.0).then_inc(zeroed, 1)
                nc.gpsimd.memset(tri[:], 1.0).then_inc(tri_ready, 1)
                pool.wait_ge(tri_ready, 1)
                nc.gpsimd.affine_select(out=tri[:], in_=tri[:], compare_op=ALU.is_gt, fill=0.0, base=0,
                                        pattern=[[1, E_], [-1, E_]], channel_multiplier=0).then_inc(tri_ready, 1)
                with pool.Fori(0, PAIRS) as t:
                    for s in two:
                        rstd_on_pool(nc, pool, t, K, stats[s], vare[s], rstd[s], 1e-5, stat, pstep, rs)
                    pstep.close(), rs.close()

            @block.vector
            def _(v):
                credit(v, normed, ring.emptied["V"])
                v.wait_ge(tri_ready, 2)

                with v.Fori(0, PAIRS) as t:
                    def then(ins):
                        ins.then_inc(*step.up())
                        v.wait_ge(*step.now(t))

                    for s in two:
                        v.wait_ge(*x_in[s].at(t, 16))
                        layernorm_stats(nc, v, t, K, X[s], halves[s], stats[s], step, stat)
                    for s in two:
                        v.wait_ge(*rs.at(t, s + 1))
                        v.wait_ge(*stored[s].at(t, 0))
                        for i in range(NT):
                            nc.vector.tensor_scalar(XG[s][:, i, 0:D], X[s][:, i, :], stats[s][:, i, 0:1], rstd[s][:, i:i + 1],
                                                    ALU.subtract, ALU.mult).then_inc(*normed.up())
                    over = lambda x: x[:].unsqueeze(2).broadcast_to([P, NT, E_])
                    for s in two:
                        v.wait_ge(*ring.ready(t, ("logits", s)))
                        nc.vector.tensor_copy(lg[s][:], ring.bank(("logits", s))[:, 0:NT * E_].rearrange("p (t e) -> p t e", t=NT))\
                            .then_inc(*ring.out(("logits", s)))
                        v.wait_ge(*ring.moved(t, ("logits", s)))
                        then(nc.vector.tensor_reduce(mx[s][:], lg[s][:], AX, ALU.max))
                        nc.vector.tensor_tensor(zz[s][:], lg[s][:], over(mx[s]), ALU.subtract).then_inc(*shifted.up())
                    for s in two:
                        b = t * STREAMS + s
                        v.wait_ge(*expd.at(t, s + 1))
                        then(nc.vector.tensor_reduce(sm[s][:], ex[s][:], AX, ALU.add))
                        then(nc.vector.reciprocal(rc[s][:], sm[s][:]))
                        prob = XG[s][:, :, D:ROW]
                        nc.vector.tensor_tensor(prob, ex[s][:], over(rc[s]), ALU.mult).then_inc(*rows_ready.up())
                        v.wait_ge(*rows_ready.now(t))
                        other = prob.unsqueeze(2).broadcast_to([P, NT, E_, E_])
                        own = prob.unsqueeze(3).broadcast_to([P, NT, E_, E_])
                        then(nc.vector.tensor_tensor(gt[s][:], other, own, ALU.is_gt))
                        then(nc.vector.tensor_tensor(eq[s][:], other, own, ALU.is_equal))
                        then(nc.vector.tensor_tensor(eq[s][:], eq[s][:], tri[:].unsqueeze(1).broadcast_to([P, NT, E_, E_]), ALU.mult))
                        then(nc.vector.tensor_tensor(gt[s][:], gt[s][:], eq[s][:], ALU.add))
                        then(nc.vector.tensor_reduce(rank[s][:], gt[s][:], AX, ALU.add))
                        then(nc.vector.tensor_tensor(bp[s][:], gt[s][:], other, ALU.mult))
                        then(nc.vector.tensor_reduce(prec[s][:], bp[s][:], AX, ALU.add))
                        then(nc.vector.tensor_scalar(sel[s][:], prec[s][:], 0.9, None, ALU.is_lt))
                        then(nc.vector.tensor_scalar(rank[s][:], rank[s][:], -1.0, -1.0, ALU.mult, ALU.add))
                        then(nc.vector.tensor_tensor(q[s][:], prob, rank[s][:], ALU.add))
                        then(nc.vector.tensor_tensor(q[s][:], q[s][:], sel[s][:], ALU.mult))
                        then(nc.vector.tensor_scalar(sel[s][:], sel[s][:], 1.0e9, -1.0e9, ALU.mult, ALU.add))
                        then(nc.vector.tensor_tensor(K.R[:, :, b, :].rearrange("p e t -> p t e"), q[s][:], sel[s][:], ALU.add))
                    step.close(), stat.close(), normed.close(), shifted.close(), rows_ready.close(), ring.emptied["V"].close()

            @block.scalar
            def _(act):
                credit(act, ring.emptied["S"], *stored)
                with act.Fori(0, PAIRS) as t:
                    for s in two:
                        for k in range(KD):
                            act.wait_ge(*ring.ready(t, ("xT", s, k)))
                            nc.scalar.activation(XT[s][:, k, :], ring.bank(("xT", s, k))[:], ACT.Copy).then_inc(*ring.out(("xT", s, k)))
                    for s in two:
                        act.wait_ge(*shifted.at(t, s + 1))
                        nc.scalar.activation(ex[s][:], zz[s][:], ACT.Exp).then_inc(*expd.up())
                    for s in two:
                        act.wait_ge(*rows_ready.at(t, s + 1))
                        act.dma_start(gb[t * STREAMS + s], XG[s][:]).then_inc(stored[s].sem, 16)
                    expd.close(), ring.emptied["S"].close()
                for s in two:
                    act.wait_ge(*stored[s].at(PAIRS, 0))

            @block.tensor
            def _(pe):
                credit(pe, ring.full)
                pe.wait_ge(w_in, 16)
                with pe.Fori(0, PAIRS) as t:
                    for s in two:
                        pe.wait_ge(*normed.at(t, NT * (s + 1)))
                        for k in range(KD):
                            bank = ring.take(pe, t, ("xT", s, k))
                            for i in range(NT):
                                mm = nc.tensor.transpose(bank[:, i * P:(i + 1) * P], XG[s][:, i, k * P:(k + 1) * P], K.ident[:])
                            mm.then_inc(*ring.full.up())
                    for s in two:
                        pe.wait_ge(*ring.moved(t, ("xT", s, KD - 1)))
                        bank = ring.take(pe, t, ("logits", s))
                        for i in range(NT):
                            for k in range(KD):
                                mm = nc.tensor.matmul(bank[:, i * E_:(i + 1) * E_], XT[s][:, k, i * P:(i + 1) * P], gw[:, k, :],
                                                      start=(k == 0), stop=(k == KD - 1))
                        mm.then_inc(*ring.full.up())
                    ring.close_pe()


def routing_phase(nc, A, K):
    R = Store(nc, "route")
    BF = mybir.dt.bfloat16
    LO, HI = 32, CAP // 32
    with R.stack:
        T, Tn, cnt, ok, stepc, left = (R.sb(n, [E_]) for n in "T Tn cnt ok stepc left".split())
        cmp_, gtm, eqm, within, tot, M, pos, lo, hi, posf = (R.sb(n, [E_, COLS]) for n in "cmp gtm eqm within tot M pos lo hi posf".split())
        posi, hii, loi = (R.sb(n, [E_, COLS], I32) for n in "posi hii loi".split())
        keep1 = R.sb("segments", [E_, COLS])
        ones, before = R.sb("ones", [P]), R.sb("before", [P])
        hiota, liota = R.sb("hi_iota", [HI]), R.sb("lo_iota", [LO])
        ciota, piota = R.sb("col_iota", [COLS]), R.sb("part_iota", [1])
        LH = R.sb("hot_hi", [E_, COLS, 96], BF)
        RL = R.sb("hot_lo", [E_, COLS, LO], BF)
        vacant = R.rows("vacant", [HI, E_, LO])
        i1, i2, un = (R.rows(n, [HI, E_, LO]) for n in ("i1", "i2", "un"))
        slots = R.rows("slots", [HI, E_, LO], I32)
        banks = R.banks()
        const = R.sem("consts")
        step = Sig(R.sem("vector_step"), 4)
        counted = Sig(R.sem("counted"), 1)
        partial = Sig(R.sem("partial_counts"), 1)
        st2 = Sig(R.sem("tail_step"), 0)
        masks, sums = R.sem("mask_ready"), R.sem("mask_summed")
        hot, made, listed, listed_in, out_ready = R.sem("hot_ready"), R.sem("lists_made"), R.sem("list_stored"), R.sem("list_in"), R.sem("slots_ready")
        cs, cs2 = Sig(R.sem("const_step"), 0), Sig(R.sem("start_step"), 0)
        halved = Sig(R.sem("step_halved"), 1)
        ITER = 29
        over = lambda x: x[:].unsqueeze(2).broadcast_to([P, E_, COLS])
        flat = lambda x: x[:].rearrange("p e c -> p (e c)")
        with nc.Block() as block:
            @block.gpsimd
            def _(pool):
                nc.gpsimd.memset(ones[:], 1.0).then_inc(const, 1)
                nc.gpsimd.memset(before[:], 1.0).then_inc(*cs.up())
                pool.wait_ge(*cs.now(0))
                nc.gpsimd.affine_select(out=before[:], in_=before[:], compare_op=ALU.is_gt, fill=0.0, base=0,
                                        pattern=[[1, P]], channel_multiplier=-1).then_inc(const, 1)
                nc.gpsimd.memset(keep1[:], 1.0).then_inc(*cs.up())
                pool.wait_ge(*cs.now(0))
                nc.gpsimd.memset(keep1[:, :, 0:1], 0.0).then_inc(const, 1)
                nc.gpsimd.iota(hiota[:], [[1, HI]], 0, 0, allow_small_or_imprecise_dtypes=True).then_inc(const, 1)
                nc.gpsimd.iota(liota[:], [[1, LO]], 0, 0, allow_small_or_imprecise_dtypes=True).then_inc(const, 1)
                nc.gpsimd.iota(ciota[:], [[1, COLS]], 0, 0, allow_small_or_imprecise_dtypes=True).then_inc(const, 1)
                nc.gpsimd.iota(piota[:], [[1, 1]], 0, 1, allow_small_or_imprecise_dtypes=True).then_inc(const, 1)
                nc.gpsimd.iota(vacant[:], [[0, E_], [1, LO]], N, LO, allow_small_or_imprecise_dtypes=True).then_inc(const, 1)
                nc.gpsimd.memset(LH[:], 0.0).then_inc(const, 1)

            @block.vector
            def _(v):
                nc.vector.memset(T[:], -8.0).then_inc(*cs2.up())
                nc.vector.memset(stepc[:], 4.0).then_inc(*cs2.up())
                v.wait_ge(*cs2.now(0))
                v.wait_ge(const, 9)
                with v.Fori(0, ITER) as t:
                    def then(ins):
                        ins.then_inc(*step.up())
                        v.wait_ge(*step.now(t))
                    then(nc.vector.tensor_tensor(Tn[:], T[:], stepc[:], ALU.add))
                    then(nc.vector.tensor_tensor(cmp_[:], K.R[:].rearrange("p e b t -> p e (b t)"), over(Tn), ALU.is_ge))
                    nc.vector.tensor_reduce(cnt[:], cmp_[:], AX, ALU.add).then_inc(*partial.up())
                    v.wait_ge(*counted.at(t, 1))
                    nc.vector.scalar_tensor_tensor(out=ok[:], in0=banks[0][:, 0:E_], scalar=float(CAP) - 0.5, in1=stepc[:],
                                                   op0=ALU.is_gt, op1=ALU.mult).then_inc(*step.up())
                    v.wait_ge(*step.now(t))
                    nc.vector.tensor_tensor(T[:], T[:], ok[:], ALU.add).then_inc(*step.up())
                    v.wait_ge(*step.now(t))
                    nc.vector.tensor_scalar(stepc[:], stepc[:], 0.5, None, ALU.mult).then_inc(*halved.up())
                    v.wait_ge(*halved.now(t))
                    step.close(), partial.close(), halved.close()

                def then2(ins):
                    ins.then_inc(*st2.up())
                    v.wait_ge(*st2.now(0))

                Rv = K.R[:].rearrange("p e b t -> p e (b t)")
                def prefix(base):
                    then2(nc.vector.tensor_copy(flat(tot), banks[base + 1][:, 0:E_ * COLS]))
                    then2(nc.vector.tensor_tensor_scan(flat(pos), flat(keep1), flat(tot), 0.0, ALU.mult, ALU.add))
                    then2(nc.vector.tensor_tensor(pos[:], pos[:], tot[:], ALU.subtract))
                    then2(nc.vector.tensor_tensor(flat(pos), banks[base][:, 0:E_ * COLS], flat(pos), ALU.add))

                then2(nc.vector.tensor_tensor(gtm[:], Rv, over(T), ALU.is_gt))
                nc.vector.tensor_tensor(eqm[:], Rv, over(T), ALU.is_equal).then_inc(masks, 1)
                then2(nc.vector.tensor_reduce(cnt[:], gtm[:], AX, ALU.add))
                nc.vector.tensor_copy(ok[:], cnt[:]).then_inc(masks, 1)
                v.wait_ge(sums, 1)
                prefix(1)
                v.wait_ge(sums, 2)
                then2(nc.vector.tensor_scalar(left[:], banks[0][:, 0:E_], -1.0, float(CAP), ALU.mult, ALU.add))
                then2(nc.vector.tensor_tensor(M[:], pos[:], over(left), ALU.is_lt))
                then2(nc.vector.tensor_tensor(M[:], M[:], eqm[:], ALU.mult))
                nc.vector.tensor_tensor(M[:], M[:], gtm[:], ALU.add).then_inc(masks, 1)
                v.wait_ge(masks, 3)
                v.wait_ge(sums, 3)
                prefix(3)
                then2(nc.vector.tensor_copy(posi[:], pos[:]))
                then2(nc.vector.tensor_scalar(hii[:], posi[:], 5, None, ALU.arith_shift_right))
                then2(nc.vector.tensor_scalar(loi[:], posi[:], LO - 1, None, ALU.bitwise_and))
                then2(nc.vector.tensor_copy(hi[:], hii[:]))
                then2(nc.vector.tensor_copy(lo[:], loi[:]))
                then2(nc.vector.tensor_scalar(cmp_[:], M[:], 1000.0, -1000.0, ALU.mult, ALU.add))
                then2(nc.vector.tensor_tensor(hi[:], hi[:], cmp_[:], ALU.add))
                for e in range(E_):
                    wide = lambda x, n: x[:, e, :].unsqueeze(2).broadcast_to([P, COLS, n])
                    hot_hi = LH[:, e, :, 0:HI]
                    then2(nc.vector.tensor_tensor(hot_hi, wide(hi, HI), hiota[:].unsqueeze(1).broadcast_to([P, COLS, HI]), ALU.is_equal))
                    nc.vector.tensor_tensor(RL[:, e], wide(lo, LO), liota[:].unsqueeze(1).broadcast_to([P, COLS, LO]), ALU.is_equal).then_inc(*st2.up())
                    nc.vector.tensor_scalar(LH[:, e, :, 32:32 + HI], hot_hi, piota[:, 0:1], None, ALU.mult).then_inc(*st2.up())
                    nc.vector.tensor_tensor(LH[:, e, :, 64:64 + HI], hot_hi, ciota[:].unsqueeze(2).broadcast_to([P, COLS, HI]), ALU.mult).then_inc(hot, 1)
                v.wait_ge(made, 1)
                L = banks[5]
                fl = lambda x: x[:].rearrange("p e l -> p (e l)")
                then2(nc.vector.tensor_scalar(fl(i1), L[64:64 + HI, 0:E_ * LO], float(P), None, ALU.mult))
                then2(nc.vector.tensor_tensor(fl(i2), L[32:32 + HI, 0:E_ * LO], fl(i1), ALU.add))
                then2(nc.vector.tensor_scalar(fl(un), L[0:HI, 0:E_ * LO], -1.0, 1.0, ALU.mult, ALU.add))
                then2(nc.vector.tensor_tensor(un[:], un[:], vacant[:], ALU.mult))
                nc.vector.tensor_tensor(slots[:], i2[:], un[:], ALU.add).then_inc(out_ready, 1)

            @block.tensor
            def _(pe):
                pe.wait_ge(const, 9)
                with pe.Fori(0, ITER) as t:
                    pe.wait_ge(*partial.at(t, 1))
                    nc.tensor.matmul(banks[0][:, 0:E_], ones[:], cnt[:], start=True, stop=True).then_inc(*counted.up())
                    counted.close()
                pe.wait_ge(masks, 1)
                nc.tensor.matmul(banks[1][:, 0:E_ * COLS], before[:], flat(eqm), start=True, stop=True)
                nc.tensor.matmul(banks[2][:, 0:E_ * COLS], ones[:], flat(eqm), start=True, stop=True).then_inc(sums, 1)
                pe.wait_ge(masks, 2)
                nc.tensor.matmul(banks[0][:, 0:E_], ones[:], ok[:], start=True, stop=True).then_inc(sums, 1)
                pe.wait_ge(masks, 3)
                nc.tensor.matmul(banks[3][:, 0:E_ * COLS], before[:], flat(M), start=True, stop=True)
                nc.tensor.matmul(banks[4][:, 0:E_ * COLS], ones[:], flat(M), start=True, stop=True).then_inc(sums, 1)
                for e in range(E_):
                    pe.wait_ge(hot, e + 1)
                    for c in range(COLS):
                        mm = nc.tensor.matmul(banks[5][0:96, e * LO:(e + 1) * LO], LH[:, e, c, :], RL[:, e, c, :],
                                              start=(c == 0), stop=(c == COLS - 1))
                mm.then_inc(made, 1)

            @block.sync
            def _(sp):
                sp.wait_ge(out_ready, 1)
                sp.dma_start(K.slots_d[:, :].rearrange("e (h l) -> h e l", h=HI), slots[:]).then_inc(listed, 16)
                sp.wait_ge(listed, 16)
                sp.dma_start(K.idx[:], K.slots_d[:, :].rearrange("e (t p) -> p e t", p=P), allow_slow_non_contiguous=True).then_inc(listed_in, 16)
                sp.wait_ge(listed_in, 16)


def expert_phase(nc, A, K):
    R = Store(nc, "expert")
    TURNS = E_ // STREAMS
    with R.stack:
        two = range(STREAMS)
        W1 = [R.sb(f"w1{s}", [KD, F_]) for s in two]
        W2 = [R.sb(f"w2{s}", [KF, D]) for s in two]
        GX = [R.sb(f"rows{s}", [SLOTS, ROW]) for s in two]
        XT = [R.sb(f"xT{s}", [KD, CAP]) for s in two]
        HT = [R.sb(f"hT{s}", [KF, CAP]) for s in two]
        Y = [R.sb(f"y{s}", [SLOTS, D]) for s in two]
        sc = [R.sb(f"share{s}", [SLOTS]) for s in two]
        ic = [R.sb(f"idx{s}", [SLOTS], I32) for s in two]
        gb, tg = R.sb("g", [1]), R.sb("tanh_g", [1])
        groups = [(("xT", s, k), "S") for s in two for k in range(KD)]
        groups += [(("hT", s, m), "S") for s in two for m in range(KF)]
        groups += [(("y", s, i), "V") for s in two for i in range(SLOTS // 2)]
        ring = Ring(R.banks(), groups, R.sem("bank_full"), {"V": R.sem("emptied_V"), "S": R.sem("emptied_S")})
        g_in, tgs = R.sem("g_in"), R.sem("tanh_ready")
        w_in = [Sig(R.sem(f"weights_in{s}"), 32) for s in two]
        copied = Sig(R.sem("idx_copied"), STREAMS)
        rows_in = [Sig(R.sem(f"rows_in{s}"), 16 * SLOTS) for s in two]
        share = Sig(R.sem("share_ready"), STREAMS)
        added = [Sig(R.sem(f"rows_added{s}"), 16 * SLOTS) for s in two]
        y_free = Sig(R.sem("y_free"), STREAMS, STREAMS)
        w1 = A["w1T"].rearrange("e (k p) f -> e p k f", p=P)
        w2 = A["w2T"].rearrange("e (k p) d -> e p k d", p=P)
        with nc.Block() as block:
            @block.sync
            def _(sp):
                sp.dma_start(gb[:], A["g_ffn"][0:1].partition_broadcast(P)).then_inc(g_in, 16)
                with sp.Fori(0, TURNS) as t:
                    for s in two:
                        sp.wait_ge(*ring.used(t, ("y", s, SLOTS // 2 - 1)))
                        sp.dma_start(W1[s][:], w1[t * STREAMS + s]).then_inc(w_in[s].sem, 16)
                        sp.dma_start(W2[s][:], w2[t * STREAMS + s]).then_inc(w_in[s].sem, 16)

            @block.gpsimd
            def _(pool):
                def add_rows(t, s):
                    for i in range(SLOTS):
                        hold(pool, K.pool_passed, *ring.moved(t, ("y", s, i // 2)))
                        pool.indirect_dma_start(K.x2_d[:, :], bass.IndirectOffsetOnAxis(ap=ic[s][:, i:i + 1], axis=0),
                                                Y[s][:, i, :], None, compute_op=ALU.add).then_inc(added[s].sem, 16)
                    pool.wait_ge(*added[s].at(t, 16 * SLOTS))
                    pool.sem_inc(y_free.sem, 1)

                def gather(t, s):
                    nc.gpsimd.tensor_copy(ic[s][:], K.idx[:, t * STREAMS + s, :]).then_inc(copied.sem, 1)
                    hold(pool, K.pool_passed, *copied.at(t, s + 1))
                    for i in range(SLOTS):
                        pool.indirect_dma_start(GX[s][:, i, :], None, K.xg_d[:, :],
                                                bass.IndirectOffsetOnAxis(ap=ic[s][:, i:i + 1], axis=0)).then_inc(rows_in[s].sem, 16)

                credit(pool, y_free)
                for s in two:
                    gather(0, s)
                with pool.Fori(1, TURNS) as t:
                    for s in two:
                        add_rows(t - 1, s)
                        gather(t, s)
                for s in two:
                    add_rows(TURNS - 1, s)

            @block.scalar
            def _(act):
                act.wait_ge(g_in, 16)
                nc.scalar.activation(tg[:], gb[:], ACT.Tanh).then_inc(tgs, 1)
                credit(act, ring.emptied["S"])
                with act.Fori(0, TURNS) as t:
                    for s in two:
                        for k in range(KD):
                            act.wait_ge(*ring.ready(t, ("xT", s, k)))
                            nc.scalar.activation(XT[s][:, k, :], ring.bank(("xT", s, k))[:], ACT.Copy).then_inc(*ring.out(("xT", s, k)))
                    for s in two:
                        for m in range(KF):
                            act.wait_ge(*ring.ready(t, ("hT", s, m)))
                            nc.scalar.activation(HT[s][:, m, :], ring.bank(("hT", s, m))[:], ACT.Gelu).then_inc(*ring.out(("hT", s, m)))
                    ring.emptied["S"].close()

            @block.vector
            def _(v):
                credit(v, ring.emptied["V"])
                v.wait_ge(tgs, 1)
                with v.Fori(0, TURNS) as t:
                    for s in two:
                        v.wait_ge(*rows_in[s].at(t, 16 * SLOTS))
                        nc.vector.tensor_scalar(sc[s][:], GX[s][:, :, D + t * STREAMS + s], tg[:, 0:1], None, ALU.mult).then_inc(*share.up())
                    for s in two:
                        v.wait_ge(*share.at(t, s + 1))
                        v.wait_ge(*y_free.prev(t, s + 1))
                        for i in range(SLOTS):
                            name = ("y", s, i // 2)
                            if i % 2 == 0:
                                v.wait_ge(*ring.ready(t, name))
                            ins = nc.vector.tensor_scalar(Y[s][:, i, :], ring.bank(name)[:, i % 2 * D:(i % 2 + 1) * D], sc[s][:, i:i + 1], None, ALU.mult)
                            if i % 2:
                                ins.then_inc(*ring.out(name))
                    share.close(), ring.emptied["V"].close()

            @block.tensor
            def _(pe):
                credit(pe, ring.full)
                with pe.Fori(0, TURNS) as t:
                    for s in two:
                        pe.wait_ge(*rows_in[s].at(t, 16 * SLOTS))
                        for k in range(KD):
                            bank = ring.take(pe, t, ("xT", s, k))
                            for i in range(SLOTS):
                                mm = nc.tensor.transpose(bank[:, i * P:(i + 1) * P], GX[s][:, i, k * P:(k + 1) * P], K.ident[:])
                            mm.then_inc(*ring.full.up())
                    for s in two:
                        pe.wait_ge(*w_in[s].at(t, 32))
                        pe.wait_ge(*ring.moved(t, ("xT", s, KD - 1)))
                        for m in range(KF):
                            bank = ring.take(pe, t, ("hT", s, m))
                            for k in range(KD):
                                mm = nc.tensor.matmul(bank[:], W1[s][:, k, m * P:(m + 1) * P], XT[s][:, k, :], start=(k == 0), stop=(k == KD - 1))
                            mm.then_inc(*ring.full.up())
                    for s in two:
                        pe.wait_ge(*ring.moved(t, ("hT", s, KF - 1)))
                        for g in range(SLOTS // 2):
                            bank = ring.take(pe, t, ("y", s, g))
                            for i in range(2):
                                for m in range(KF):
                                    mm = nc.tensor.matmul(bank[:, i * D:(i + 1) * D], HT[s][:, m, (2 * g + i) * P:(2 * g + i + 1) * P], W2[s][:, m, :],
                                                          start=(m == 0), stop=(m == KF - 1))
                            mm.then_inc(*ring.full.up())
                    ring.close_pe()


def retrieval_phase(nc, A, K):
    R = Store(nc, "retr")
    two = range(STREAMS)
    PARTS = ((0,), (1, 3), (2,))
    with R.stack:
        X, Q, C, ST, Z = ([R.sb(f"{n}{s}", shape) for s in two] for n, shape in
                          (("x", [NT, D]), ("q", [NT, D]), ("cT", [KD, S]), ("scores", [NT, S]), ("y", [NT, D])))
        halves = [R.sb(f"halves{s}", [NT, 6]) for s in two]
        stats = [R.sb(f"stats{s}", [NT, 2]) for s in two]
        vare, rstd = ([R.sb(f"{n}{s}", [NT]) for s in two] for n in ("vare", "rstd"))
        gb, tg = R.sb("g", [1]), R.sb("tanh_g", [1])
        groups = [(("s", s, j), "S") for s in two for j in range(len(PARTS))] + [(("p", s, g), "V") for s in two for g in range(NT // 2)]
        ring = Ring(R.banks(), groups, R.sem("bank_full"), {"V": R.sem("emptied_V"), "S": R.sem("emptied_S")})
        g_in, tgs = R.sem("g_in"), R.sem("tanh_ready")
        x_in = [Sig(R.sem(f"x_in{s}"), 16) for s in two]
        c_in = [Sig(R.sem(f"ctx_in{s}"), 16) for s in two]
        stored = [Sig(R.sem(f"stored{s}"), 32, 32) for s in two]
        step = Sig(R.sem("vector_step"), STREAMS * 2 * NT)
        stat = Sig(R.sem("stats_ready"), 2 * STREAMS * NT)
        normed = Sig(R.sem("x_normed"), STREAMS)
        masked = Sig(R.sem("scores_masked"), STREAMS)
        x3 = Sig(R.sem("x3_ready"), STREAMS)
        y0 = Sig(R.sem("y_ready"), STREAMS)
        pstep = Sig(R.sem("pool_step"), 2 * STREAMS)
        rs = Sig(R.sem("rstd_ready"), 2 * STREAMS)
        rows = lambda d: d.rearrange("(b t p) d -> b p t d", p=P, t=NT)
        xb, x3b, yb = rows(K.x2_d[0:N, :]), rows(K.x3_d[:, :]), rows(K.y_d[0:N, :])
        with nc.Block() as block:
            @block.sync
            def _(sp):
                sp.dma_start(gb[:], A["g_xattn"][1:2].partition_broadcast(P)).then_inc(g_in, 16)
                with sp.Fori(0, PAIRS) as t:
                    for s in two:
                        sp.wait_ge(*ring.used(t, ("s", s, 2)))
                        sp.dma_start(C[s][:], K.ctxT_d[t * STREAMS + s]).then_inc(c_in[s].sem, 16)
                        sp.wait_ge(*stored[s].at(t, 0))
                        sp.dma_start(X[s][:], xb[t * STREAMS + s]).then_inc(x_in[s].sem, 16)

            @block.gpsimd
            def _(pool):
                with pool.Fori(0, PAIRS) as t:
                    for s in two:
                        rstd_on_pool(nc, pool, t, K, stats[s], vare[s], rstd[s], 1e-5, stat, pstep, rs)
                    for s in two:
                        hold(pool, K.pool_passed, *ring.moved(t, ("s", s, 2)))
                        diag = ST[s][:, :, 0:P]
                        nc.gpsimd.affine_select(out=diag, in_=diag, compare_op=ALU.is_ge, fill=0.0, base=0,
                                                pattern=[[0, NT], [1, P]], channel_multiplier=-1).then_inc(*masked.up())
                    for s in two:
                        rstd_on_pool(nc, pool, t, K, stats[s], vare[s], rstd[s], 1e-5, stat, pstep, rs)
                    pstep.close(), rs.close(), masked.close()

            @block.vector
            def _(v):
                credit(v, ring.emptied["V"])
                v.wait_ge(tgs, 1)
                with v.Fori(0, PAIRS) as t:
                    for s in two:
                        v.wait_ge(*x_in[s].at(t, 16))
                        layernorm_stats(nc, v, t, K, X[s], halves[s], stats[s], step, stat)
                    for s in two:
                        v.wait_ge(*rs.at(t, s + 1))
                        for i in range(NT):
                            ins = nc.vector.tensor_scalar(Q[s][:, i, :], X[s][:, i, :], stats[s][:, i, 0:1], rstd[s][:, i:i + 1], ALU.subtract, ALU.mult)
                        ins.then_inc(*normed.up())
                    for s in two:
                        v.wait_ge(*stored[s].at(t, 0))
                        for g in range(NT // 2):
                            name, rows2 = ("p", s, g), slice(2 * g, 2 * g + 2)
                            v.wait_ge(*ring.ready(t, name))
                            psum = ring.bank(name)[:].rearrange("p (t d) -> p t d", t=2)
                            nc.vector.tensor_tensor(Z[s][:, rows2, :], psum, Q[s][:, rows2, :], ALU.add).then_inc(*ring.out(name))
                        v.wait_ge(*ring.moved(t, ("p", s, NT // 2 - 1)))
                        nc.vector.scalar_tensor_tensor(out=X[s][:], in0=Z[s][:], scalar=tg[:, 0:1], in1=X[s][:], op0=ALU.mult, op1=ALU.add).then_inc(*x3.up())
                        v.wait_ge(*x3.now(t))
                        layernorm_stats(nc, v, t, K, X[s], halves[s], stats[s], step, stat)
                    for s in two:
                        v.wait_ge(*rs.at(t, STREAMS + s + 1))
                        for i in range(NT):
                            ins = nc.vector.tensor_scalar(Z[s][:, i, :], X[s][:, i, :], stats[s][:, i, 0:1], rstd[s][:, i:i + 1], ALU.subtract, ALU.mult)
                        ins.then_inc(*y0.up())
                    step.close(), stat.close(), normed.close(), x3.close(), y0.close(), ring.emptied["V"].close()

            @block.scalar
            def _(act):
                act.wait_ge(g_in, 16)
                nc.scalar.activation(tg[:], gb[:], ACT.Tanh).then_inc(tgs, 1)
                credit(act, ring.emptied["S"], *stored)
                with act.Fori(0, PAIRS) as t:
                    for s in two:
                        for g, js in enumerate(PARTS):
                            act.wait_ge(*ring.ready(t, ("s", s, g)))
                            at = 0
                            for j in js:
                                n = S - j * P
                                ins = nc.scalar.activation(ST[s][:, j, 0:n], ring.bank(("s", s, g))[:, at:at + n], ACT.Copy)
                                at += n
                            ins.then_inc(*ring.out(("s", s, g)))
                    for s in two:
                        act.wait_ge(*x3.at(t, s + 1))
                        act.dma_start(x3b[t * STREAMS + s], X[s][:]).then_inc(stored[s].sem, 16)
                        act.wait_ge(*y0.at(t, s + 1))
                        act.dma_start(yb[t * STREAMS + s], Z[s][:]).then_inc(stored[s].sem, 16)
                    ring.emptied["S"].close()
                for s in two:
                    act.wait_ge(*stored[s].at(PAIRS, 0))

            @block.tensor
            def _(pe):
                credit(pe, ring.full)
                with pe.Fori(0, PAIRS) as t:
                    for s in two:
                        pe.wait_ge(*c_in[s].at(t, 16))
                        for g, js in enumerate(PARTS):
                            bank = ring.take(pe, t, ("s", s, g))
                            at = 0
                            for j in js:
                                n = S - j * P
                                for k in range(KD):
                                    mm = nc.tensor.matmul(bank[:, at:at + n], C[s][:, k, j * P:(j + 1) * P], C[s][:, k, j * P:S], start=(k == 0), stop=(k == KD - 1))
                                at += n
                            mm.then_inc(*ring.full.up())
                    for s in two:
                        pe.wait_ge(*normed.at(t, s + 1))
                        pe.wait_ge(*masked.at(t, s + 1))
                        for g in range(NT // 2):
                            bank = ring.take(pe, t, ("p", s, g))
                            for i in (2 * g, 2 * g + 1):
                                for j in range(i + 1):
                                    mm = nc.tensor.matmul(bank[:, i % 2 * D:(i % 2 + 1) * D], ST[s][:, j, (i - j) * P:(i - j + 1) * P], Q[s][:, j, :],
                                                          start=(j == 0), stop=(j == i))
                            mm.then_inc(*ring.full.up())
                    ring.close_pe()
LAYERS = 2
LH = 8
LD = 64
INNER = LH * LD
HID = 682
MH = -(-HID // P)
TAIL = HID - (MH - 1) * P
PAIRS_H = INNER // P
SMALL, TABLES = 16 * 7, 16 * 4
FAR = -3.0e38


def start_ring(engine, sig, before, work):
    engine.sem_inc(sig.sem, before)
    sig.n = before
    work()
    engine.wait_ge(sig.sem, sig.n)
    engine.sem_inc(sig.sem, sig.per - sig.n)
    sig.n = 0


def layer_phase(nc, A, K):
    R = Store(nc, "layer")
    two = range(STREAMS)
    TILE_UNITS = [(i, s) for i in range(NT) for s in two]
    HEAD_UNITS = [(h, s) for h in range(LH) for s in two]
    U, V1 = len(HEAD_UNITS), LD + 1
    TLAG, PLAG, VLAG, RB, TR, TB = 2, 2, 4, 4, 3, 2
    with R.stack:
        weight = lambda n, shape: [R.sb(f"{n}_high", shape, R32), R.sb(f"{n}_low", shape)]
        Wqkv, Wo, W1, W2 = (weight(n, shape) for n, shape in (("wqkv", [KD, 3 * INNER]), ("wo", [PAIRS_H, D]), ("w1", [KD, 2 * HID]), ("w2", [MH, D])))
        Wqkv, Wo, W1, W2 = ((x[0], R.rounded(f"{n}_low", list(x[1].shape[1:])), x[1]) for n, x in (("wqkv", Wqkv), ("wo", Wo), ("w1", W1), ("w2", W2)))
        ba, bg, b2 = R.sb("b1_a", [MH]), R.sb("b1_g", [MH]), R.sb("b2", [D])
        lng, lnb = R.sb("ln_g", [KD]), R.sb("ln_b", [KD])
        qks = R.sb("qk_scale", [2, LD])
        At, Bt = R.sb("along", [NT, 2, LD]), R.sb("across", [NT, 2, LD])
        gb, tg = R.sb("g", [1]), R.sb("tanh_g", [1])
        mask = R.sb("mask", [2, P])
        shift, carry = R.sb("shift", [P]), R.sb("carry", [P])
        Y = [R.sb(f"y{s}", [NT, D]) for s in two]
        HT = [R.sb(f"hT{s}", [KD, S + 1], R32) for s in two]
        V = [R.sb(f"v{s}", [NT, LH, V1]) for s in two]
        QKT = [R.sb(f"qkT{s}", [2 * PAIRS_H, S]) for s in two]
        O = [R.sb(f"o{s}", [NT, INNER]) for s in two]
        OB = [R.sb(f"oT{s}", [2 + PAIRS_H * S], R32) for s in two]
        T1 = [R.sb(f"along_t{i}", [2 * LH, LD]) for i in range(TB)]
        ss, pw, rn = ([R.sb(f"{n}{i}", [2 * LH]) for i in range(TB)] for n in ("ss", "pw", "rn"))
        SM, PT = ([R.sb(f"{n}{i}", [NT, 2, P]) for i in range(c)] for n, c in (("scores", RB), ("probsT", TR)))
        nmax, rden = ([R.sb(f"{n}{i}", [NT]) for i in range(RB)] for n in ("nmax", "rden"))
        halves = [R.sb(f"halves{s}", [NT, 2, 6]) for s in two]
        stats = [R.sb(f"stats{s}", [NT, 2]) for s in two]
        vare, rstd = ([R.sb(f"{n}{s}", [NT]) for s in two] for n in ("vare", "rstd"))

        flat3 = lambda x: x[:].rearrange("p w b j -> p (w b j)")
        SQ, T2 = ([flat3(x).rearrange("p (h d) -> p h d", d=LD) for x in part] for part in (SM[0:TB], SM[TB:2 * TB]))
        GL = [flat3(SM[i // 2])[:, i % 2 * S:(i % 2 + 1) * S] for i in range(RB)]
        X3 = [x[:].rearrange("p (t a) d -> p t (a d)", t=NT) for x in T1]
        Z = [x[:, :, 0:D] for x in O]
        OT = [x[:, 2:2 + PAIRS_H * S].rearrange("p (k n) -> p k n", n=S) for x in OB]
        QKR = [R.rounded(f"qkT{s}", [2 * PAIRS_H, S]) for s in two]
        OTL = [x[:, 0:PAIRS_H, :] for x in QKR]
        HH = [x[:, 0:MH, :] for x in QKR]
        SPARE = [flat3(x) for x in PT[0:3] + SM[2:3]]
        SPARER = [flat3(R.rounded(n, [NT, 2, P])) for n in ("probsT0", "probsT1", "probsT2", "scores2")]
        AFF = lambda s, k: SPARE[s * KD + k][:, 0:S]

        def hidden(s, m, low=False):
            if m < 2:
                return (QKR if low else QKT)[s][:, MH + m, :]
            return (SPARER if low else SPARE)[2 * s + (m - 2) // 2][:, m % 2 * S:(m % 2 + 1) * S]

        def hT(s, k, at=0, n=S):
            low = OB[s][:, 1 + at:1 + at + n] if k else OB[s][:, S + 2 + at:S + 2 + at + n]
            return HT[s][:, k, k + at:k + at + n], low

        def late(s, k, i):
            return hT(s, k, i * P - k, P)

        groups = []
        for m in range(len(TILE_UNITS) + TLAG):
            if m < len(TILE_UNITS):
                groups += [(("q", m), "V"), (("k", m), "V"), (("v", m), "S")]
            if m >= TLAG:
                groups += [(("qkT", m - TLAG, c), "S") for c in range(2)]
        for k in range(U + VLAG):
            if k < U:
                groups += [(("sim", k, g), "V") for g in range(NT // 2)]
            if PLAG <= k < U + PLAG:
                groups += [(("pT", k - PLAG, 0), "S"), (("pT", k - PLAG, 1), "V")]
            if k >= VLAG:
                groups += [(("o", k - VLAG), "V")]
        groups += [(("oT", s, k), "V") for s in two for k in range(PAIRS_H)]
        groups += [(("wo", s, g), "V") for s in two for g in range(NT // 2)]
        groups += [(("late", s), "V") for s in two]
        groups += [(("nT", s, k), "V") for s in two for k in range(KD)]
        groups += [((n, s, m), w) for s in two for m in range(MH) for n, w in (("g", "S"), ("a", "V"))]
        hT_first = len(groups)
        groups += [(("hT", s, k), "V") for s in two for k in range(KD)]
        groups += [(("w2", s, g), "V") for s in two for g in range(NT // 2)]
        ring = Ring(R.banks(), groups, R.sem("bank_full"), {"V": R.sem("emptied_V"), "S": R.sem("emptied_S")})

        g_in, consts, mset, tgs, vones = R.sem("g_in"), R.sem("consts"), R.sem("mask_step"), R.sem("tanh_ready"), R.sem("ones_set")
        win = {n: R.sem(f"{n}_in") for n in "wqkv wo w1 w2 small tables".split()}
        weights = (("wqkv", Wqkv), ("wo", Wo), ("w1", W1))
        w_high, w_split, w2_split = (Sig(R.sem(n), c) for n, c in (("weights_high", 3), ("weights_split", 3), ("w2_split", 4)))
        tabs = Sig(R.sem("scaled_tables"), 4)
        y_in = [Sig(R.sem(f"y_in{s}"), 16) for s in two]
        x3_in = [Sig(R.sem(f"x3_in{s}"), 16) for s in two]
        stored = [Sig(R.sem(f"stored{s}"), 32, 32) for s in two]
        h_high = Sig(R.sem("hT_high"), STREAMS * KD, STREAMS * KD)
        o_high = Sig(R.sem("oT_high"), STREAMS * PAIRS_H)
        n_high, n_low = Sig(R.sem("nT_high"), STREAMS * KD), Sig(R.sem("nT_low"), STREAMS * KD)
        hid_high, hid_low = Sig(R.sem("hidden_high"), STREAMS * MH), Sig(R.sem("hidden_low"), STREAMS * MH)
        M8 = len(TILE_UNITS)
        sq = Sig(R.sem("squares_ready"), M8)
        ssum = Sig(R.sem("square_sums"), M8)
        pstep = Sig(R.sem("pool_step"), M8 + STREAMS)
        roped = Sig(R.sem("rotated"), M8)
        rnorm = Sig(R.sem("norm_ready"), M8)
        qk = Sig(R.sem("qk_ready"), M8, M8)
        smax = Sig(R.sem("scores_ready"), U)
        probs = Sig(R.sem("probs_ready"), U)
        rd = Sig(R.sem("sums_inverted"), U)
        stat = Sig(R.sem("stats_ready"), STREAMS * NT)
        step = Sig(R.sem("vector_step"), STREAMS * 2 * NT)
        rs = Sig(R.sem("rstd_ready"), STREAMS)
        yb2 = Sig(R.sem("bias_added"), STREAMS)
        fin = Sig(R.sem("out_ready"), STREAMS)
        rows = lambda d: d.rearrange("(b t p) d -> b p t d", p=P, t=NT)
        x3b, ob = rows(K.x3_d[:, :]), A["out"].rearrange("b (t p) d -> b p t d", p=P)
        yb = rows(K.y_d[:, :])

        with nc.Block() as block:
            @block.sync
            def _(sp):
                sp.dma_start(gb[:], A["g_ffn"][1:2].partition_broadcast(P)).then_inc(g_in, 16)
                for s in two:
                    sp.dma_start(Y[s][:], yb[s]).then_inc(y_in[s].sem, 16)
                with sp.Fori(0, LAYERS) as l:
                    t0 = l * PAIRS
                    sp.wait_ge(*ring.used(t0, ("v", M8 - 1)))
                    sp.dma_start(Wqkv[2][:], A["L1_ffn_wqkv"][l].rearrange("(k p) n -> p k n", p=P)).then_inc(win["wqkv"], 16)
                    sp.wait_ge(*ring.used(t0, ("wo", STREAMS - 1, NT // 2 - 1)))
                    sp.dma_start(Wo[2][:], A["L1_ffn_wo"][l].rearrange("(k p) n -> p k n", p=P)).then_inc(win["wo"], 16)
                    sp.wait_ge(*qk.prev(t0, M8))
                    sp.dma_start(At[:], A["cos"].rearrange("(t p) c d -> p t c d", p=P)).then_inc(win["tables"], 16)
                    sp.dma_start(Bt[:], A["sin"].rearrange("(t p) c d -> p t c d", p=P)).then_inc(win["tables"], 16)
                    for c, n in enumerate(("q", "k")):
                        sp.dma_start(qks[:, c, :], A[f"L1_ffn_{n}_scale"][l].partition_broadcast(P)).then_inc(win["tables"], 16)
                    sp.wait_ge(*ring.moved_before(t0, ("a", STREAMS - 1, MH - 1)))
                    sp.dma_start(W1[2][:], A["L1_ffn_w1"][l].rearrange("(k p) n -> p k n", p=P)).then_inc(win["w1"], 16)
                    sp.dma_start(b2[:], A["L1_ffn_b2"][l].partition_broadcast(P)).then_inc(win["small"], 16)
                    for tile, name in ((lng, "g"), (lnb, "b")):
                        sp.dma_start(tile[:], A[f"L1_ffn_ln_{name}"][l].rearrange("(k p) -> p k", p=P), allow_slow_non_contiguous=True).then_inc(win["small"], 16)
                    for tile, half in ((ba, 0), (bg, 1)):
                        b1 = A["L1_ffn_b1"][l][half * HID:(half + 1) * HID]
                        sp.dma_start(tile[:, 0:MH - 1], b1[0:(MH - 1) * P].rearrange("(m p) -> p m", p=P), allow_slow_non_contiguous=True).then_inc(win["small"], 16)
                        sp.dma_start(tile[0:TAIL, MH - 1:MH], b1[(MH - 1) * P:HID].rearrange("(p m) -> p m", m=1), allow_slow_non_contiguous=True).then_inc(win["small"], 16)
                    sp.wait_ge(*ring.used(t0, ("w2", STREAMS - 1, NT // 2 - 1)))
                    w2 = A["L1_ffn_w2"][l]
                    sp.dma_start(W2[2][:, 0:MH - 1, :], w2[0:(MH - 1) * P].rearrange("(k p) n -> p k n", p=P)).then_inc(win["w2"], 16)
                    sp.dma_start(W2[2][0:TAIL, MH - 1, :], w2[(MH - 1) * P:HID]).then_inc(win["w2"], 16)
                    with sp.Fori(0, PAIRS) as p:
                        t = t0 + p
                        sp.wait_ge(*ring.ready(t, ("qkT", M8 - 1, 1)))
                        for s in two:
                            sp.dma_start(X3[s], x3b[p * STREAMS + s]).then_inc(x3_in[s].sem, 16)
                        for s in two:
                            hold(sp, K.sp_passed, *ring.moved(t, ("late", s)))
                            sp.wait_ge(*yb2.at(t, s + 1))
                            hold(sp, K.sp_passed, *stored[s].at(t, 0))
                            sp.dma_start(Y[s][:], yb[(t + 1) * STREAMS + s]).then_inc(y_in[s].sem, 16)

            @block.gpsimd
            def _(pool):
                for s in two:
                    nc.gpsimd.memset(V[s][:, :, :, LD:V1], 1.0).then_inc(vones, 1)
                    nc.gpsimd.memset(plain(HT[s][:, 1, 0:1]), 0.0).then_inc(vones, 1)
                    nc.gpsimd.memset(plain(OB[s][:, 0:1]), 0.0).then_inc(vones, 1)
                for x in (mask, shift, carry):
                    nc.gpsimd.memset(x[:], 0.0).then_inc(mset, 1)
                pool.wait_ge(mset, 3)
                nc.gpsimd.affine_select(out=mask[:, 0, :], in_=mask[:, 0, :], compare_op=ALU.is_ge, fill=FAR, base=0,
                                        pattern=[[1, P]], channel_multiplier=-1).then_inc(consts, 1)
                nc.gpsimd.affine_select(out=mask[:, 1, :], in_=mask[:, 1, :], compare_op=ALU.is_ge, fill=FAR, base=0,
                                        pattern=[[-1, P]], channel_multiplier=1).then_inc(consts, 1)
                nc.gpsimd.affine_select(out=shift[:], in_=shift[:], compare_op=ALU.not_equal, fill=1.0, base=1,
                                        pattern=[[-1, P]], channel_multiplier=1).then_inc(consts, 1)
                nc.gpsimd.affine_select(out=carry[:], in_=carry[:], compare_op=ALU.not_equal, fill=1.0, base=1 - P,
                                        pattern=[[P, P]], channel_multiplier=1).then_inc(consts, 1)
                with pool.Fori(0, LAYERS) as l:
                    pool.wait_ge(win["tables"], l * TABLES + TABLES)
                    half = LD // 2
                    tab = lambda x: x.unsqueeze(1).broadcast_to([P, NT, LD])
                    for c in range(2):
                        nc.gpsimd.tensor_tensor(At[:, :, c, :], At[:, :, c, :], tab(qks[:, c, :]), ALU.mult).then_inc(*tabs.up())
                        for a, b in ((0, half), (half, 0)):
                            ins = nc.gpsimd.tensor_tensor(Bt[:, :, c, a:a + half], Bt[:, :, c, a:a + half],
                                                          qks[:, c, b:b + half].unsqueeze(1).broadcast_to([P, NT, half]), ALU.mult)
                        ins.then_inc(*tabs.up())
                    tabs.close()
                    pool.wait_ge(win["small"], l * SMALL + SMALL)
                    hold(pool, K.pool_passed, win["w2"], l * 32 + 32)
                    parts = (slice(0, P), slice(0, MH - 1)), (slice(0, TAIL), slice(MH - 1, MH))
                    for rows2, m in parts:
                        nc.gpsimd.tensor_copy(W2[0][rows2, m, :], W2[2][rows2, m, :]).then_inc(*w2_split.up())
                    pool.wait_ge(*w2_split.now(l))
                    for rows2, m in parts:
                        nc.gpsimd.tensor_tensor(W2[1][rows2, m, :], W2[2][rows2, m, :], plain(W2[0][rows2, m, :]), ALU.subtract).then_inc(*w2_split.up())
                    w2_split.close()
                    with pool.Fori(0, PAIRS) as p:
                        t = l * PAIRS + p
                        for m in range(M8):
                            i = m % TB
                            pool.wait_ge(*ssum.at(t, m + 1))
                            nc.gpsimd.tensor_tensor(pw[i][:], ss[i][:], K.half[:, 0:2 * LH], ALU.pow).then_inc(*pstep.up())
                            hold(pool, K.pool_passed, *pstep.now(t))
                            nc.gpsimd.tensor_scalar(rn[i][:], pw[i][:], 1.0e12, None, ALU.min).then_inc(*rnorm.up())
                            pool.wait_ge(*ring.moved(t, ("k", m)))
                            nc.gpsimd.tensor_tensor(T1[i][:], T1[i][:], T2[i], ALU.add).then_inc(*roped.up())
                        for s in two:
                            pool.wait_ge(*ring.moved(t, ("wo", s, NT // 2 - 1)))
                            nc.gpsimd.tensor_tensor(O[s][:, :, D:2 * D], Y[s][:], b2[:].unsqueeze(1).broadcast_to([P, NT, D]), ALU.add).then_inc(*yb2.up())
                            hold(pool, K.pool_passed, *stat.at(t, (s + 1) * NT))
                            nc.gpsimd.tensor_scalar(vare[s][:], stats[s][:, :, 1], 1e-5, None, ALU.add).then_inc(*pstep.up())
                            pool.wait_ge(*pstep.now(t))
                            nc.gpsimd.tensor_tensor(rstd[s][:], vare[s][:], K.half[:, 0:NT], ALU.pow).then_inc(*rs.up())
                        for x in (pstep, rnorm, roped, yb2, rs):
                            x.close()

            @block.vector
            def _(v):
                def low_hT(t):
                    for s in two:
                        for k in range(KD):
                            name = ("hT", s, k)
                            v.wait_ge(*h_high.at(t, s * KD + k + 1))
                            high, low = hT(s, k)
                            nc.vector.tensor_tensor(low, ring.bank(name)[:], plain(high), ALU.subtract).then_inc(*ring.out(name))

                v.wait_ge(consts, 4)
                v.wait_ge(tgs, 1)
                credit(v, qk)
                start_ring(v, ring.emptied["V"], ring.rank[("hT", 0, 0)] - 1, lambda: low_hT(-1))
                wide = lambda x, shape: x.broadcast_to(shape)
                hf = LD // 2
                with v.Fori(0, LAYERS) as l:
                    for name, W in weights:
                        v.wait_ge(*w_high.at(l, w_split.n + 1))
                        nc.vector.tensor_tensor(W[1][:], W[2][:], plain(W[0][:]), ALU.subtract).then_inc(*w_split.up())
                    w_split.close()
                    hold(v, K.v_passed, *tabs.at(l, 4))
                    with v.Fori(0, PAIRS) as p:
                        t = l * PAIRS + p

                        def rotate(m):
                            i, s = TILE_UNITS[m]
                            b = m % TB
                            if m >= TB:
                                v.wait_ge(*ring.ready(t, ("qkT", m - TB, 1)))
                            else:
                                v.wait_ge(*stored[b].at(t, 0))
                            v.wait_ge(*sq.at(t, m + 1))
                            for c, name in enumerate(("q", "k")):
                                v.wait_ge(*ring.ready(t, (name, m)))
                                x = ring.bank((name, m))[:].rearrange("p (h d) -> p h d", h=LH)
                                heads = slice(c * LH, (c + 1) * LH)
                                nc.vector.tensor_tensor(T1[b][:, heads, :], x, wide(At[:, i, c, :].unsqueeze(1), [P, LH, LD]), ALU.mult)
                                nc.vector.tensor_tensor(T2[b][:, heads, 0:hf], x[:, :, hf:LD], wide(Bt[:, i, c, 0:hf].unsqueeze(1), [P, LH, hf]), ALU.mult)
                                nc.vector.tensor_tensor(T2[b][:, heads, hf:LD], x[:, :, 0:hf], wide(Bt[:, i, c, hf:LD].unsqueeze(1), [P, LH, hf]), ALU.mult)\
                                    .then_inc(*ring.out((name, m)))
                            nc.vector.tensor_reduce(ss[b][:], SQ[b], AX, ALU.add).then_inc(*ssum.up())

                        def scale(m):
                            b = m % TB
                            v.wait_ge(*roped.at(t, m + 1))
                            nc.vector.tensor_tensor(T1[b][:], T1[b][:], wide(rn[b][:].unsqueeze(2), [P, 2 * LH, LD]), ALU.mult).then_inc(*qk.up())

                        for m in range(M8 + 1):
                            if m < M8:
                                rotate(m)
                            if m >= 1:
                                scale(m - 1)

                        for k in range(U + VLAG):
                            if k < U:
                                for w in range(NT):
                                    name, c = ("sim", k, w // 2), w % 2
                                    if c == 0:
                                        hold(v, K.v_passed, *ring.ready(t, name))
                                    own = slice(1 if w == 0 else 0, 2)
                                    psum = ring.bank(name)[:, c * 2 * P:(c + 1) * 2 * P].rearrange("p (b j) -> p b j", b=2)
                                    ins = nc.vector.tensor_tensor_reduce(SM[k % RB][:, w, own, :], psum[:, own, :], mask[:, own, :], -1.0, 3.0e38,
                                                                         ALU.add, ALU.min, nmax[k % RB][:, w:w + 1])
                                    if c == 1:
                                        ins.then_inc(*ring.out(name))
                            if PLAG <= k < U + PLAG:
                                name = ("pT", k - PLAG, 1)
                                v.wait_ge(*ring.ready(t, name))
                                nc.vector.tensor_copy(PT[(k - PLAG) % TR][:, 2:4], ring.bank(name)[:].rearrange("p (w b j) -> p w b j", w=2, b=2)).then_inc(*ring.out(name))
                            if k >= VLAG:
                                u = k - VLAG
                                h, s = HEAD_UNITS[u]
                                v.wait_ge(*ring.ready(t, ("o", u)))
                                sums = ring.bank(("o", u))[:, 0:NT * V1].rearrange("p (w d) -> p w d", w=NT)
                                nc.vector.reciprocal(rden[u % RB][:], sums[:, :, LD]).then_inc(*rd.up())
                                v.wait_ge(*rd.now(t))
                                nc.vector.tensor_tensor(O[s][:, :, h * LD:(h + 1) * LD], sums[:, :, 0:LD], wide(rden[u % RB][:].unsqueeze(2), [P, NT, LD]), ALU.mult)\
                                    .then_inc(*ring.out(("o", u)))
                        for s in two:
                            for k in range(PAIRS_H):
                                name = ("oT", s, k)
                                v.wait_ge(*o_high.at(t, s * PAIRS_H + k + 1))
                                nc.vector.tensor_tensor(OTL[s][:, k, :], ring.bank(name)[:], plain(OT[s][:, k, :]), ALU.subtract).then_inc(*ring.out(name))
                        for s in two:
                            for g in range(NT // 2):
                                name = ("wo", s, g)
                                v.wait_ge(*ring.ready(t, name))
                                part = Y[s][:, 2 * g:2 * g + 2, :]
                                nc.vector.tensor_tensor(part, ring.bank(name)[:].rearrange("p (t d) -> p t d", t=2), part, ALU.add).then_inc(*ring.out(name))
                        for s in two:
                            later = ring.bank(("late", s))[:].rearrange("p (t d) -> p t d", t=NT)
                            v.wait_ge(*ring.ready(t, ("late", s)))
                            first = step.n
                            for i in range(NT):
                                nc.vector.bn_stats(halves[s][:, i, 0, :], Y[s][:, i, 0:P]).then_inc(*step.up())
                                nc.vector.bn_stats(halves[s][:, i, 1, :], later[:, i, :]).then_inc(*step.up())
                            hold(v, K.v_passed, *step.at(t, first + 2 * NT))
                            for i in range(NT):
                                nc.vector.bn_aggr(stats[s][:, i, :], halves[s][:, i].rearrange("p a b -> p (a b)")).then_inc(*stat.up())
                        for s in two:
                            later = ring.bank(("late", s))[:].rearrange("p (t d) -> p t d", t=NT)
                            v.wait_ge(*rs.at(t, s + 1))
                            for i in range(NT):
                                nc.vector.tensor_scalar(O[s][:, i, 0:P], Y[s][:, i, 0:P], stats[s][:, i, 0:1], rstd[s][:, i:i + 1], ALU.subtract, ALU.mult)
                                ins = nc.vector.tensor_scalar(O[s][:, i, P:D], later[:, i, :], stats[s][:, i, 0:1], rstd[s][:, i:i + 1], ALU.subtract, ALU.mult)
                            ins.then_inc(*ring.out(("late", s)))
                        for n in range(STREAMS * KD + 1):
                            if n < STREAMS * KD:
                                s, k = n // KD, n % KD
                                name = ("nT", s, k)
                                v.wait_ge(*ring.ready(t, name))
                                nc.vector.tensor_scalar(AFF(s, k), ring.bank(name)[:], lng[:, k:k + 1], lnb[:, k:k + 1], ALU.mult, ALU.add).then_inc(*ring.out(name))
                            if n:
                                s, k = (n - 1) // KD, (n - 1) % KD
                                high, low = hT(s, k)
                                v.wait_ge(*n_high.at(t, n))
                                nc.vector.tensor_tensor(low, AFF(s, k), plain(high), ALU.subtract).then_inc(*n_low.up())

                        def hidden_low(n):
                            s, m = n // MH, n % MH
                            r = P if m < MH - 1 else TAIL
                            v.wait_ge(*hid_high.at(t, n + 1))
                            nc.vector.tensor_tensor(hidden(s, m, True)[0:r, :], hidden(s, m)[0:r, :], plain(HH[s][0:r, m, :]), ALU.subtract).then_inc(*hid_low.up())

                        for n in range(STREAMS * MH):
                            s, m = n // MH, n % MH
                            r = P if m < MH - 1 else TAIL
                            v.wait_ge(*ring.ready(t, ("a", s, m)))
                            v.wait_ge(*ring.moved(t, ("g", s, m)))
                            nc.vector.scalar_tensor_tensor(out=hidden(s, m)[0:r, :], in0=ring.bank(("a", s, m))[0:r, :], scalar=ba[0:r, m:m + 1],
                                                           in1=GL[n % RB][0:r, :], op0=ALU.add, op1=ALU.mult).then_inc(*ring.out(("a", s, m)))
                            if n:
                                hidden_low(n - 1)
                        hidden_low(STREAMS * MH - 1)
                        low_hT(t)
                        for s in two:
                            v.wait_ge(*yb2.at(t, s + 1))
                            for g in range(NT // 2):
                                name, part = ("w2", s, g), slice(2 * g, 2 * g + 2)
                                v.wait_ge(*ring.ready(t, name))
                                nc.vector.tensor_tensor(Z[s][:, part, :], ring.bank(name)[:].rearrange("p (t d) -> p t d", t=2), O[s][:, part, D:2 * D], ALU.add)\
                                    .then_inc(*ring.out(name))
                            v.wait_ge(*x3_in[s].at(t, 16))
                            v.wait_ge(*ring.moved(t, ("w2", s, NT // 2 - 1)))
                            nc.vector.scalar_tensor_tensor(out=X3[s], in0=Z[s], scalar=tg[:, 0:1], in1=X3[s], op0=ALU.mult, op1=ALU.add).then_inc(*fin.up())
                        for x in (ssum, qk, rd, stat, step, fin, n_low, hid_low, ring.emptied["V"]):
                            x.close()

            @block.scalar
            def _(act):
                act.wait_ge(g_in, 16)
                nc.scalar.activation(tg[:], gb[:], ACT.Tanh).then_inc(tgs, 1)
                act.wait_ge(vones, 3 * STREAMS)
                credit(act, ring.emptied["S"], *stored)

                def high_hT(t):
                    for s in two:
                        for k in range(KD):
                            act.wait_ge(*ring.ready(t, ("hT", s, k)))
                            nc.scalar.activation(hT(s, k)[0], ring.bank(("hT", s, k))[:], ACT.Copy).then_inc(*h_high.up())
                    h_high.close()

                high_hT(-1)
                with act.Fori(0, LAYERS) as l:
                    for name, W in weights:
                        act.wait_ge(win[name], l * 16 + 16)
                        nc.scalar.activation(W[0][:], W[2][:], ACT.Copy).then_inc(*w_high.up())
                    w_high.close()
                    act.wait_ge(win["small"], l * SMALL + SMALL)
                    with act.Fori(0, PAIRS) as p:
                        t = l * PAIRS + p

                        for m in range(M8 + TLAG):
                            if m < M8:
                                i, s = TILE_UNITS[m]
                                if m >= TB:
                                    act.wait_ge(*ssum.at(t, m - TB + 1))
                                for c, name in enumerate(("q", "k")):
                                    act.wait_ge(*ring.ready(t, (name, m)))
                                    ins = nc.scalar.activation(SQ[m % TB][:, c * LH:(c + 1) * LH, :].rearrange("p h d -> p (h d)"), ring.bank((name, m))[:], ACT.Square)
                                ins.then_inc(*sq.up())
                                act.wait_ge(*ring.ready(t, ("v", m)))
                                nc.scalar.activation(V[s][:, i, :, 0:LD], ring.bank(("v", m))[:].rearrange("p (h d) -> p h d", h=LH), ACT.Copy).then_inc(*ring.out(("v", m)))
                            if m >= TLAG:
                                i, s = TILE_UNITS[m - TLAG]
                                for c in range(2):
                                    name = ("qkT", m - TLAG, c)
                                    act.wait_ge(*ring.ready(t, name))
                                    nc.scalar.activation(QKT[s][:, c * PAIRS_H:(c + 1) * PAIRS_H, i * P:(i + 1) * P],
                                                         ring.bank(name)[:].rearrange("p (h j) -> p h j", h=PAIRS_H), ACT.Copy).then_inc(*ring.out(name))
                        for k in range(U + PLAG):
                            if k < U:
                                for w in range(NT):
                                    if w % 2 == 0:
                                        act.wait_ge(*ring.moved(t, ("sim", k, w // 2)))
                                    own = slice(1 if w == 0 else 0, 2)
                                    x = SM[k % RB][:, w, own, :]
                                    ins = nc.scalar.activation(x, x, ACT.Exp, bias=nmax[k % RB][:, w:w + 1], scale=-1.0)
                                ins.then_inc(*probs.up())
                            if k >= PLAG:
                                name = ("pT", k - PLAG, 0)
                                act.wait_ge(*ring.ready(t, name))
                                part = ring.bank(name)[:, P:4 * P]
                                nc.scalar.activation(PT[(k - PLAG) % TR][:].rearrange("p w b j -> p (w b j)")[:, P:4 * P], part, ACT.Copy).then_inc(*ring.out(name))
                        for s in two:
                            for k in range(PAIRS_H):
                                act.wait_ge(*ring.ready(t, ("oT", s, k)))
                                nc.scalar.activation(OT[s][:, k, :], ring.bank(("oT", s, k))[:], ACT.Copy).then_inc(*o_high.up())
                        for s in two:
                            for k in range(KD):
                                act.wait_ge(*ring.moved(t, ("nT", s, k)))
                                nc.scalar.activation(hT(s, k)[0], AFF(s, k), ACT.Copy).then_inc(*n_high.up())

                        def hidden_high(n):
                            s, m = n // MH, n % MH
                            r = P if m < MH - 1 else TAIL
                            act.wait_ge(*ring.moved(t, ("a", s, m)))
                            nc.scalar.activation(HH[s][0:r, m, :], hidden(s, m)[0:r, :], ACT.Copy).then_inc(*hid_high.up())

                        for n in range(STREAMS * MH):
                            s, m = n // MH, n % MH
                            r = P if m < MH - 1 else TAIL
                            act.wait_ge(*ring.ready(t, ("g", s, m)))
                            if n >= RB:
                                act.wait_ge(*ring.moved(t, ("a", (n - RB) // MH, (n - RB) % MH)))
                            nc.scalar.activation(GL[n % RB][0:r, :], ring.bank(("g", s, m))[0:r, :], ACT.Gelu, bias=bg[0:r, m:m + 1])\
                                .then_inc(*ring.out(("g", s, m)))
                            if n:
                                hidden_high(n - 1)
                        hidden_high(STREAMS * MH - 1)
                        high_hT(t)
                        for s in two:
                            act.wait_ge(*ring.moved(t, ("w2", s, NT // 2 - 1)))
                            act.dma_start(yb[(t + PAIRS) * STREAMS + s], Z[s]).then_inc(stored[s].sem, 16)
                            act.wait_ge(*fin.at(t, s + 1))
                            act.dma_start(ob[p * STREAMS + s], X3[s]).then_inc(stored[s].sem, 16)
                        for x in (sq, probs, o_high, n_high, hid_high, ring.emptied["S"]):
                            x.close()
                for s in two:
                    act.wait_ge(*stored[s].at(LAYERS * PAIRS, 0))

            @block.tensor
            def _(pe):
                pe.wait_ge(consts, 4)
                pe.wait_ge(vones, 3 * STREAMS)

                def turn_y(t, fresh):
                    for s in two:
                        pe.wait_ge(*y_in[s].at(t + 1, 16))
                        for k in range(KD):
                            bank = ring.bank(("hT", s, k)) if fresh else ring.take(pe, t, ("hT", s, k))
                            for i in range(NT):
                                mm = nc.tensor.transpose(bank[:, i * P:(i + 1) * P], Y[s][:, i, k * P:(k + 1) * P], K.ident[:])
                            mm.then_inc(*ring.full.up())

                start_ring(pe, ring.full, hT_first, lambda: turn_y(-1, True))
                with pe.Fori(0, LAYERS) as l:
                    hold(pe, K.pe_passed, *w_split.at(l, 1))
                    with pe.Fori(0, PAIRS) as p:
                        t = l * PAIRS + p
                        full = lambda: ring.full.up()
                        for m in range(M8 + TLAG):
                            if m < M8:
                                i, s = TILE_UNITS[m]
                                if i == 0:
                                    pe.wait_ge(*ring.moved_before(t, ("hT", s, KD - 1)))
                                for c, name in enumerate("qkv"):
                                    bank = ring.take(pe, t, (name, m))
                                    for k in range(KD):
                                        mm = split_matmul(nc, bank[:], late(s, k, i), [x[:, k, c * INNER:(c + 1) * INNER] for x in Wqkv[0:2]],
                                                          start=(k == 0), stop=(k == KD - 1))
                                    mm.then_inc(*full())
                            if m >= TLAG:
                                u = m - TLAG
                                pe.wait_ge(*qk.at(t, u + 1))
                                for c in range(2):
                                    bank = ring.take(pe, t, ("qkT", u, c))
                                    src = T1[u % TB][:, c * LH:(c + 1) * LH, :].rearrange("p h d -> p (h d)")
                                    for g in range(PAIRS_H):
                                        mm = nc.tensor.transpose(bank[:, g * P:(g + 1) * P], src[:, g * P:(g + 1) * P], K.ident[:])
                                    mm.then_inc(*full())
                        for k in range(U + VLAG):
                            if k < U:
                                h, s = HEAD_UNITS[k]
                                if h == 0:
                                    pe.wait_ge(*ring.moved(t, ("qkT", M8 - STREAMS + s, 1)))
                                part, g = slice(h % 2 * LD, h % 2 * LD + LD), h // 2
                                for w in range(NT):
                                    if w % 2 == 0:
                                        bank = ring.take(pe, t, ("sim", k, w // 2))
                                    a = 1 if w == 0 else 0
                                    mm = nc.tensor.matmul(bank[:, (w % 2 * 2 + a) * P:(w % 2 * 2 + 2) * P], QKT[s][part, g, w * P:(w + 1) * P],
                                                          QKT[s][part, PAIRS_H + g, (w - 1 + a) * P:(w + 1) * P], start=True, stop=True)
                                    if w % 2:
                                        mm.then_inc(*full())
                            if PLAG <= k < U + PLAG:
                                u = k - PLAG
                                pe.wait_ge(*probs.at(t, u + 1))
                                for w in range(NT):
                                    if w % 2 == 0:
                                        bank = ring.take(pe, t, ("pT", u, w // 2))
                                    for a in range(1 if w == 0 else 0, 2):
                                        c = w % 2 * 2 + a
                                        mm = turned(nc, bank[:, c * P:(c + 1) * P], SM[u % RB][:, w, a, :], K.ident[:])
                                    if w % 2:
                                        mm.then_inc(*full())
                            if k >= VLAG:
                                u = k - VLAG
                                h, s = HEAD_UNITS[u]
                                pe.wait_ge(*ring.moved(t, ("pT", u, 0)))
                                pe.wait_ge(*ring.moved(t, ("pT", u, 1)))
                                bank = ring.take(pe, t, ("o", u))
                                for w in range(NT):
                                    for a in range(1 if w == 0 else 0, 2):
                                        mm = nc.tensor.matmul(bank[:, w * V1:(w + 1) * V1], PT[u % TR][:, w, a, :], V[s][:, w - 1 + a, h, :],
                                                              start=(a == 0 or w == 0), stop=(a == 1))
                                mm.then_inc(*full())
                        for s in two:
                            pe.wait_ge(*ring.moved(t, ("o", U - STREAMS + s)))
                            for k in range(PAIRS_H):
                                bank = ring.take(pe, t, ("oT", s, k))
                                for i in range(NT):
                                    mm = nc.tensor.transpose(bank[:, i * P:(i + 1) * P], O[s][:, i, k * P:(k + 1) * P], K.ident[:])
                                mm.then_inc(*full())
                        pe.wait_ge(*w_split.at(l, 2))
                        for s in two:
                            pe.wait_ge(*ring.moved(t, ("oT", s, PAIRS_H - 1)))
                            for g in range(NT // 2):
                                bank = ring.take(pe, t, ("wo", s, g))
                                for i in (2 * g, 2 * g + 1):
                                    for k in range(PAIRS_H):
                                        mm = split_matmul(nc, bank[:, i % 2 * D:(i % 2 + 1) * D], [x[s][:, k, i * P:(i + 1) * P] for x in (OT, OTL)],
                                                          [x[:, k, :] for x in Wo[0:2]], start=(k == 0), stop=(k == PAIRS_H - 1))
                                mm.then_inc(*full())
                        for s in two:
                            pe.wait_ge(*ring.moved(t, ("wo", s, NT // 2 - 1)))
                            bank = ring.take(pe, t, ("late", s))
                            for i in range(NT):
                                mm = nc.tensor.matmul(bank[:, i * P:(i + 1) * P], shift[:], Y[s][:, i, P:D], start=True, stop=(i == 0))
                                if i:
                                    mm = nc.tensor.matmul(bank[:, i * P:(i + 1) * P], carry[:], Y[s][:, i - 1, P:D], start=False, stop=True)
                            mm.then_inc(*full())
                        for s in two:
                            pe.wait_ge(*ring.moved(t, ("late", s)))
                            for k in range(KD):
                                bank = ring.take(pe, t, ("nT", s, k))
                                for i in range(NT):
                                    mm = turned(nc, bank[:, i * P:(i + 1) * P], O[s][:, i, k * P:(k + 1) * P], K.ident[:])
                                mm.then_inc(*full())
                        pe.wait_ge(*w_split.at(l, 3))
                        for s in two:
                            pe.wait_ge(*n_low.at(t, (s + 1) * KD))
                            for m in range(MH):
                                r = P if m < MH - 1 else TAIL
                                for name, at in (("g", HID), ("a", 0)):
                                    bank = ring.take(pe, t, (name, s, m))
                                    for k in range(KD):
                                        mm = split_matmul(nc, bank[0:r, :], [x[:, k, at + m * P:at + m * P + r] for x in W1[0:2]], hT(s, k),
                                                          start=(k == 0), stop=(k == KD - 1))
                                    mm.then_inc(*full())
                        turn_y(t, False)
                        pe.wait_ge(*w2_split.at(l, 4))
                        for s in two:
                            pe.wait_ge(*hid_low.at(t, (s + 1) * MH))
                            for g in range(NT // 2):
                                bank = ring.take(pe, t, ("w2", s, g))
                                for i in (2 * g, 2 * g + 1):
                                    for m in range(MH):
                                        r = P if m < MH - 1 else TAIL
                                        mm = split_matmul(nc, bank[:, i % 2 * D:(i % 2 + 1) * D],
                                                          (HH[s][0:r, m, i * P:(i + 1) * P], hidden(s, m, True)[0:r, i * P:(i + 1) * P]),
                                                          [x[0:r, m, :] for x in W2[0:2]], start=(m == 0), stop=(m == MH - 1))
                                mm.then_inc(*full())
                        ring.close_pe()


def program(nc, A):

    class K:
        keep = Store(nc, "keep")

    def scratch(name, shape, dt=FP):
        return nc.dram_tensor(name, shape, dt, kind="Internal").ap()

    K.xnT_d, K.ctxT_d = scratch("xnT", (B, P, KD, S)), scratch("ctxT", (B, P, KD, S))
    K.m_d = scratch("running_max", (B * H, S))
    K.x2_d, K.x3_d = scratch("x2", (N + CAP, D)), scratch("x3", (N, D))
    K.y_d = scratch("y", ((LAYERS + 1) * N, D))
    K.xg_d, K.slots_d = scratch("expert_rows", (N + CAP, ROW)), scratch("slots", (E_, CAP), I32)
    with K.keep.stack:
        setup(nc, A, K)
        first = Store(nc, "first")
        with nc.cleanup_on_exit(), first.stack:
            K.gates = first.sb("gates", [2, NT, B, H])
            K.acol, K.nlcol = first.sb("a_columns", [NT, B, H]), first.sb("exp_columns", [NT, B, H])
            normalize_phase(nc, A, K)
            scan_phase(nc, A, K)
            mlstm_phase(nc, A, K)
        second = Store(nc, "second")
        with second.stack:
            K.R = second.sb("priorities", [E_, B, NT])
            K.idx = second.sb("slot_tokens", [E_, SLOTS], I32)
            router_phase(nc, A, K)
            routing_phase(nc, A, K)
            expert_phase(nc, A, K)
        retrieval_phase(nc, A, K)
        layer_phase(nc, A, K)


_INS = ["x", "ctx_1024", "g_xattn", "g_ffn", "L0_xattn_ig_kernel", "L0_xattn_ig_bias", "L0_xattn_fg_kernel",
        "L0_xattn_fg_bias", "L0_xattn_outnorm_weight", "L1_ffn_wqkv", "L1_ffn_q_scale", "L1_ffn_k_scale",
        "L1_ffn_wo", "L1_ffn_ln_g", "L1_ffn_ln_b", "L1_ffn_w1", "L1_ffn_b1", "L1_ffn_w2", "L1_ffn_b2"]


def position_tables():
    f = np.float32
    half = np.arange(0, LD, 2).astype(f)
    inv_freq = f(1) / f(10000.0) ** (half / f(LD))
    pos = np.arange(S).astype(f)
    freqs = pos[:, None] * inv_freq[None]
    freqs = np.concatenate([freqs, freqs], -1)
    base = (half + f(0.4 * LD)) / f(1.4 * LD)
    scale = base[None] ** ((pos - f(S // 2)) / f(64))[:, None]
    scale = np.concatenate([scale, scale], -1)
    sign = np.where(np.arange(LD) < LD // 2, -1, 1).astype(f)
    c, s = np.cos(freqs), np.sin(freqs) * sign
    return np.stack([c * scale * f(8), c / scale], 1).astype(f), np.stack([s * scale * f(8), s / scale], 1).astype(f)


def kernel(**inputs):
    import numpy as _np
    import concourse.bacc as _bacc
    from concourse.bass_utils import run_bass_kernel_spmd as _run

    nc = _bacc.Bacc("TRN2", target_bir_lowering=False, num_devices=1)
    arrays = {name: _np.ascontiguousarray(inputs[name]) for name in _INS}
    arrays["gate_wT"] = _np.ascontiguousarray(inputs["L0_ffn_gate_w"].T)
    arrays["w1T"] = _np.ascontiguousarray(inputs["L0_ffn_w1"].transpose(0, 2, 1))
    arrays["w2T"] = _np.ascontiguousarray(inputs["L0_ffn_w2"].transpose(0, 2, 1))
    arrays["cos"], arrays["sin"] = position_tables()
    A = {n: nc.dram_tensor(n, a.shape, mybir.dt.from_np(a.dtype), kind="ExternalInput").ap() for n, a in arrays.items()}
    A["out"] = nc.dram_tensor("out", (B, S, D), FP, kind="ExternalOutput").ap()
    program(nc, A)
    return _run(nc, [arrays], core_ids=[0]).results[0]["out"]
```

```python
import concourse.bass as bass
from concourse import mybir
from contextlib import ExitStack
import numpy as np

FP = mybir.dt.float32
I32 = mybir.dt.int32
R32 = mybir.dt.float32r
ALU = mybir.AluOpType
ACT = mybir.ActivationFunctionType
AX = mybir.AxisListType.X

P = 128
B, S, D = 8, 512, 256
NT = S // P
KD = D // P
N = B * S
STREAMS = 2
PAIRS = B // STREAMS


class Sig:

    def __init__(self, sem, per, credit=0):
        self.sem, self.per, self.credit, self.n = sem, per, credit, 0

    def up(self, by=1):
        self.n += by
        return self.sem, by

    def at(self, turn, k):
        return self.sem, turn * self.per + (self.credit + k)

    def prev(self, turn, k):
        assert self.credit >= self.per and k > 0
        return self.sem, turn * self.per + (self.credit - self.per + k)

    def now(self, turn):
        return self.at(turn, self.n)

    def close(self):
        assert self.n == self.per, (self.sem.name, self.n, self.per)
        self.n = 0


class Ring:

    def __init__(self, banks, groups, full, emptied):
        self.banks, self.names = banks, [g for g, _ in groups]
        self.who = dict(groups)
        assert len(self.who) == len(groups)
        self.index = {g: i for i, g in enumerate(self.names)}
        count = {"V": 0, "S": 0}
        self.rank = {}
        for g, w in groups:
            count[w] += 1
            self.rank[g] = count[w]
        self.full = Sig(full, len(groups), len(groups))
        self.emptied = {w: Sig(emptied[w], count[w], count[w]) for w in "VS"}
        self.taken = 0

    def bank(self, name):
        return self.banks[self.index[name] % 8]

    def take(self, pe, turn, name):
        i = self.index[name]
        assert i == self.taken, (name, self.names[self.taken])
        self.taken += 1
        if i >= 8:
            last, back = self.names[i - 8], 0
        else:
            last, back = self.names[max(j for j in range(len(self.names)) if j % 8 == i)], 1
        sig = self.emptied[self.who[last]]
        pe.wait_ge(sig.sem, turn * sig.per + (sig.credit - back * sig.per + self.rank[last]))
        return self.bank(name)

    def ready(self, turn, name):
        return self.full.at(turn, self.index[name] + 1)

    def used(self, turn, name):
        return self.full.prev(turn, self.index[name] + 1)

    def out(self, name):
        sig = self.emptied[self.who[name]]
        assert sig.n == self.rank[name] - 1, name
        return sig.up()

    def moved(self, turn, name):
        return self.emptied[self.who[name]].at(turn, self.rank[name])

    def moved_before(self, turn, name):
        return self.emptied[self.who[name]].prev(turn, self.rank[name])

    def close_pe(self):
        assert self.taken == len(self.names)
        self.taken = 0
        self.full.close()


def plain(ap):
    return ap.bitcast(FP)


def split_matmul(nc, out, weights, data, start, stop):
    (wh, wl), (dh, dl) = weights, data
    nc.tensor.matmul(out, wh, dh, start=start, stop=False)
    nc.tensor.matmul(out, wh, dl, start=False, stop=False)
    return nc.tensor.matmul(out, wl, dh, start=False, stop=stop)


def turned(nc, out, data, ident):
    return nc.tensor.matmul(out, data, ident, start=True, stop=True)


def hold(engine, passed, sem, value):
    engine.wait_ge(sem, value)
    engine.sem_inc(passed, 1)


def credit(engine, *sigs):
    for sig in sigs:
        engine.sem_inc(sig.sem, sig.credit)
H = 4
DH = D // H


class Store:

    def __init__(self, nc, phase):
        self.nc, self.phase, self.stack, self.place = nc, phase, ExitStack(), {}

    def sb(self, name, shape, dt=FP):
        self.place[name] = -(-self.nc.sbuf_base // 32) * 32
        return self.stack.enter_context(self.nc.sbuf_tensor(f"{self.phase}_{name}", [P] + shape, dt))

    def rounded(self, name, shape):
        return self.nc.alloc_sbuf_tensor_at(f"{self.phase}_{name}_r", [P] + shape, R32, offset=self.place[name])

    def rows(self, name, shape, dt=FP):
        return self.stack.enter_context(self.nc.sbuf_tensor(f"{self.phase}_{name}", shape, dt))

    def banks(self):
        return [self.stack.enter_context(self.nc.psum_tensor(f"{self.phase}_bank{i}", [P, 512], FP)) for i in range(8)]

    def sem(self, name):
        return self.nc.alloc_semaphore(f"{self.phase}_{name}")


def tiles(ap):
    return ap.rearrange("(t p) d -> p t d", p=P)


def setup(nc, A, K):
    sem_zero, sem_ready = nc.alloc_semaphore("const_zero"), nc.alloc_semaphore("const_ready")
    K.ident = K.keep.sb("ident", [P])
    K.half = K.keep.sb("minus_half", [64])
    K.one = K.keep.sb("one", [1])
    K.v_passed, K.pool_passed, K.pe_passed, K.sp_passed = (nc.alloc_semaphore(f"{n}_waits") for n in ("vector", "pool", "tensor", "sync"))
    with nc.Block() as block:
        @block.gpsimd
        def _(pool):
            nc.gpsimd.memset(K.ident[:], 0.0).then_inc(sem_zero, 1)
            nc.gpsimd.memset(K.half[:], -0.5).then_inc(sem_ready, 1)
            nc.gpsimd.memset(K.one[:], 1.0).then_inc(sem_ready, 1)
            pool.wait_ge(sem_zero, 1)
            nc.gpsimd.affine_select(out=K.ident[:], in_=K.ident[:], compare_op=ALU.not_equal, fill=1.0,
                                    base=0, pattern=[[-1, P]], channel_multiplier=1).then_inc(sem_ready, 1)
            pool.wait_ge(sem_ready, 3)


def normalize_phase(nc, A, K):
    R = Store(nc, "nrm")
    FOUR, TURNS = 4, B // 4
    with R.stack:
        X = [R.sb(f"x{s}", [NT, D]) for s in range(FOUR)]
        C = [R.sb(f"ctx{s}", [NT, D]) for s in range(FOUR)]
        XN = [R.sb(f"xn{s}", [NT, D]) for s in range(FOUR)]
        XT = [R.sb(f"xT{s}", [KD, S]) for s in range(FOUR)]
        CT = [R.sb(f"cT{s}", [KD, S]) for s in range(FOUR)]
        halves = [R.sb(f"halves{s}", [NT, 6]) for s in range(FOUR)]
        stats = [R.sb(f"stats{s}", [NT, 2]) for s in range(FOUR)]
        vare = [R.sb(f"vare{s}", [NT]) for s in range(FOUR)]
        rstd = [R.sb(f"rstd{s}", [NT]) for s in range(FOUR)]
        kern = R.sb("kern", [3 * KD, 2, H])
        Wg = R.sb("Wg", [2 * KD, 2, H])
        bias = R.sb("bias", [2, H])
        groups = []
        for s in range(FOUR):
            groups += [(("cT", s, k), "S") for k in range(KD)]
        for s in range(FOUR):
            groups += [(("xT", s, k), "S") for k in range(KD)]
        for s in range(FOUR):
            groups += [(("gate", s), "V")]
        ring = Ring(R.banks(), groups, R.sem("bank_full"), {"V": R.sem("emptied_V"), "S": R.sem("emptied_S")})
        w_in = R.sem("weights_in")
        x_in = [Sig(R.sem(f"x_in{s}"), 16) for s in range(FOUR)]
        c_in = [Sig(R.sem(f"ctx_in{s}"), 16) for s in range(FOUR)]
        stored = [Sig(R.sem(f"stored{s}"), 32, 32) for s in range(FOUR)]
        step = Sig(R.sem("vector_step"), FOUR * NT)
        stat = Sig(R.sem("stats_ready"), FOUR * NT)
        normed = Sig(R.sem("x_normed"), FOUR * NT, FOUR * NT)
        pstep = Sig(R.sem("pool_step"), FOUR)
        rs = Sig(R.sem("rstd_ready"), FOUR)
        wg = R.sem("gate_weights")
        xb = A["x"].rearrange("b (t p) d -> b p t d", p=P)
        cb = A["ctx_1024"].rearrange("b (t p) d -> b p t d", p=P)
        with nc.Block() as block:
            @block.sync
            def _(sp):
                for i, name in enumerate(("ig", "fg")):
                    sp.dma_start(kern[:, :, i, :], A[f"L0_xattn_{name}_kernel"].rearrange("(k p) h -> p k h", p=P)).then_inc(w_in, 16)
                    sp.dma_start(bias[:, i, :], A[f"L0_xattn_{name}_bias"].partition_broadcast(P)).then_inc(w_in, 16)
                with sp.Fori(0, TURNS) as t:
                    for s in range(FOUR):
                        sp.wait_ge(*ring.used(t, ("cT", s, KD - 1)))
                        sp.dma_start(C[s][:], cb[t * FOUR + s]).then_inc(c_in[s].sem, 16)
                        sp.wait_ge(*normed.prev(t, NT * (s + 1)))
                        sp.dma_start(X[s][:], xb[t * FOUR + s]).then_inc(x_in[s].sem, 16)

            @block.vector
            def _(v):
                credit(v, normed, ring.emptied["V"])
                v.wait_ge(w_in, 64)
                nc.vector.tensor_copy(Wg[:, 0:KD], kern[:, 0:KD]).then_inc(wg, 1)
                nc.vector.tensor_tensor(Wg[:, KD:2 * KD], kern[:, KD:2 * KD], kern[:, 2 * KD:3 * KD], ALU.add).then_inc(wg, 1)
                with v.Fori(0, TURNS) as t:
                    for s in range(FOUR):
                        v.wait_ge(*x_in[s].at(t, 16))
                        for i in range(NT):
                            nc.vector.bn_stats(halves[s][:, i, :], X[s][:, i, :]).then_inc(*step.up())
                        hold(v, K.v_passed, *step.at(t, (s + 1) * NT))
                        for i in range(NT):
                            nc.vector.bn_aggr(stats[s][:, i, :], halves[s][:, i, :]).then_inc(*stat.up())
                    for s in range(FOUR):
                        v.wait_ge(*rs.at(t, s + 1))
                        for i in range(NT):
                            nc.vector.tensor_scalar(XN[s][:, i, :], X[s][:, i, :], stats[s][:, i, 0:1], rstd[s][:, i:i + 1],
                                                    ALU.subtract, ALU.mult).then_inc(*normed.up())
                    for s in range(FOUR):
                        v.wait_ge(*ring.ready(t, ("gate", s)))
                        psum = ring.bank(("gate", s))[:, 0:NT * 2 * H].rearrange("p (t g h) -> p g t h", t=NT, g=2)
                        nc.vector.tensor_tensor(K.gates[:, :, :, t * FOUR + s, :], psum,
                                                bias[:].unsqueeze(2).broadcast_to([P, 2, NT, H]), ALU.add).then_inc(*ring.out(("gate", s)))
                    step.close(), stat.close(), normed.close(), ring.emptied["V"].close()

            @block.gpsimd
            def _(pool):
                with pool.Fori(0, TURNS) as t:
                    for s in range(FOUR):
                        hold(pool, K.pool_passed, *stat.at(t, (s + 1) * NT))
                        nc.gpsimd.tensor_scalar(vare[s][:], stats[s][:, :, 1], 1e-5, None, ALU.add).then_inc(*pstep.up())
                        pool.wait_ge(*pstep.now(t))
                        nc.gpsimd.tensor_tensor(rstd[s][:], vare[s][:], K.half[:, 0:NT], ALU.pow).then_inc(*rs.up())
                    pstep.close(), rs.close()

            @block.scalar
            def _(act):
                credit(act, ring.emptied["S"], *stored)
                with act.Fori(0, TURNS) as t:
                    for name, T, scratch in (("cT", CT, K.ctxT_d), ("xT", XT, K.xnT_d)):
                        for s in range(FOUR):
                            act.wait_ge(*stored[s].at(t, 0))
                            for k in range(KD):
                                act.wait_ge(*ring.ready(t, (name, s, k)))
                                nc.scalar.activation(T[s][:, k, :], ring.bank((name, s, k))[:], ACT.Copy).then_inc(*ring.out((name, s, k)))
                    for name, T, scratch in (("cT", CT, K.ctxT_d), ("xT", XT, K.xnT_d)):
                        for s in range(FOUR):
                            act.wait_ge(*ring.moved(t, (name, s, KD - 1)))
                            act.dma_start(scratch[t * FOUR + s], T[s][:]).then_inc(stored[s].sem, 16)
                    ring.emptied["S"].close()
                for s in range(FOUR):
                    act.wait_ge(*stored[s].at(TURNS, 0))

            @block.tensor
            def _(pe):
                pe.wait_ge(wg, 2)
                credit(pe, ring.full)
                with pe.Fori(0, TURNS) as t:
                    for name, src, sig in (("cT", C, c_in), ("xT", XN, None)):
                        for s in range(FOUR):
                            if sig:
                                pe.wait_ge(*sig[s].at(t, 16))
                            else:
                                pe.wait_ge(*normed.at(t, NT * (s + 1)))
                            for k in range(KD):
                                bank = ring.take(pe, t, (name, s, k))
                                for i in range(NT):
                                    mm = nc.tensor.transpose(bank[:, i * P:(i + 1) * P], src[s][:, i, k * P:(k + 1) * P], K.ident[:])
                                mm.then_inc(*ring.full.up())
                    for s in range(FOUR):
                        pe.wait_ge(*ring.moved(t, ("xT", s, KD - 1)))
                        bank = ring.take(pe, t, ("gate", s))
                        for i in range(NT):
                            for k in range(2 * KD):
                                T = (XT if k < KD else CT)[s]
                                mm = nc.tensor.matmul(bank[:, i * 2 * H:(i + 1) * 2 * H], T[:, k % KD, i * P:(i + 1) * P],
                                                      Wg[:, k].rearrange("p g h -> p (g h)"), start=(k == 0), stop=(k == 2 * KD - 1))
                        mm.then_inc(*ring.full.up())
                    ring.close_pe()


def scan_phase(nc, A, K):
    R = Store(nc, "scan")
    BH = B * H
    with R.stack:
        row = lambda name: R.rows(name, [BH, S])
        f, nf, nabs, e, l, minf, lf, F, a, m, Fm, nl, ones = map(row, "f nf nabs e l minf lf F a m Fm nl ones".split())
        banks = R.banks()
        turned, step, sstep = R.sem("gates_turned"), Sig(R.sem("vector_step"), 0), Sig(R.sem("scalar_step"), 0)
        rows_ready, back, kept = R.sem("rows_ready"), R.sem("columns_turned"), R.sem("m_stored")
        with nc.Block() as block:
            @block.tensor
            def _(pe):
                for kind in range(2):
                    for i in range(NT):
                        mm = nc.tensor.transpose(banks[kind][0:BH, i * P:(i + 1) * P],
                                                 K.gates[:, kind, i].rearrange("p b h -> p (b h)"), K.ident[:])
                    mm.then_inc(turned, 1)
                pe.wait_ge(rows_ready, 1)
                for i in range(NT):
                    mm = nc.tensor.transpose(banks[2][:, i * BH:(i + 1) * BH], a[:, i * P:(i + 1) * P], K.ident[0:BH, 0:BH])
                mm.then_inc(back, 1)
                pe.wait_ge(rows_ready, 2)
                for i in range(NT):
                    mm = nc.tensor.transpose(banks[3][:, i * BH:(i + 1) * BH], nl[:, i * P:(i + 1) * P], K.ident[0:BH, 0:BH])
                mm.then_inc(back, 1)

            @block.vector
            def _(v):
                def then(ins):
                    ins.then_inc(*step.up())
                    v.wait_ge(*step.now(0))
                then(nc.vector.memset(ones[:], 1.0))
                v.wait_ge(turned, 2)
                then(nc.vector.tensor_copy(f[:], banks[1][0:BH, :]))
                then(nc.vector.tensor_scalar(nf[:], f[:], -1.0, None, ALU.mult))
                then(nc.vector.tensor_tensor(nabs[:], f[:], nf[:], ALU.min))
                then(nc.vector.tensor_scalar(minf[:], f[:], 0.0, None, ALU.min))
                v.wait_ge(*sstep.at(0, 2))
                then(nc.vector.tensor_tensor(lf[:], minf[:], l[:], ALU.subtract))
                then(nc.vector.tensor_tensor_scan(F[:], ones[:], lf[:], 0.0, ALU.mult, ALU.add))
                then(nc.vector.tensor_tensor(a[:], banks[0][0:BH, :], F[:], ALU.subtract))
                then(nc.vector.tensor_tensor_scan(m[:], a[:], a[:], -3.0e38, ALU.max, ALU.max))
                nc.vector.tensor_tensor(Fm[:], F[:], m[:], ALU.add).then_inc(rows_ready, 1)
                v.wait_ge(back, 1)
                nc.vector.tensor_copy(K.acol[:].rearrange("p t b h -> p (t b h)"), banks[2][:, 0:NT * BH]).then_inc(*step.up())
                v.wait_ge(back, 2)
                nc.vector.tensor_copy(K.nlcol[:].rearrange("p t b h -> p (t b h)"), banks[3][:, 0:NT * BH]).then_inc(*step.up())

            @block.scalar
            def _(act):
                act.wait_ge(*step.at(0, 4))
                nc.scalar.activation(e[:], nabs[:], ACT.Exp).then_inc(*sstep.up())
                act.wait_ge(*sstep.now(0))
                nc.scalar.activation(l[:], e[:], ACT.Ln, bias=K.one[0:BH, :]).then_inc(*sstep.up())
                act.wait_ge(rows_ready, 1)
                nc.scalar.activation(nl[:], Fm[:], ACT.Exp, scale=-1.0).then_inc(rows_ready, 1)

            @block.sync
            def _(sp):
                sp.wait_ge(rows_ready, 1)
                sp.dma_start(K.m_d[:, :], m[:]).then_inc(kept, 16)
                sp.wait_ge(kept, 16)


def mlstm_phase(nc, A, K):
    R = Store(nc, "mlstm")
    UNITS = [(h, s) for h in range(H) for s in range(STREAMS)]
    U, RB, LAG = len(UNITS), 4, 2
    HLAG, NLAG = LAG + 1, LAG + 2
    W = DH + 1
    with R.stack:
        X = [R.sb(f"x{s}", [NT, D]) for s in range(STREAMS)]
        XT = [R.sb(f"xT{s}", [KD, 2, S]) for s in range(STREAMS)]
        CT = [R.sb(f"cT{s}", [KD, S]) for s in range(STREAMS)]
        VE = [R.sb(f"v{s}", [NT, H, W]) for s in range(STREAMS)]
        MB = [R.sb(f"m{s}", [H, S]) for s in range(STREAMS)]
        DT = [R.sb(f"decay{i}", [NT, S]) for i in range(RB)]
        CM = [R.sb(f"weights{i}", [NT, S]) for i in range(RB)]
        hh = [R.sb(f"hh{i}", [NT, DH]) for i in range(RB)]
        halves = [R.sb(f"halves{i}", [NT, 6]) for i in range(RB)]
        stats = [R.sb(f"stats{i}", [NT, 2]) for i in range(RB)]
        den, rden, vare, rstd = ([R.sb(f"{n}{i}", [NT]) for i in range(RB)] for n in "den rden vare rstd".split())
        gb, tg, wb, wt = R.sb("g", [2]), R.sb("tanh_g", [2]), R.sb("w", [D]), R.sb("w_tanh", [D])
        groups = []
        for k in range(U + LAG):
            if k < U:
                groups += [(("qk", k, j), "V") for j in range(3)]
            if k >= LAG:
                groups += [(("pv", k - LAG), "S")]
        ring = Ring(R.banks(), groups, R.sem("bank_full"), {"V": R.sem("scores_emptied"), "S": R.sem("sums_emptied")})
        par_in = R.sem("params_in")
        names = ("xT", "cT", "v", "m", "x")
        loaded = {n: [Sig(R.sem(f"{n}_in{s}"), {"v": 16 * NT, "xT": 32}.get(n, 16)) for s in range(STREAMS)] for n in names}
        stored = [Sig(R.sem(f"stored{s}"), 16, 16) for s in range(STREAMS)]
        ones = R.sem("ones_set")
        tgs, wts = R.sem("tanh_ready"), R.sem("w_ready")
        decay = Sig(R.sem("decay_ready"), U, U)
        masked = Sig(R.sem("decay_masked"), U)
        step = Sig(R.sem("vector_step"), U * (5 + NT + 2))
        stat = Sig(R.sem("stats_ready"), U * NT)
        pstep = Sig(R.sem("pool_step"), U)
        rs = Sig(R.sem("rstd_ready"), U)
        x1 = Sig(R.sem("x1_ready"), U)
        xb = A["x"].rearrange("b (t p) d -> b p t d", p=P)
        vb = A["ctx_1024"].rearrange("b (t p) (h d) -> b t p h d", p=P, h=H)
        mb = K.m_d[:, :].rearrange("(b h) s -> b (h s)", h=H)
        ob = K.x2_d[0:N, :].rearrange("(b t p) d -> b p t d", p=P, t=NT)
        with nc.Block() as block:
            @block.sync
            def _(sp):
                sp.dma_start(gb[:, 0:1], A["g_xattn"][0:1].partition_broadcast(P)).then_inc(par_in, 16)
                sp.dma_start(wb[:], A["L0_xattn_outnorm_weight"].rearrange("h d -> (h d)").partition_broadcast(P)).then_inc(par_in, 16)
                sp.wait_ge(ones, 3 * STREAMS)
                with sp.Fori(0, PAIRS) as t:
                    for s in range(STREAMS):
                        sp.wait_ge(*ring.used(t, ("qk", U - STREAMS + s, 2)))
                        for i in range(2):
                            rows = slice(i * DH, (i + 1) * DH)
                            sp.dma_start(XT[s][rows, :, i, :], K.xnT_d[t * STREAMS + s][rows]).then_inc(loaded["xT"][s].sem, 16)
                        sp.dma_start(CT[s][:], K.ctxT_d[t * STREAMS + s]).then_inc(loaded["cT"][s].sem, 16)
                        sp.wait_ge(*decay.prev(t, U - STREAMS + s + 1))
                        sp.dma_start(MB[s][:], mb[t * STREAMS + s].partition_broadcast(P)).then_inc(loaded["m"][s].sem, 16)
                    for s in range(STREAMS):
                        sp.wait_ge(*ring.used(t, ("pv", U - STREAMS + s)))
                        for i in range(NT):
                            sp.dma_start(VE[s][:, i, :, 0:DH], vb[t * STREAMS + s, i]).then_inc(loaded["v"][s].sem, 16)
                    for s in range(STREAMS):
                        sp.wait_ge(*stored[s].at(t, 0))
                        sp.dma_start(X[s][:], xb[t * STREAMS + s]).then_inc(loaded["x"][s].sem, 16)

            @block.scalar
            def _(act):
                act.wait_ge(par_in, 32)
                nc.scalar.activation(tg[:, 0:1], gb[:, 0:1], ACT.Tanh).then_inc(tgs, 1)
                credit(act, decay, *stored)

                def store(t):
                    for s in range(STREAMS):
                        act.wait_ge(*x1.at(t, U - STREAMS + s + 1))
                        act.dma_start(ob[t * STREAMS + s], X[s][:]).then_inc(stored[s].sem, 16)

                def turn(t, earlier):
                    for k in range(U):
                        h, s = UNITS[k]
                        if h == 0:
                            act.wait_ge(*loaded["m"][s].at(t, 16))
                        act.wait_ge(*(ring.moved(t, ("qk", k - RB, 2)) if k >= RB else ring.moved_before(t, ("qk", U + k - RB, 2))))
                        for j in range(NT):
                            bcol = K.acol[:, j, t * STREAMS + s, h:h + 1]
                            e = nc.scalar.activation(DT[k % RB][:, j, 0:S - j * P], MB[s][:, h, j * P:S], ACT.Exp, bias=bcol, scale=-1.0)
                        e.then_inc(*decay.up())
                        if earlier is not None and k == RB - 1:
                            store(earlier)
                    decay.close()

                turn(0, None)
                with act.Fori(1, PAIRS) as t:
                    turn(t, t - 1)
                store(PAIRS - 1)
                for s in range(STREAMS):
                    act.wait_ge(*stored[s].at(PAIRS, 0))

            @block.gpsimd
            def _(pool):
                for s in range(STREAMS):
                    nc.gpsimd.memset(VE[s][:, :, :, DH:W], 1.0).then_inc(ones, 1)
                with pool.Fori(0, PAIRS) as t:
                    for k in range(U + NLAG):
                        if k < U:
                            hold(pool, K.pool_passed, *decay.at(t, k + 1))
                            diag = DT[k % RB][:, :, 0:P]
                            nc.gpsimd.affine_select(out=diag, in_=diag, compare_op=ALU.is_ge, fill=0.0, base=0,
                                                    pattern=[[0, NT], [1, P]], channel_multiplier=-1).then_inc(*masked.up())
                        if k >= NLAG:
                            i = (k - NLAG) % RB
                            hold(pool, K.pool_passed, *stat.at(t, (k - NLAG + 1) * NT))
                            nc.gpsimd.tensor_scalar(vare[i][:], stats[i][:, :, 1], 1e-6, None, ALU.add).then_inc(*pstep.up())
                            pool.wait_ge(*pstep.now(t))
                            nc.gpsimd.tensor_tensor(rstd[i][:], vare[i][:], K.half[:, 0:NT], ALU.pow).then_inc(*rs.up())
                    masked.close(), pstep.close(), rs.close()

            @block.vector
            def _(v):
                for s in range(STREAMS):
                    nc.vector.memset(XT[s][DH:P, :, 0, :], 0.0).then_inc(ones, 1)
                    nc.vector.memset(XT[s][0:DH, :, 1, :], 0.0).then_inc(ones, 1)
                v.wait_ge(tgs, 1)
                nc.vector.tensor_scalar(wt[:], wb[:], tg[:, 0:1], None, ALU.mult).then_inc(wts, 1)
                v.wait_ge(wts, 1)
                credit(v, ring.emptied["V"], ring.emptied["S"])

                def then(t, ins):
                    ins.then_inc(*step.up())
                    v.wait_ge(*step.now(t))

                over = lambda x: x[:].unsqueeze(2).broadcast_to([P, NT, DH])
                with v.Fori(0, PAIRS) as t:
                    for k in range(U + NLAG):
                        if k < U:
                            v.wait_ge(*masked.at(t, k + 1))
                            for g, js in enumerate(((0,), (1, 3), (2,))):
                                v.wait_ge(*ring.ready(t, ("qk", k, g)))
                                at = 0
                                for j in js:
                                    n = S - j * P
                                    ins = nc.vector.scalar_tensor_tensor(out=CM[k % RB][:, j, 0:n], in0=ring.bank(("qk", k, g))[:, at:at + n],
                                                                         scalar=float(DH) ** -0.5, in1=DT[k % RB][:, j, 0:n],
                                                                         op0=ALU.mult, op1=ALU.mult)
                                    at += n
                                ins.then_inc(*ring.out(("qk", k, g)))
                        if HLAG <= k < U + HLAG:
                            u = k - HLAG
                            (h, s), i, name = UNITS[u], u % RB, ("pv", u)
                            v.wait_ge(*ring.ready(t, name))
                            sums = ring.bank(name)[:, 0:NT * W].rearrange("p (t w) -> p t w", t=NT)
                            then(t, nc.vector.tensor_scalar(den[i][:], sums[:, :, DH], -1.0, None, ALU.mult))
                            then(t, nc.vector.tensor_tensor(den[i][:], sums[:, :, DH], den[i][:], ALU.max))
                            then(t, nc.vector.tensor_tensor(den[i][:], den[i][:], K.nlcol[:, :, t * STREAMS + s, h], ALU.max))
                            then(t, nc.vector.tensor_scalar(den[i][:], den[i][:], 1e-6, None, ALU.add))
                            then(t, nc.vector.reciprocal(rden[i][:], den[i][:]))
                            nc.vector.tensor_tensor(hh[i][:], sums[:, :, 0:DH], over(rden[i]), ALU.mult).then_inc(*ring.out(name))
                            v.wait_ge(*ring.moved(t, name))
                            for j in range(NT):
                                nc.vector.bn_stats(halves[i][:, j, :], hh[i][:, j, :]).then_inc(*step.up())
                            hold(v, K.v_passed, *step.now(t))
                            for j in range(NT):
                                nc.vector.bn_aggr(stats[i][:, j, :], halves[i][:, j, :]).then_inc(*stat.up())
                        if k >= NLAG:
                            u = k - NLAG
                            (h, s), i = UNITS[u], u % RB
                            if h == 0:
                                v.wait_ge(*loaded["x"][s].at(t, 16))
                            v.wait_ge(*rs.at(t, u + 1))
                            for j in range(NT):
                                ins = nc.vector.tensor_scalar(hh[i][:, j, :], hh[i][:, j, :], stats[i][:, j, 0:1], rstd[i][:, j:j + 1], ALU.subtract, ALU.mult)
                            then(t, ins)
                            head = slice(h * DH, (h + 1) * DH)
                            then(t, nc.vector.tensor_tensor(hh[i][:], hh[i][:], wt[:, head].unsqueeze(1).broadcast_to([P, NT, DH]), ALU.mult))
                            nc.vector.tensor_tensor(X[s][:, :, head], X[s][:, :, head], hh[i][:], ALU.add).then_inc(*x1.up())
                    step.close(), stat.close(), x1.close(), ring.emptied["V"].close(), ring.emptied["S"].close()

            @block.tensor
            def _(pe):
                credit(pe, ring.full)
                pe.wait_ge(ones, 3 * STREAMS)
                with pe.Fori(0, PAIRS) as t:
                    for k in range(U + LAG):
                        scores = {("qk", k, g): ring.take(pe, t, ("qk", k, g)) for g in range(3)} if k < U else {}
                        sums = ring.take(pe, t, ("pv", k - LAG)) if k >= LAG else None
                        for g, js in enumerate(((0,), (1, 3), (2,))):
                            if k < U:
                                h, s = UNITS[k]
                                if h == 0 and g == 0:
                                    pe.wait_ge(*loaded["xT"][s].at(t, 32))
                                    pe.wait_ge(*loaded["cT"][s].at(t, 16))
                                kd = h // 2
                                at = 0
                                for j in js:
                                    n = S - j * P
                                    mm = nc.tensor.matmul(scores["qk", k, g][:, at:at + n], CT[s][:, kd, j * P:(j + 1) * P], XT[s][:, kd, h % 2, j * P:S],
                                                          start=True, stop=True)
                                    at += n
                                mm.then_inc(*ring.full.up())
                            if k >= LAG:
                                h, s = UNITS[k - LAG]
                                if g == 0:
                                    if h == 0:
                                        pe.wait_ge(*loaded["v"][s].at(t, 16 * NT))
                                    pe.wait_ge(*ring.moved(t, ("qk", k - LAG, 2)))
                                for i in ((0, 1), (2,), (3,))[g]:
                                    for j in range(i + 1):
                                        mm = nc.tensor.matmul(sums[:, i * W:(i + 1) * W], CM[(k - LAG) % RB][:, j, (i - j) * P:(i - j + 1) * P],
                                                              VE[s][:, j, h, :], start=(j == 0), stop=(j == i))
                        if k >= LAG:
                            mm.then_inc(*ring.full.up())
                    ring.close_pe()
E_ = 8
F_ = 256
KF = F_ // P
CAP = N // E_
SLOTS = CAP // P
ROW = D + E_
COLS = N // P


def layernorm_stats(nc, v, t, K, src, halves, stats, step, stat):
    first = step.n
    for i in range(NT):
        nc.vector.bn_stats(halves[:, i, :], src[:, i, :]).then_inc(*step.up())
    hold(v, K.v_passed, *step.at(t, first + NT))
    for i in range(NT):
        nc.vector.bn_aggr(stats[:, i, :], halves[:, i, :]).then_inc(*stat.up())


def rstd_on_pool(nc, pool, t, K, stats, vare, rstd, eps, stat, pstep, rs):
    hold(pool, K.pool_passed, *stat.at(t, (rs.n + 1) * NT))
    nc.gpsimd.tensor_scalar(vare[:], stats[:, :, 1], eps, None, ALU.add).then_inc(*pstep.up())
    pool.wait_ge(*pstep.now(t))
    nc.gpsimd.tensor_tensor(rstd[:], vare[:], K.half[:, 0:NT], ALU.pow).then_inc(*rs.up())


def router_phase(nc, A, K):
    R = Store(nc, "router")
    with R.stack:
        FOUR, TURNS = 4, B // 4
        streams = range(FOUR)
        X = [R.sb(f"x{s}", [NT, D]) for s in streams]
        T4 = FOUR * NT
        rows4 = R.sb("row", [T4, ROW])
        XG = [rows4[:, s * NT:(s + 1) * NT, :] for s in streams]
        XT = [R.sb(f"xT{s}", [KD, S]) for s in streams]
        halves = [R.sb(f"halves{s}", [NT, 6]) for s in streams]
        stats = [R.sb(f"stats{s}", [NT, 2]) for s in streams]
        vare, rstd = ([R.sb(f"{n}{s}", [NT]) for s in streams] for n in ("vare", "rstd"))
        lg, zz, ex, rank, prec, sel, q = (R.sb(n, [T4, E_]) for n in "logits shifted exps rank before selected priority".split())
        mx, sm, rc = (R.sb(n, [T4]) for n in "max sum inverse".split())
        gt, eq, bp = (R.sb(n, [T4, E_, E_]) for n in "greater equal before_by".split())
        gw = R.sb("gate_w", [KD, E_])
        tri = R.sb("earlier", [E_, E_])
        zero = R.sb("zero", [SLOTS, ROW])
        groups = [(("xT", s, k), "S") for s in streams for k in range(KD)] + [(("logits", s), "V") for s in streams]
        ring = Ring(R.banks(), groups, R.sem("bank_full"), {"V": R.sem("emptied_V"), "S": R.sem("emptied_S")})
        w_in, tri_ready, zeroed, dummies = R.sem("gate_in"), R.sem("tri_ready"), R.sem("zeroed"), R.sem("dummy_rows")
        x_in = [Sig(R.sem(f"x_in{s}"), 16) for s in streams]
        stored = [Sig(R.sem(f"stored{s}"), 16, 16) for s in streams]
        step = Sig(R.sem("vector_step"), FOUR * NT + 16)
        stat = Sig(R.sem("stats_ready"), FOUR * NT)
        normed = Sig(R.sem("x_normed"), FOUR * NT, FOUR * NT)
        pstep = Sig(R.sem("pool_step"), FOUR)
        rs = Sig(R.sem("rstd_ready"), FOUR)
        shifted = Sig(R.sem("logits_shifted"), 1)
        expd = Sig(R.sem("exp_ready"), 1)
        rows_ready = Sig(R.sem("rows_ready"), 1)
        xb = K.x2_d[0:N, :].rearrange("(b t p) d -> b p t d", p=P, t=NT)
        gb = K.xg_d[0:N, :].rearrange("(b t p) d -> b p t d", p=P, t=NT)
        with nc.Block() as block:
            @block.sync
            def _(sp):
                sp.dma_start(gw[:], A["gate_wT"].rearrange("(k p) e -> p k e", p=P)).then_inc(w_in, 16)
                with sp.Fori(0, TURNS) as t:
                    for s in streams:
                        sp.wait_ge(*normed.prev(t, NT * (s + 1)))
                        sp.dma_start(X[s][:], xb[t * FOUR + s]).then_inc(x_in[s].sem, 16)
                sp.wait_ge(zeroed, 1)
                sp.dma_start(K.xg_d[N:N + CAP, :].rearrange("(t p) d -> p t d", p=P), zero[:]).then_inc(dummies, 16)
                sp.dma_start(K.x2_d[N:N + CAP, :].rearrange("(t p) d -> p t d", p=P), zero[:, :, 0:D]).then_inc(dummies, 16)
                sp.wait_ge(dummies, 32)

            @block.gpsimd
            def _(pool):
                nc.gpsimd.memset(zero[:], 0.0).then_inc(zeroed, 1)
                nc.gpsimd.memset(tri[:], 1.0).then_inc(tri_ready, 1)
                pool.wait_ge(tri_ready, 1)
                nc.gpsimd.affine_select(out=tri[:], in_=tri[:], compare_op=ALU.is_gt, fill=0.0, base=0,
                                        pattern=[[1, E_], [-1, E_]], channel_multiplier=0).then_inc(tri_ready, 1)
                with pool.Fori(0, TURNS) as t:
                    for s in streams:
                        rstd_on_pool(nc, pool, t, K, stats[s], vare[s], rstd[s], 1e-5, stat, pstep, rs)
                    pstep.close(), rs.close()

            @block.vector
            def _(v):
                credit(v, normed, ring.emptied["V"])
                v.wait_ge(tri_ready, 2)

                with v.Fori(0, TURNS) as t:
                    def then(ins):
                        ins.then_inc(*step.up())
                        v.wait_ge(*step.now(t))

                    for s in streams:
                        v.wait_ge(*x_in[s].at(t, 16))
                        layernorm_stats(nc, v, t, K, X[s], halves[s], stats[s], step, stat)
                    for s in streams:
                        v.wait_ge(*rs.at(t, s + 1))
                        v.wait_ge(*stored[s].at(t, 0))
                        for i in range(NT):
                            nc.vector.tensor_scalar(XG[s][:, i, 0:D], X[s][:, i, :], stats[s][:, i, 0:1], rstd[s][:, i:i + 1],
                                                    ALU.subtract, ALU.mult).then_inc(*normed.up())
                    over = lambda x: x[:].unsqueeze(2).broadcast_to([P, T4, E_])
                    pairs = lambda x: x.broadcast_to([P, T4, E_, E_])
                    for s in streams:
                        v.wait_ge(*ring.ready(t, ("logits", s)))
                        nc.vector.tensor_copy(lg[:, s * NT:(s + 1) * NT, :], ring.bank(("logits", s))[:, 0:NT * E_].rearrange("p (t e) -> p t e", t=NT))\
                            .then_inc(*ring.out(("logits", s)))
                    v.wait_ge(*ring.moved(t, ("logits", FOUR - 1)))
                    then(nc.vector.tensor_reduce(mx[:], lg[:], AX, ALU.max))
                    nc.vector.tensor_tensor(zz[:], lg[:], over(mx), ALU.subtract).then_inc(*shifted.up())
                    v.wait_ge(*expd.at(t, 1))
                    then(nc.vector.tensor_reduce(sm[:], ex[:], AX, ALU.add))
                    then(nc.vector.reciprocal(rc[:], sm[:]))
                    prob = rows4[:, :, D:ROW]
                    nc.vector.tensor_tensor(prob, ex[:], over(rc), ALU.mult).then_inc(*rows_ready.up())
                    v.wait_ge(*rows_ready.now(t))
                    other, own = pairs(prob.unsqueeze(2)), pairs(prob.unsqueeze(3))
                    nc.vector.tensor_tensor(gt[:], other, own, ALU.is_gt).then_inc(*step.up())
                    then(nc.vector.tensor_tensor(eq[:], other, own, ALU.is_equal))
                    then(nc.vector.tensor_tensor(eq[:], eq[:], tri[:].unsqueeze(1).broadcast_to([P, T4, E_, E_]), ALU.mult))
                    then(nc.vector.tensor_tensor(gt[:], gt[:], eq[:], ALU.add))
                    nc.vector.tensor_reduce(rank[:], gt[:], AX, ALU.add).then_inc(*step.up())
                    then(nc.vector.tensor_tensor(bp[:], gt[:], other, ALU.mult))
                    then(nc.vector.tensor_reduce(prec[:], bp[:], AX, ALU.add))
                    then(nc.vector.tensor_scalar(sel[:], prec[:], 0.9, None, ALU.is_lt))
                    then(nc.vector.tensor_scalar(rank[:], rank[:], -1.0, -1.0, ALU.mult, ALU.add))
                    then(nc.vector.tensor_tensor(q[:], prob, rank[:], ALU.add))
                    then(nc.vector.tensor_tensor(q[:], q[:], sel[:], ALU.mult))
                    nc.vector.tensor_scalar(sel[:], sel[:], 1.0e9, -1.0e9, ALU.mult, ALU.add).then_inc(*step.up())
                    v.wait_ge(*step.now(t))
                    turn_R = K.R[:].rearrange("p e (g b) t -> p g (b t) e", g=TURNS)[:, t]
                    nc.vector.tensor_tensor(turn_R, q[:], sel[:], ALU.add).then_inc(*step.up())
                    step.close(), stat.close(), normed.close(), shifted.close(), rows_ready.close(), ring.emptied["V"].close()

            @block.scalar
            def _(act):
                credit(act, ring.emptied["S"], *stored)
                with act.Fori(0, TURNS) as t:
                    for s in streams:
                        for k in range(KD):
                            act.wait_ge(*ring.ready(t, ("xT", s, k)))
                            nc.scalar.activation(XT[s][:, k, :], ring.bank(("xT", s, k))[:], ACT.Copy).then_inc(*ring.out(("xT", s, k)))
                    act.wait_ge(*shifted.at(t, 1))
                    nc.scalar.activation(ex[:], zz[:], ACT.Exp).then_inc(*expd.up())
                    act.wait_ge(*rows_ready.at(t, 1))
                    for s in streams:
                        act.dma_start(gb[t * FOUR + s], XG[s]).then_inc(stored[s].sem, 16)
                    expd.close(), ring.emptied["S"].close()
                for s in streams:
                    act.wait_ge(*stored[s].at(TURNS, 0))

            @block.tensor
            def _(pe):
                credit(pe, ring.full)
                pe.wait_ge(w_in, 16)
                with pe.Fori(0, TURNS) as t:
                    for s in streams:
                        pe.wait_ge(*normed.at(t, NT * (s + 1)))
                        for k in range(KD):
                            bank = ring.take(pe, t, ("xT", s, k))
                            for i in range(NT):
                                mm = nc.tensor.transpose(bank[:, i * P:(i + 1) * P], XG[s][:, i, k * P:(k + 1) * P], K.ident[:])
                            mm.then_inc(*ring.full.up())
                    for s in streams:
                        pe.wait_ge(*ring.moved(t, ("xT", s, KD - 1)))
                        bank = ring.take(pe, t, ("logits", s))
                        for i in range(NT):
                            for k in range(KD):
                                mm = nc.tensor.matmul(bank[:, i * E_:(i + 1) * E_], XT[s][:, k, i * P:(i + 1) * P], gw[:, k, :],
                                                      start=(k == 0), stop=(k == KD - 1))
                        mm.then_inc(*ring.full.up())
                    ring.close_pe()


def routing_phase(nc, A, K):
    R = Store(nc, "route")
    BF = mybir.dt.bfloat16
    LO, HI = 32, CAP // 32
    with R.stack:
        T, Tn, cnt, ok, stepc, left = (R.sb(n, [E_]) for n in "T Tn cnt ok stepc left".split())
        cmp_, gtm, eqm, within, tot, M, pos, lo, hi, posf = (R.sb(n, [E_, COLS]) for n in "cmp gtm eqm within tot M pos lo hi posf".split())
        posi, hii, loi = (R.sb(n, [E_, COLS], I32) for n in "posi hii loi".split())
        keep1 = R.sb("segments", [E_, COLS])
        ones, before = R.sb("ones", [P]), R.sb("before", [P])
        hiota, liota = R.sb("hi_iota", [HI]), R.sb("lo_iota", [LO])
        ciota, piota = R.sb("col_iota", [COLS]), R.sb("part_iota", [1])
        LH = R.sb("hot_hi", [E_, COLS, 96], BF)
        RL = R.sb("hot_lo", [E_, COLS, LO], BF)
        vacant = R.rows("vacant", [HI, E_, LO])
        i1, i2, un = (R.rows(n, [HI, E_, LO]) for n in ("i1", "i2", "un"))
        slots = R.rows("slots", [HI, E_, LO], I32)
        banks = R.banks()
        const = R.sem("consts")
        step = Sig(R.sem("vector_step"), 4)
        counted = Sig(R.sem("counted"), 1)
        partial = Sig(R.sem("partial_counts"), 1)
        st2 = Sig(R.sem("tail_step"), 0)
        masks, sums = R.sem("mask_ready"), R.sem("mask_summed")
        hot, made, listed, listed_in, out_ready = R.sem("hot_ready"), R.sem("lists_made"), R.sem("list_stored"), R.sem("list_in"), R.sem("slots_ready")
        cs, cs2 = Sig(R.sem("const_step"), 0), Sig(R.sem("start_step"), 0)
        halved = Sig(R.sem("step_halved"), 1)
        ITER = 29
        over = lambda x: x[:].unsqueeze(2).broadcast_to([P, E_, COLS])
        flat = lambda x: x[:].rearrange("p e c -> p (e c)")
        with nc.Block() as block:
            @block.gpsimd
            def _(pool):
                nc.gpsimd.memset(ones[:], 1.0).then_inc(const, 1)
                nc.gpsimd.memset(before[:], 1.0).then_inc(*cs.up())
                pool.wait_ge(*cs.now(0))
                nc.gpsimd.affine_select(out=before[:], in_=before[:], compare_op=ALU.is_gt, fill=0.0, base=0,
                                        pattern=[[1, P]], channel_multiplier=-1).then_inc(const, 1)
                nc.gpsimd.memset(keep1[:], 1.0).then_inc(*cs.up())
                pool.wait_ge(*cs.now(0))
                nc.gpsimd.memset(keep1[:, :, 0:1], 0.0).then_inc(const, 1)
                nc.gpsimd.iota(hiota[:], [[1, HI]], 0, 0, allow_small_or_imprecise_dtypes=True).then_inc(const, 1)
                nc.gpsimd.iota(liota[:], [[1, LO]], 0, 0, allow_small_or_imprecise_dtypes=True).then_inc(const, 1)
                nc.gpsimd.iota(ciota[:], [[1, COLS]], 0, 0, allow_small_or_imprecise_dtypes=True).then_inc(const, 1)
                nc.gpsimd.iota(piota[:], [[1, 1]], 0, 1, allow_small_or_imprecise_dtypes=True).then_inc(const, 1)
                nc.gpsimd.iota(vacant[:], [[0, E_], [1, LO]], N, LO, allow_small_or_imprecise_dtypes=True).then_inc(const, 1)
                nc.gpsimd.memset(LH[:], 0.0).then_inc(const, 1)

            @block.vector
            def _(v):
                nc.vector.memset(T[:], -8.0).then_inc(*cs2.up())
                nc.vector.memset(stepc[:], 4.0).then_inc(*cs2.up())
                v.wait_ge(*cs2.now(0))
                v.wait_ge(const, 2)
                with v.Fori(0, ITER) as t:
                    def then(ins):
                        ins.then_inc(*step.up())
                        v.wait_ge(*step.now(t))
                    then(nc.vector.tensor_tensor(Tn[:], T[:], stepc[:], ALU.add))
                    then(nc.vector.tensor_tensor(cmp_[:], K.R[:].rearrange("p e b t -> p e (b t)"), over(Tn), ALU.is_ge))
                    nc.vector.tensor_reduce(cnt[:], cmp_[:], AX, ALU.add).then_inc(*partial.up())
                    v.wait_ge(*counted.at(t, 1))
                    nc.vector.scalar_tensor_tensor(out=ok[:], in0=banks[0][:, 0:E_], scalar=float(CAP) - 0.5, in1=stepc[:],
                                                   op0=ALU.is_gt, op1=ALU.mult).then_inc(*step.up())
                    v.wait_ge(*step.now(t))
                    nc.vector.tensor_tensor(T[:], T[:], ok[:], ALU.add).then_inc(*step.up())
                    v.wait_ge(*step.now(t))
                    nc.vector.tensor_scalar(stepc[:], stepc[:], 0.5, None, ALU.mult).then_inc(*halved.up())
                    v.wait_ge(*halved.now(t))
                    step.close(), partial.close(), halved.close()

                def then2(ins):
                    ins.then_inc(*st2.up())
                    v.wait_ge(*st2.now(0))

                Rv = K.R[:].rearrange("p e b t -> p e (b t)")
                def prefix(base):
                    then2(nc.vector.tensor_copy(flat(tot), banks[base + 1][:, 0:E_ * COLS]))
                    then2(nc.vector.tensor_tensor_scan(flat(pos), flat(keep1), flat(tot), 0.0, ALU.mult, ALU.add))
                    then2(nc.vector.tensor_tensor(pos[:], pos[:], tot[:], ALU.subtract))
                    then2(nc.vector.tensor_tensor(flat(pos), banks[base][:, 0:E_ * COLS], flat(pos), ALU.add))

                v.wait_ge(const, 9)
                then2(nc.vector.tensor_tensor(gtm[:], Rv, over(T), ALU.is_gt))
                nc.vector.tensor_tensor(eqm[:], Rv, over(T), ALU.is_equal).then_inc(masks, 1)
                then2(nc.vector.tensor_reduce(cnt[:], gtm[:], AX, ALU.add))
                nc.vector.tensor_copy(ok[:], cnt[:]).then_inc(masks, 1)
                v.wait_ge(sums, 1)
                prefix(1)
                v.wait_ge(sums, 2)
                then2(nc.vector.tensor_scalar(left[:], banks[0][:, 0:E_], -1.0, float(CAP), ALU.mult, ALU.add))
                then2(nc.vector.tensor_tensor(M[:], pos[:], over(left), ALU.is_lt))
                then2(nc.vector.tensor_tensor(M[:], M[:], eqm[:], ALU.mult))
                nc.vector.tensor_tensor(M[:], M[:], gtm[:], ALU.add).then_inc(masks, 1)
                v.wait_ge(masks, 3)
                v.wait_ge(sums, 3)
                prefix(3)
                then2(nc.vector.tensor_copy(posi[:], pos[:]))
                then2(nc.vector.tensor_scalar(hii[:], posi[:], 5, None, ALU.arith_shift_right))
                then2(nc.vector.tensor_scalar(loi[:], posi[:], LO - 1, None, ALU.bitwise_and))
                then2(nc.vector.tensor_copy(hi[:], hii[:]))
                then2(nc.vector.tensor_copy(lo[:], loi[:]))
                then2(nc.vector.tensor_scalar(cmp_[:], M[:], 1000.0, -1000.0, ALU.mult, ALU.add))
                then2(nc.vector.tensor_tensor(hi[:], hi[:], cmp_[:], ALU.add))
                for e in range(E_):
                    wide = lambda x, n: x[:, e, :].unsqueeze(2).broadcast_to([P, COLS, n])
                    hot_hi = LH[:, e, :, 0:HI]
                    then2(nc.vector.tensor_tensor(hot_hi, wide(hi, HI), hiota[:].unsqueeze(1).broadcast_to([P, COLS, HI]), ALU.is_equal))
                    nc.vector.tensor_tensor(RL[:, e], wide(lo, LO), liota[:].unsqueeze(1).broadcast_to([P, COLS, LO]), ALU.is_equal).then_inc(*st2.up())
                    nc.vector.tensor_scalar(LH[:, e, :, 32:32 + HI], hot_hi, piota[:, 0:1], None, ALU.mult).then_inc(*st2.up())
                    nc.vector.tensor_tensor(LH[:, e, :, 64:64 + HI], hot_hi, ciota[:].unsqueeze(2).broadcast_to([P, COLS, HI]), ALU.mult).then_inc(hot, 1)
                v.wait_ge(made, 1)
                L = banks[5]
                fl = lambda x: x[:].rearrange("p e l -> p (e l)")
                then2(nc.vector.tensor_scalar(fl(i1), L[64:64 + HI, 0:E_ * LO], float(P), None, ALU.mult))
                then2(nc.vector.tensor_tensor(fl(i2), L[32:32 + HI, 0:E_ * LO], fl(i1), ALU.add))
                then2(nc.vector.tensor_scalar(fl(un), L[0:HI, 0:E_ * LO], -1.0, 1.0, ALU.mult, ALU.add))
                then2(nc.vector.tensor_tensor(un[:], un[:], vacant[:], ALU.mult))
                nc.vector.tensor_tensor(slots[:], i2[:], un[:], ALU.add).then_inc(out_ready, 1)

            @block.tensor
            def _(pe):
                pe.wait_ge(const, 2)
                with pe.Fori(0, ITER) as t:
                    pe.wait_ge(*partial.at(t, 1))
                    nc.tensor.matmul(banks[0][:, 0:E_], ones[:], cnt[:], start=True, stop=True).then_inc(*counted.up())
                    counted.close()
                pe.wait_ge(masks, 1)
                nc.tensor.matmul(banks[1][:, 0:E_ * COLS], before[:], flat(eqm), start=True, stop=True)
                nc.tensor.matmul(banks[2][:, 0:E_ * COLS], ones[:], flat(eqm), start=True, stop=True).then_inc(sums, 1)
                pe.wait_ge(masks, 2)
                nc.tensor.matmul(banks[0][:, 0:E_], ones[:], ok[:], start=True, stop=True).then_inc(sums, 1)
                pe.wait_ge(masks, 3)
                nc.tensor.matmul(banks[3][:, 0:E_ * COLS], before[:], flat(M), start=True, stop=True)
                nc.tensor.matmul(banks[4][:, 0:E_ * COLS], ones[:], flat(M), start=True, stop=True).then_inc(sums, 1)
                for e in range(E_):
                    pe.wait_ge(hot, e + 1)
                    for c in range(COLS):
                        mm = nc.tensor.matmul(banks[5][0:96, e * LO:(e + 1) * LO], LH[:, e, c, :], RL[:, e, c, :],
                                              start=(c == 0), stop=(c == COLS - 1))
                mm.then_inc(made, 1)

            @block.sync
            def _(sp):
                sp.wait_ge(out_ready, 1)
                sp.dma_start(K.slots_d[:, :].rearrange("e (h l) -> h e l", h=HI), slots[:]).then_inc(listed, 16)
                sp.wait_ge(listed, 16)
                sp.dma_start(K.idx[:], K.slots_d[:, :].rearrange("e (t p) -> p e t", p=P), allow_slow_non_contiguous=True).then_inc(listed_in, 16)
                sp.wait_ge(listed_in, 16)


def expert_phase(nc, A, K):
    R = Store(nc, "expert")
    TURNS = E_ // STREAMS
    with R.stack:
        two = range(STREAMS)
        W1 = [R.sb(f"w1{s}", [KD, F_]) for s in two]
        W2 = [R.sb(f"w2{s}", [KF, D]) for s in two]
        GX = [R.sb(f"rows{s}", [SLOTS, ROW]) for s in two]
        XT = [R.sb(f"xT{s}", [KD, CAP]) for s in two]
        HT = [R.sb(f"hT{s}", [KF, CAP]) for s in two]
        Y = [R.sb(f"y{s}", [SLOTS, D]) for s in two]
        sc = [R.sb(f"share{s}", [SLOTS]) for s in two]
        ic = [R.sb(f"idx{s}", [SLOTS], I32) for s in two]
        gb, tg = R.sb("g", [1]), R.sb("tanh_g", [1])
        groups = [(("xT", s, k), "S") for s in two for k in range(KD)]
        groups += [(("hT", s, m), "S") for s in two for m in range(KF)]
        groups += [(("y", s, i), "V") for s in two for i in range(SLOTS // 2)]
        ring = Ring(R.banks(), groups, R.sem("bank_full"), {"V": R.sem("emptied_V"), "S": R.sem("emptied_S")})
        g_in, tgs = R.sem("g_in"), R.sem("tanh_ready")
        w_in = [Sig(R.sem(f"weights_in{s}"), 32) for s in two]
        copied = Sig(R.sem("idx_copied"), STREAMS)
        rows_in = [Sig(R.sem(f"rows_in{s}"), 16 * SLOTS) for s in two]
        share = Sig(R.sem("share_ready"), STREAMS)
        added = [Sig(R.sem(f"rows_added{s}"), 16 * SLOTS) for s in two]
        y_free = Sig(R.sem("y_free"), STREAMS, STREAMS)
        w1 = A["w1T"].rearrange("e (k p) f -> e p k f", p=P)
        w2 = A["w2T"].rearrange("e (k p) d -> e p k d", p=P)
        with nc.Block() as block:
            @block.sync
            def _(sp):
                sp.dma_start(gb[:], A["g_ffn"][0:1].partition_broadcast(P)).then_inc(g_in, 16)
                with sp.Fori(0, TURNS) as t:
                    for s in two:
                        sp.wait_ge(*ring.used(t, ("y", s, SLOTS // 2 - 1)))
                        sp.dma_start(W1[s][:], w1[t * STREAMS + s]).then_inc(w_in[s].sem, 16)
                        sp.dma_start(W2[s][:], w2[t * STREAMS + s]).then_inc(w_in[s].sem, 16)

            @block.gpsimd
            def _(pool):
                def add_rows(t, s):
                    for i in range(SLOTS):
                        hold(pool, K.pool_passed, *ring.moved(t, ("y", s, i // 2)))
                        pool.indirect_dma_start(K.x2_d[:, :], bass.IndirectOffsetOnAxis(ap=ic[s][:, i:i + 1], axis=0),
                                                Y[s][:, i, :], None, compute_op=ALU.add).then_inc(added[s].sem, 16)
                    pool.wait_ge(*added[s].at(t, 16 * SLOTS))
                    pool.sem_inc(y_free.sem, 1)

                def gather(t, s):
                    nc.gpsimd.tensor_copy(ic[s][:], K.idx[:, t * STREAMS + s, :]).then_inc(copied.sem, 1)
                    hold(pool, K.pool_passed, *copied.at(t, s + 1))
                    for i in range(SLOTS):
                        pool.indirect_dma_start(GX[s][:, i, :], None, K.xg_d[:, :],
                                                bass.IndirectOffsetOnAxis(ap=ic[s][:, i:i + 1], axis=0)).then_inc(rows_in[s].sem, 16)

                credit(pool, y_free)
                for s in two:
                    gather(0, s)
                with pool.Fori(1, TURNS) as t:
                    for s in two:
                        add_rows(t - 1, s)
                        gather(t, s)
                for s in two:
                    add_rows(TURNS - 1, s)

            @block.scalar
            def _(act):
                act.wait_ge(g_in, 16)
                nc.scalar.activation(tg[:], gb[:], ACT.Tanh).then_inc(tgs, 1)
                credit(act, ring.emptied["S"])
                with act.Fori(0, TURNS) as t:
                    for s in two:
                        for k in range(KD):
                            act.wait_ge(*ring.ready(t, ("xT", s, k)))
                            nc.scalar.activation(XT[s][:, k, :], ring.bank(("xT", s, k))[:], ACT.Copy).then_inc(*ring.out(("xT", s, k)))
                    for s in two:
                        for m in range(KF):
                            act.wait_ge(*ring.ready(t, ("hT", s, m)))
                            nc.scalar.activation(HT[s][:, m, :], ring.bank(("hT", s, m))[:], ACT.Gelu).then_inc(*ring.out(("hT", s, m)))
                    ring.emptied["S"].close()

            @block.vector
            def _(v):
                credit(v, ring.emptied["V"])
                v.wait_ge(tgs, 1)
                with v.Fori(0, TURNS) as t:
                    for s in two:
                        v.wait_ge(*rows_in[s].at(t, 16 * SLOTS))
                        nc.vector.tensor_scalar(sc[s][:], GX[s][:, :, D + t * STREAMS + s], tg[:, 0:1], None, ALU.mult).then_inc(*share.up())
                    for s in two:
                        v.wait_ge(*share.at(t, s + 1))
                        v.wait_ge(*y_free.prev(t, s + 1))
                        for i in range(SLOTS):
                            name = ("y", s, i // 2)
                            if i % 2 == 0:
                                v.wait_ge(*ring.ready(t, name))
                            ins = nc.vector.tensor_scalar(Y[s][:, i, :], ring.bank(name)[:, i % 2 * D:(i % 2 + 1) * D], sc[s][:, i:i + 1], None, ALU.mult)
                            if i % 2:
                                ins.then_inc(*ring.out(name))
                    share.close(), ring.emptied["V"].close()

            @block.tensor
            def _(pe):
                credit(pe, ring.full)
                with pe.Fori(0, TURNS) as t:
                    for s in two:
                        pe.wait_ge(*rows_in[s].at(t, 16 * SLOTS))
                        for k in range(KD):
                            bank = ring.take(pe, t, ("xT", s, k))
                            for i in range(SLOTS):
                                mm = nc.tensor.transpose(bank[:, i * P:(i + 1) * P], GX[s][:, i, k * P:(k + 1) * P], K.ident[:])
                            mm.then_inc(*ring.full.up())
                    for s in two:
                        pe.wait_ge(*w_in[s].at(t, 32))
                        pe.wait_ge(*ring.moved(t, ("xT", s, KD - 1)))
                        for m in range(KF):
                            bank = ring.take(pe, t, ("hT", s, m))
                            for k in range(KD):
                                mm = nc.tensor.matmul(bank[:], W1[s][:, k, m * P:(m + 1) * P], XT[s][:, k, :], start=(k == 0), stop=(k == KD - 1))
                            mm.then_inc(*ring.full.up())
                    for s in two:
                        pe.wait_ge(*ring.moved(t, ("hT", s, KF - 1)))
                        for g in range(SLOTS // 2):
                            bank = ring.take(pe, t, ("y", s, g))
                            for i in range(2):
                                for m in range(KF):
                                    mm = nc.tensor.matmul(bank[:, i * D:(i + 1) * D], HT[s][:, m, (2 * g + i) * P:(2 * g + i + 1) * P], W2[s][:, m, :],
                                                          start=(m == 0), stop=(m == KF - 1))
                            mm.then_inc(*ring.full.up())
                    ring.close_pe()


def retrieval_phase(nc, A, K):
    R = Store(nc, "retr")
    two = range(STREAMS)
    PARTS = ((0,), (1, 3), (2,))
    with R.stack:
        X, Q, C, ST, Z = ([R.sb(f"{n}{s}", shape) for s in two] for n, shape in
                          (("x", [NT, D]), ("q", [NT, D]), ("cT", [KD, S]), ("scores", [NT, S]), ("y", [NT, D])))
        halves = [R.sb(f"halves{s}", [NT, 6]) for s in two]
        stats = [R.sb(f"stats{s}", [NT, 2]) for s in two]
        vare, rstd = ([R.sb(f"{n}{s}", [NT]) for s in two] for n in ("vare", "rstd"))
        gb, tg = R.sb("g", [1]), R.sb("tanh_g", [1])
        groups = [(("s", s, j), "S") for s in two for j in range(len(PARTS))] + [(("p", s, g), "V") for s in two for g in range(NT // 2)]
        ring = Ring(R.banks(), groups, R.sem("bank_full"), {"V": R.sem("emptied_V"), "S": R.sem("emptied_S")})
        g_in, tgs = R.sem("g_in"), R.sem("tanh_ready")
        x_in = [Sig(R.sem(f"x_in{s}"), 16) for s in two]
        c_in = [Sig(R.sem(f"ctx_in{s}"), 16) for s in two]
        stored = [Sig(R.sem(f"stored{s}"), 32, 32) for s in two]
        step = Sig(R.sem("vector_step"), STREAMS * 2 * NT)
        stat = Sig(R.sem("stats_ready"), 2 * STREAMS * NT)
        normed = Sig(R.sem("x_normed"), STREAMS)
        masked = Sig(R.sem("scores_masked"), STREAMS)
        x3 = Sig(R.sem("x3_ready"), STREAMS)
        y0 = Sig(R.sem("y_ready"), STREAMS)
        pstep = Sig(R.sem("pool_step"), 2 * STREAMS)
        rs = Sig(R.sem("rstd_ready"), 2 * STREAMS)
        rows = lambda d: d.rearrange("(b t p) d -> b p t d", p=P, t=NT)
        xb, x3b, yb = rows(K.x2_d[0:N, :]), rows(K.x3_d[:, :]), rows(K.y_d[0:N, :])
        with nc.Block() as block:
            @block.sync
            def _(sp):
                sp.dma_start(gb[:], A["g_xattn"][1:2].partition_broadcast(P)).then_inc(g_in, 16)
                with sp.Fori(0, PAIRS) as t:
                    for s in two:
                        sp.wait_ge(*ring.used(t, ("s", s, 2)))
                        sp.dma_start(C[s][:], K.ctxT_d[t * STREAMS + s]).then_inc(c_in[s].sem, 16)
                        sp.wait_ge(*stored[s].at(t, 0))
                        sp.dma_start(X[s][:], xb[t * STREAMS + s]).then_inc(x_in[s].sem, 16)

            @block.gpsimd
            def _(pool):
                with pool.Fori(0, PAIRS) as t:
                    for s in two:
                        rstd_on_pool(nc, pool, t, K, stats[s], vare[s], rstd[s], 1e-5, stat, pstep, rs)
                    for s in two:
                        hold(pool, K.pool_passed, *ring.moved(t, ("s", s, 2)))
                        diag = ST[s][:, :, 0:P]
                        nc.gpsimd.affine_select(out=diag, in_=diag, compare_op=ALU.is_ge, fill=0.0, base=0,
                                                pattern=[[0, NT], [1, P]], channel_multiplier=-1).then_inc(*masked.up())
                    for s in two:
                        rstd_on_pool(nc, pool, t, K, stats[s], vare[s], rstd[s], 1e-5, stat, pstep, rs)
                    pstep.close(), rs.close(), masked.close()

            @block.vector
            def _(v):
                credit(v, ring.emptied["V"])
                v.wait_ge(tgs, 1)
                with v.Fori(0, PAIRS) as t:
                    for s in two:
                        v.wait_ge(*x_in[s].at(t, 16))
                        layernorm_stats(nc, v, t, K, X[s], halves[s], stats[s], step, stat)
                    for s in two:
                        v.wait_ge(*rs.at(t, s + 1))
                        for i in range(NT):
                            ins = nc.vector.tensor_scalar(Q[s][:, i, :], X[s][:, i, :], stats[s][:, i, 0:1], rstd[s][:, i:i + 1], ALU.subtract, ALU.mult)
                        ins.then_inc(*normed.up())
                    for s in two:
                        v.wait_ge(*stored[s].at(t, 0))
                        for g in range(NT // 2):
                            name, rows2 = ("p", s, g), slice(2 * g, 2 * g + 2)
                            v.wait_ge(*ring.ready(t, name))
                            psum = ring.bank(name)[:].rearrange("p (t d) -> p t d", t=2)
                            nc.vector.tensor_tensor(Z[s][:, rows2, :], psum, Q[s][:, rows2, :], ALU.add).then_inc(*ring.out(name))
                        v.wait_ge(*ring.moved(t, ("p", s, NT // 2 - 1)))
                        nc.vector.scalar_tensor_tensor(out=X[s][:], in0=Z[s][:], scalar=tg[:, 0:1], in1=X[s][:], op0=ALU.mult, op1=ALU.add).then_inc(*x3.up())
                        v.wait_ge(*x3.now(t))
                        layernorm_stats(nc, v, t, K, X[s], halves[s], stats[s], step, stat)
                    for s in two:
                        v.wait_ge(*rs.at(t, STREAMS + s + 1))
                        for i in range(NT):
                            ins = nc.vector.tensor_scalar(Z[s][:, i, :], X[s][:, i, :], stats[s][:, i, 0:1], rstd[s][:, i:i + 1], ALU.subtract, ALU.mult)
                        ins.then_inc(*y0.up())
                    step.close(), stat.close(), normed.close(), x3.close(), y0.close(), ring.emptied["V"].close()

            @block.scalar
            def _(act):
                act.wait_ge(g_in, 16)
                nc.scalar.activation(tg[:], gb[:], ACT.Tanh).then_inc(tgs, 1)
                credit(act, ring.emptied["S"], *stored)
                with act.Fori(0, PAIRS) as t:
                    for s in two:
                        for g, js in enumerate(PARTS):
                            act.wait_ge(*ring.ready(t, ("s", s, g)))
                            at = 0
                            for j in js:
                                n = S - j * P
                                ins = nc.scalar.activation(ST[s][:, j, 0:n], ring.bank(("s", s, g))[:, at:at + n], ACT.Copy)
                                at += n
                            ins.then_inc(*ring.out(("s", s, g)))
                    for s in two:
                        act.wait_ge(*x3.at(t, s + 1))
                        act.dma_start(x3b[t * STREAMS + s], X[s][:]).then_inc(stored[s].sem, 16)
                        act.wait_ge(*y0.at(t, s + 1))
                        act.dma_start(yb[t * STREAMS + s], Z[s][:]).then_inc(stored[s].sem, 16)
                    ring.emptied["S"].close()
                for s in two:
                    act.wait_ge(*stored[s].at(PAIRS, 0))

            @block.tensor
            def _(pe):
                credit(pe, ring.full)
                with pe.Fori(0, PAIRS) as t:
                    for s in two:
                        pe.wait_ge(*c_in[s].at(t, 16))
                        for g, js in enumerate(PARTS):
                            bank = ring.take(pe, t, ("s", s, g))
                            at = 0
                            for j in js:
                                n = S - j * P
                                for k in range(KD):
                                    mm = nc.tensor.matmul(bank[:, at:at + n], C[s][:, k, j * P:(j + 1) * P], C[s][:, k, j * P:S], start=(k == 0), stop=(k == KD - 1))
                                at += n
                            mm.then_inc(*ring.full.up())
                    for s in two:
                        pe.wait_ge(*normed.at(t, s + 1))
                        pe.wait_ge(*masked.at(t, s + 1))
                        for g in range(NT // 2):
                            bank = ring.take(pe, t, ("p", s, g))
                            for i in (2 * g, 2 * g + 1):
                                for j in range(i + 1):
                                    mm = nc.tensor.matmul(bank[:, i % 2 * D:(i % 2 + 1) * D], ST[s][:, j, (i - j) * P:(i - j + 1) * P], Q[s][:, j, :],
                                                          start=(j == 0), stop=(j == i))
                            mm.then_inc(*ring.full.up())
                    ring.close_pe()
LAYERS = 2
LH = 8
LD = 64
INNER = LH * LD
HID = 682
MH = -(-HID // P)
TAIL = HID - (MH - 1) * P
PAIRS_H = INNER // P
SMALL, TABLES = 16 * 7, 16 * 4
FAR = -3.0e38


def start_ring(engine, sig, before, work):
    engine.sem_inc(sig.sem, before)
    sig.n = before
    work()
    engine.wait_ge(sig.sem, sig.n)
    engine.sem_inc(sig.sem, sig.per - sig.n)
    sig.n = 0


def layer_phase(nc, A, K):
    R = Store(nc, "layer")
    two = range(STREAMS)
    TILE_UNITS = [(i, s) for i in range(NT) for s in two]
    HEAD_UNITS = [(h, s) for h in range(LH) for s in two]
    U, V1 = len(HEAD_UNITS), LD + 1
    TLAG, PLAG, VLAG, RB, TR, TB = 2, 2, 4, 4, 3, 2
    with R.stack:
        weight = lambda n, shape: [R.sb(f"{n}_high", shape, R32), R.sb(f"{n}_low", shape)]
        Wqkv, Wo, W1, W2 = (weight(n, shape) for n, shape in (("wqkv", [KD, 3 * INNER]), ("wo", [PAIRS_H, D]), ("w1", [KD, 2 * HID]), ("w2", [MH, D])))
        Wqkv, Wo, W1, W2 = ((x[0], R.rounded(f"{n}_low", list(x[1].shape[1:])), x[1]) for n, x in (("wqkv", Wqkv), ("wo", Wo), ("w1", W1), ("w2", W2)))
        ba, bg, b2 = R.sb("b1_a", [MH]), R.sb("b1_g", [MH]), R.sb("b2", [D])
        lng, lnb = R.sb("ln_g", [KD]), R.sb("ln_b", [KD])
        qks = R.sb("qk_scale", [2, LD])
        At, Bt = R.sb("along", [NT, 2, LD]), R.sb("across", [NT, 2, LD])
        gb, tg = R.sb("g", [1]), R.sb("tanh_g", [1])
        mask = R.sb("mask", [2, P])
        shift, carry = R.sb("shift", [P]), R.sb("carry", [P])
        Y = [R.sb(f"y{s}", [NT, D]) for s in two]
        HT = [R.sb(f"hT{s}", [KD, S + 1], R32) for s in two]
        V = [R.sb(f"v{s}", [NT, LH, V1]) for s in two]
        QKT = [R.sb(f"qkT{s}", [2 * PAIRS_H, S]) for s in two]
        O = [R.sb(f"o{s}", [NT, INNER]) for s in two]
        OB = [R.sb(f"oT{s}", [2 + PAIRS_H * S], R32) for s in two]
        T1 = [R.sb(f"along_t{i}", [2 * LH, LD]) for i in range(TB)]
        ss, pw, rn = ([R.sb(f"{n}{i}", [2 * LH]) for i in range(TB)] for n in ("ss", "pw", "rn"))
        SM, PT = ([R.sb(f"{n}{i}", [NT, 2, P]) for i in range(c)] for n, c in (("scores", RB), ("probsT", TR)))
        nmax, rden = ([R.sb(f"{n}{i}", [NT]) for i in range(RB)] for n in ("nmax", "rden"))
        halves = [R.sb(f"halves{s}", [NT, 2, 6]) for s in two]
        stats = [R.sb(f"stats{s}", [NT, 2]) for s in two]
        vare, rstd = ([R.sb(f"{n}{s}", [NT]) for s in two] for n in ("vare", "rstd"))

        flat3 = lambda x: x[:].rearrange("p w b j -> p (w b j)")
        SQ, T2 = ([flat3(x).rearrange("p (h d) -> p h d", d=LD) for x in part] for part in (SM[0:TB], SM[TB:2 * TB]))
        GL = [flat3(SM[i // 2])[:, i % 2 * S:(i % 2 + 1) * S] for i in range(RB)]
        X3 = [x[:].rearrange("p (t a) d -> p t (a d)", t=NT) for x in T1]
        Z = [x[:, :, 0:D] for x in O]
        OT = [x[:, 2:2 + PAIRS_H * S].rearrange("p (k n) -> p k n", n=S) for x in OB]
        QKR = [R.rounded(f"qkT{s}", [2 * PAIRS_H, S]) for s in two]
        OTL = [x[:, 0:PAIRS_H, :] for x in QKR]
        HH = [x[:, 0:MH, :] for x in QKR]
        SPARE = [flat3(x) for x in PT[0:3] + SM[2:3]]
        SPARER = [flat3(R.rounded(n, [NT, 2, P])) for n in ("probsT0", "probsT1", "probsT2", "scores2")]
        AFF = lambda s, k: SPARE[s * KD + k][:, 0:S]

        def hidden(s, m, low=False):
            if m < 2:
                return (QKR if low else QKT)[s][:, MH + m, :]
            return (SPARER if low else SPARE)[2 * s + (m - 2) // 2][:, m % 2 * S:(m % 2 + 1) * S]

        def hT(s, k, at=0, n=S):
            low = OB[s][:, 1 + at:1 + at + n] if k else OB[s][:, S + 2 + at:S + 2 + at + n]
            return HT[s][:, k, k + at:k + at + n], low

        def late(s, k, i):
            return hT(s, k, i * P - k, P)

        groups = []
        for m in range(len(TILE_UNITS) + TLAG):
            if m < len(TILE_UNITS):
                groups += [(("q", m), "V"), (("k", m), "V"), (("v", m), "S")]
            if m >= TLAG:
                groups += [(("qkT", m - TLAG, c), "S") for c in range(2)]
        for k in range(U + VLAG):
            if k < U:
                groups += [(("sim", k, g), "V") for g in range(NT // 2)]
            if PLAG <= k < U + PLAG:
                groups += [(("pT", k - PLAG, 0), "S"), (("pT", k - PLAG, 1), "V")]
            if k >= VLAG:
                groups += [(("o", k - VLAG), "V")]
        groups += [(("oT", s, k), "V") for s in two for k in range(PAIRS_H)]
        groups += [(("wo", s, g), "V") for s in two for g in range(NT // 2)]
        groups += [(("late", s), "V") for s in two]
        groups += [(("nT", s, k), "V") for s in two for k in range(KD)]
        groups += [((n, s, m), w) for s in two for m in range(MH) for n, w in (("g", "S"), ("a", "V"))]
        hT_first = len(groups)
        groups += [(("hT", s, k), "V") for s in two for k in range(KD)]
        groups += [(("w2", s, g), "V") for s in two for g in range(NT // 2)]
        ring = Ring(R.banks(), groups, R.sem("bank_full"), {"V": R.sem("emptied_V"), "S": R.sem("emptied_S")})

        g_in, consts, mset, tgs, vones = R.sem("g_in"), R.sem("consts"), R.sem("mask_step"), R.sem("tanh_ready"), R.sem("ones_set")
        win = {n: R.sem(f"{n}_in") for n in "wqkv wo w1 w2 small tables".split()}
        weights = (("wqkv", Wqkv), ("wo", Wo), ("w1", W1))
        w_high, w_split, w2_split = (Sig(R.sem(n), c) for n, c in (("weights_high", 3), ("weights_split", 3), ("w2_split", 4)))
        tabs = Sig(R.sem("scaled_tables"), 4)
        y_in = [Sig(R.sem(f"y_in{s}"), 16) for s in two]
        x3_in = [Sig(R.sem(f"x3_in{s}"), 16) for s in two]
        stored = [Sig(R.sem(f"stored{s}"), 32, 32) for s in two]
        h_high = Sig(R.sem("hT_high"), STREAMS * KD, STREAMS * KD)
        o_high = Sig(R.sem("oT_high"), STREAMS * PAIRS_H)
        n_high, n_low = Sig(R.sem("nT_high"), STREAMS * KD), Sig(R.sem("nT_low"), STREAMS * KD)
        hid_high, hid_low = Sig(R.sem("hidden_high"), STREAMS * MH), Sig(R.sem("hidden_low"), STREAMS * MH)
        M8 = len(TILE_UNITS)
        sq = Sig(R.sem("squares_ready"), M8)
        ssum = Sig(R.sem("square_sums"), M8)
        pstep = Sig(R.sem("pool_step"), M8 + STREAMS)
        roped = Sig(R.sem("rotated"), M8)
        rnorm = Sig(R.sem("norm_ready"), M8)
        qk = Sig(R.sem("qk_ready"), M8, M8)
        smax = Sig(R.sem("scores_ready"), U)
        probs = Sig(R.sem("probs_ready"), U)
        rd = Sig(R.sem("sums_inverted"), U)
        stat = Sig(R.sem("stats_ready"), STREAMS * NT)
        step = Sig(R.sem("vector_step"), STREAMS * 2 * NT)
        rs = Sig(R.sem("rstd_ready"), STREAMS)
        yb2 = Sig(R.sem("bias_added"), STREAMS)
        fin = Sig(R.sem("out_ready"), STREAMS)
        rows = lambda d: d.rearrange("(b t p) d -> b p t d", p=P, t=NT)
        x3b, ob = rows(K.x3_d[:, :]), A["out"].rearrange("b (t p) d -> b p t d", p=P)
        yb = rows(K.y_d[:, :])

        with nc.Block() as block:
            @block.sync
            def _(sp):
                sp.dma_start(gb[:], A["g_ffn"][1:2].partition_broadcast(P)).then_inc(g_in, 16)
                for s in two:
                    sp.dma_start(Y[s][:], yb[s]).then_inc(y_in[s].sem, 16)
                with sp.Fori(0, LAYERS) as l:
                    t0 = l * PAIRS
                    sp.wait_ge(*ring.used(t0, ("v", M8 - 1)))
                    sp.dma_start(Wqkv[2][:], A["L1_ffn_wqkv"][l].rearrange("(k p) n -> p k n", p=P)).then_inc(win["wqkv"], 16)
                    sp.wait_ge(*ring.used(t0, ("wo", STREAMS - 1, NT // 2 - 1)))
                    sp.dma_start(Wo[2][:], A["L1_ffn_wo"][l].rearrange("(k p) n -> p k n", p=P)).then_inc(win["wo"], 16)
                    sp.wait_ge(*qk.prev(t0, M8))
                    sp.dma_start(At[:], A["cos"].rearrange("(t p) c d -> p t c d", p=P)).then_inc(win["tables"], 16)
                    sp.dma_start(Bt[:], A["sin"].rearrange("(t p) c d -> p t c d", p=P)).then_inc(win["tables"], 16)
                    for c, n in enumerate(("q", "k")):
                        sp.dma_start(qks[:, c, :], A[f"L1_ffn_{n}_scale"][l].partition_broadcast(P)).then_inc(win["tables"], 16)
                    sp.wait_ge(*ring.moved_before(t0, ("a", STREAMS - 1, MH - 1)))
                    sp.dma_start(W1[2][:], A["L1_ffn_w1"][l].rearrange("(k p) n -> p k n", p=P)).then_inc(win["w1"], 16)
                    sp.dma_start(b2[:], A["L1_ffn_b2"][l].partition_broadcast(P)).then_inc(win["small"], 16)
                    for tile, name in ((lng, "g"), (lnb, "b")):
                        sp.dma_start(tile[:], A[f"L1_ffn_ln_{name}"][l].rearrange("(k p) -> p k", p=P), allow_slow_non_contiguous=True).then_inc(win["small"], 16)
                    for tile, half in ((ba, 0), (bg, 1)):
                        b1 = A["L1_ffn_b1"][l][half * HID:(half + 1) * HID]
                        sp.dma_start(tile[:, 0:MH - 1], b1[0:(MH - 1) * P].rearrange("(m p) -> p m", p=P), allow_slow_non_contiguous=True).then_inc(win["small"], 16)
                        sp.dma_start(tile[0:TAIL, MH - 1:MH], b1[(MH - 1) * P:HID].rearrange("(p m) -> p m", m=1), allow_slow_non_contiguous=True).then_inc(win["small"], 16)
                    sp.wait_ge(*ring.used(t0, ("w2", STREAMS - 1, NT // 2 - 1)))
                    w2 = A["L1_ffn_w2"][l]
                    sp.dma_start(W2[2][:, 0:MH - 1, :], w2[0:(MH - 1) * P].rearrange("(k p) n -> p k n", p=P)).then_inc(win["w2"], 16)
                    sp.dma_start(W2[2][0:TAIL, MH - 1, :], w2[(MH - 1) * P:HID]).then_inc(win["w2"], 16)
                    with sp.Fori(0, PAIRS) as p:
                        t = t0 + p
                        sp.wait_ge(*ring.ready(t, ("qkT", M8 - 1, 1)))
                        for s in two:
                            sp.dma_start(X3[s], x3b[p * STREAMS + s]).then_inc(x3_in[s].sem, 16)
                        for s in two:
                            hold(sp, K.sp_passed, *ring.moved(t, ("late", s)))
                            sp.wait_ge(*yb2.at(t, s + 1))
                            hold(sp, K.sp_passed, *stored[s].at(t, 0))
                            sp.dma_start(Y[s][:], yb[(t + 1) * STREAMS + s]).then_inc(y_in[s].sem, 16)

            @block.gpsimd
            def _(pool):
                for s in two:
                    nc.gpsimd.memset(V[s][:, :, :, LD:V1], 1.0).then_inc(vones, 1)
                    nc.gpsimd.memset(plain(HT[s][:, 1, 0:1]), 0.0).then_inc(vones, 1)
                    nc.gpsimd.memset(plain(OB[s][:, 0:1]), 0.0).then_inc(vones, 1)
                for x in (mask, shift, carry):
                    nc.gpsimd.memset(x[:], 0.0).then_inc(mset, 1)
                pool.wait_ge(mset, 3)
                nc.gpsimd.affine_select(out=mask[:, 0, :], in_=mask[:, 0, :], compare_op=ALU.is_ge, fill=FAR, base=0,
                                        pattern=[[1, P]], channel_multiplier=-1).then_inc(consts, 1)
                nc.gpsimd.affine_select(out=mask[:, 1, :], in_=mask[:, 1, :], compare_op=ALU.is_ge, fill=FAR, base=0,
                                        pattern=[[-1, P]], channel_multiplier=1).then_inc(consts, 1)
                nc.gpsimd.affine_select(out=shift[:], in_=shift[:], compare_op=ALU.not_equal, fill=1.0, base=1,
                                        pattern=[[-1, P]], channel_multiplier=1).then_inc(consts, 1)
                nc.gpsimd.affine_select(out=carry[:], in_=carry[:], compare_op=ALU.not_equal, fill=1.0, base=1 - P,
                                        pattern=[[P, P]], channel_multiplier=1).then_inc(consts, 1)
                with pool.Fori(0, LAYERS) as l:
                    pool.wait_ge(win["tables"], l * TABLES + TABLES)
                    half = LD // 2
                    tab = lambda x: x.unsqueeze(1).broadcast_to([P, NT, LD])
                    for c in range(2):
                        nc.gpsimd.tensor_tensor(At[:, :, c, :], At[:, :, c, :], tab(qks[:, c, :]), ALU.mult).then_inc(*tabs.up())
                        for a, b in ((0, half), (half, 0)):
                            ins = nc.gpsimd.tensor_tensor(Bt[:, :, c, a:a + half], Bt[:, :, c, a:a + half],
                                                          qks[:, c, b:b + half].unsqueeze(1).broadcast_to([P, NT, half]), ALU.mult)
                        ins.then_inc(*tabs.up())
                    tabs.close()
                    pool.wait_ge(win["small"], l * SMALL + SMALL)
                    hold(pool, K.pool_passed, win["w2"], l * 32 + 32)
                    parts = (slice(0, P), slice(0, MH - 1)), (slice(0, TAIL), slice(MH - 1, MH))
                    for rows2, m in parts:
                        nc.gpsimd.tensor_copy(W2[0][rows2, m, :], W2[2][rows2, m, :]).then_inc(*w2_split.up())
                    pool.wait_ge(*w2_split.now(l))
                    for rows2, m in parts:
                        nc.gpsimd.tensor_tensor(W2[1][rows2, m, :], W2[2][rows2, m, :], plain(W2[0][rows2, m, :]), ALU.subtract).then_inc(*w2_split.up())
                    w2_split.close()
                    with pool.Fori(0, PAIRS) as p:
                        t = l * PAIRS + p
                        for m in range(M8):
                            i = m % TB
                            pool.wait_ge(*ssum.at(t, m + 1))
                            nc.gpsimd.tensor_tensor(pw[i][:], ss[i][:], K.half[:, 0:2 * LH], ALU.pow).then_inc(*pstep.up())
                            hold(pool, K.pool_passed, *pstep.now(t))
                            nc.gpsimd.tensor_scalar(rn[i][:], pw[i][:], 1.0e12, None, ALU.min).then_inc(*rnorm.up())
                            pool.wait_ge(*ring.moved(t, ("k", m)))
                            nc.gpsimd.tensor_tensor(T1[i][:], T1[i][:], T2[i], ALU.add).then_inc(*roped.up())
                        for s in two:
                            pool.wait_ge(*ring.moved(t, ("wo", s, NT // 2 - 1)))
                            nc.gpsimd.tensor_tensor(O[s][:, :, D:2 * D], Y[s][:], b2[:].unsqueeze(1).broadcast_to([P, NT, D]), ALU.add).then_inc(*yb2.up())
                            hold(pool, K.pool_passed, *stat.at(t, (s + 1) * NT))
                            nc.gpsimd.tensor_scalar(vare[s][:], stats[s][:, :, 1], 1e-5, None, ALU.add).then_inc(*pstep.up())
                            pool.wait_ge(*pstep.now(t))
                            nc.gpsimd.tensor_tensor(rstd[s][:], vare[s][:], K.half[:, 0:NT], ALU.pow).then_inc(*rs.up())
                        for x in (pstep, rnorm, roped, yb2, rs):
                            x.close()

            @block.vector
            def _(v):
                def low_hT(t):
                    for s in two:
                        for k in range(KD):
                            name = ("hT", s, k)
                            v.wait_ge(*h_high.at(t, s * KD + k + 1))
                            high, low = hT(s, k)
                            nc.vector.tensor_tensor(low, ring.bank(name)[:], plain(high), ALU.subtract).then_inc(*ring.out(name))

                v.wait_ge(consts, 4)
                v.wait_ge(tgs, 1)
                credit(v, qk)
                start_ring(v, ring.emptied["V"], ring.rank[("hT", 0, 0)] - 1, lambda: low_hT(-1))
                wide = lambda x, shape: x.broadcast_to(shape)
                hf = LD // 2
                with v.Fori(0, LAYERS) as l:
                    for name, W in weights:
                        v.wait_ge(*w_high.at(l, w_split.n + 1))
                        nc.vector.tensor_tensor(W[1][:], W[2][:], plain(W[0][:]), ALU.subtract).then_inc(*w_split.up())
                    w_split.close()
                    hold(v, K.v_passed, *tabs.at(l, 4))
                    with v.Fori(0, PAIRS) as p:
                        t = l * PAIRS + p

                        def rotate(m):
                            i, s = TILE_UNITS[m]
                            b = m % TB
                            if m >= TB:
                                v.wait_ge(*ring.ready(t, ("qkT", m - TB, 1)))
                            else:
                                v.wait_ge(*stored[b].at(t, 0))
                            v.wait_ge(*sq.at(t, m + 1))
                            for c, name in enumerate(("q", "k")):
                                v.wait_ge(*ring.ready(t, (name, m)))
                                x = ring.bank((name, m))[:].rearrange("p (h d) -> p h d", h=LH)
                                heads = slice(c * LH, (c + 1) * LH)
                                nc.vector.tensor_tensor(T1[b][:, heads, :], x, wide(At[:, i, c, :].unsqueeze(1), [P, LH, LD]), ALU.mult)
                                nc.vector.tensor_tensor(T2[b][:, heads, 0:hf], x[:, :, hf:LD], wide(Bt[:, i, c, 0:hf].unsqueeze(1), [P, LH, hf]), ALU.mult)
                                nc.vector.tensor_tensor(T2[b][:, heads, hf:LD], x[:, :, 0:hf], wide(Bt[:, i, c, hf:LD].unsqueeze(1), [P, LH, hf]), ALU.mult)\
                                    .then_inc(*ring.out((name, m)))
                            nc.vector.tensor_reduce(ss[b][:], SQ[b], AX, ALU.add).then_inc(*ssum.up())

                        def scale(m):
                            b = m % TB
                            v.wait_ge(*roped.at(t, m + 1))
                            nc.vector.tensor_tensor(T1[b][:], T1[b][:], wide(rn[b][:].unsqueeze(2), [P, 2 * LH, LD]), ALU.mult).then_inc(*qk.up())

                        for m in range(M8 + 1):
                            if m < M8:
                                rotate(m)
                            if m >= 1:
                                scale(m - 1)

                        for k in range(U + VLAG):
                            if k < U:
                                for w in range(NT):
                                    name, c = ("sim", k, w // 2), w % 2
                                    if c == 0:
                                        hold(v, K.v_passed, *ring.ready(t, name))
                                    own = slice(1 if w == 0 else 0, 2)
                                    psum = ring.bank(name)[:, c * 2 * P:(c + 1) * 2 * P].rearrange("p (b j) -> p b j", b=2)
                                    ins = nc.vector.tensor_tensor_reduce(SM[k % RB][:, w, own, :], psum[:, own, :], mask[:, own, :], -1.0, 3.0e38,
                                                                         ALU.add, ALU.min, nmax[k % RB][:, w:w + 1])
                                    if c == 1:
                                        ins.then_inc(*ring.out(name))
                            if PLAG <= k < U + PLAG:
                                name = ("pT", k - PLAG, 1)
                                v.wait_ge(*ring.ready(t, name))
                                nc.vector.tensor_copy(PT[(k - PLAG) % TR][:, 2:4], ring.bank(name)[:].rearrange("p (w b j) -> p w b j", w=2, b=2)).then_inc(*ring.out(name))
                            if k >= VLAG:
                                u = k - VLAG
                                h, s = HEAD_UNITS[u]
                                v.wait_ge(*ring.ready(t, ("o", u)))
                                sums = ring.bank(("o", u))[:, 0:NT * V1].rearrange("p (w d) -> p w d", w=NT)
                                nc.vector.reciprocal(rden[u % RB][:], sums[:, :, LD]).then_inc(*rd.up())
                                v.wait_ge(*rd.now(t))
                                nc.vector.tensor_tensor(O[s][:, :, h * LD:(h + 1) * LD], sums[:, :, 0:LD], wide(rden[u % RB][:].unsqueeze(2), [P, NT, LD]), ALU.mult)\
                                    .then_inc(*ring.out(("o", u)))
                        for s in two:
                            for k in range(PAIRS_H):
                                name = ("oT", s, k)
                                v.wait_ge(*o_high.at(t, s * PAIRS_H + k + 1))
                                nc.vector.tensor_tensor(OTL[s][:, k, :], ring.bank(name)[:], plain(OT[s][:, k, :]), ALU.subtract).then_inc(*ring.out(name))
                        for s in two:
                            for g in range(NT // 2):
                                name = ("wo", s, g)
                                v.wait_ge(*ring.ready(t, name))
                                part = Y[s][:, 2 * g:2 * g + 2, :]
                                nc.vector.tensor_tensor(part, ring.bank(name)[:].rearrange("p (t d) -> p t d", t=2), part, ALU.add).then_inc(*ring.out(name))
                        for s in two:
                            later = ring.bank(("late", s))[:].rearrange("p (t d) -> p t d", t=NT)
                            v.wait_ge(*ring.ready(t, ("late", s)))
                            first = step.n
                            for i in range(NT):
                                nc.vector.bn_stats(halves[s][:, i, 0, :], Y[s][:, i, 0:P]).then_inc(*step.up())
                                nc.vector.bn_stats(halves[s][:, i, 1, :], later[:, i, :]).then_inc(*step.up())
                            hold(v, K.v_passed, *step.at(t, first + 2 * NT))
                            for i in range(NT):
                                nc.vector.bn_aggr(stats[s][:, i, :], halves[s][:, i].rearrange("p a b -> p (a b)")).then_inc(*stat.up())
                        for s in two:
                            later = ring.bank(("late", s))[:].rearrange("p (t d) -> p t d", t=NT)
                            v.wait_ge(*rs.at(t, s + 1))
                            for i in range(NT):
                                nc.vector.tensor_scalar(O[s][:, i, 0:P], Y[s][:, i, 0:P], stats[s][:, i, 0:1], rstd[s][:, i:i + 1], ALU.subtract, ALU.mult)
                                ins = nc.vector.tensor_scalar(O[s][:, i, P:D], later[:, i, :], stats[s][:, i, 0:1], rstd[s][:, i:i + 1], ALU.subtract, ALU.mult)
                            ins.then_inc(*ring.out(("late", s)))
                        for n in range(STREAMS * KD + 1):
                            if n < STREAMS * KD:
                                s, k = n // KD, n % KD
                                name = ("nT", s, k)
                                v.wait_ge(*ring.ready(t, name))
                                nc.vector.tensor_scalar(AFF(s, k), ring.bank(name)[:], lng[:, k:k + 1], lnb[:, k:k + 1], ALU.mult, ALU.add).then_inc(*ring.out(name))
                            if n:
                                s, k = (n - 1) // KD, (n - 1) % KD
                                high, low = hT(s, k)
                                v.wait_ge(*n_high.at(t, n))
                                nc.vector.tensor_tensor(low, AFF(s, k), plain(high), ALU.subtract).then_inc(*n_low.up())

                        def hidden_low(n):
                            s, m = n // MH, n % MH
                            r = P if m < MH - 1 else TAIL
                            v.wait_ge(*hid_high.at(t, n + 1))
                            nc.vector.tensor_tensor(hidden(s, m, True)[0:r, :], hidden(s, m)[0:r, :], plain(HH[s][0:r, m, :]), ALU.subtract).then_inc(*hid_low.up())

                        for n in range(STREAMS * MH):
                            s, m = n // MH, n % MH
                            r = P if m < MH - 1 else TAIL
                            v.wait_ge(*ring.ready(t, ("a", s, m)))
                            v.wait_ge(*ring.moved(t, ("g", s, m)))
                            nc.vector.scalar_tensor_tensor(out=hidden(s, m)[0:r, :], in0=ring.bank(("a", s, m))[0:r, :], scalar=ba[0:r, m:m + 1],
                                                           in1=GL[n % RB][0:r, :], op0=ALU.add, op1=ALU.mult).then_inc(*ring.out(("a", s, m)))
                            if n:
                                hidden_low(n - 1)
                        hidden_low(STREAMS * MH - 1)
                        low_hT(t)
                        for s in two:
                            v.wait_ge(*yb2.at(t, s + 1))
                            for g in range(NT // 2):
                                name, part = ("w2", s, g), slice(2 * g, 2 * g + 2)
                                v.wait_ge(*ring.ready(t, name))
                                nc.vector.tensor_tensor(Z[s][:, part, :], ring.bank(name)[:].rearrange("p (t d) -> p t d", t=2), O[s][:, part, D:2 * D], ALU.add)\
                                    .then_inc(*ring.out(name))
                            v.wait_ge(*x3_in[s].at(t, 16))
                            v.wait_ge(*ring.moved(t, ("w2", s, NT // 2 - 1)))
                            nc.vector.scalar_tensor_tensor(out=X3[s], in0=Z[s], scalar=tg[:, 0:1], in1=X3[s], op0=ALU.mult, op1=ALU.add).then_inc(*fin.up())
                        for x in (ssum, qk, rd, stat, step, fin, n_low, hid_low, ring.emptied["V"]):
                            x.close()

            @block.scalar
            def _(act):
                act.wait_ge(g_in, 16)
                nc.scalar.activation(tg[:], gb[:], ACT.Tanh).then_inc(tgs, 1)
                act.wait_ge(vones, 3 * STREAMS)
                credit(act, ring.emptied["S"], *stored)

                def high_hT(t):
                    for s in two:
                        for k in range(KD):
                            act.wait_ge(*ring.ready(t, ("hT", s, k)))
                            nc.scalar.activation(hT(s, k)[0], ring.bank(("hT", s, k))[:], ACT.Copy).then_inc(*h_high.up())
                    h_high.close()

                high_hT(-1)
                with act.Fori(0, LAYERS) as l:
                    for name, W in weights:
                        act.wait_ge(win[name], l * 16 + 16)
                        nc.scalar.activation(W[0][:], W[2][:], ACT.Copy).then_inc(*w_high.up())
                    w_high.close()
                    act.wait_ge(win["small"], l * SMALL + SMALL)
                    with act.Fori(0, PAIRS) as p:
                        t = l * PAIRS + p

                        for m in range(M8 + TLAG):
                            if m < M8:
                                i, s = TILE_UNITS[m]
                                if m >= TB:
                                    act.wait_ge(*ssum.at(t, m - TB + 1))
                                for c, name in enumerate(("q", "k")):
                                    act.wait_ge(*ring.ready(t, (name, m)))
                                    ins = nc.scalar.activation(SQ[m % TB][:, c * LH:(c + 1) * LH, :].rearrange("p h d -> p (h d)"), ring.bank((name, m))[:], ACT.Square)
                                ins.then_inc(*sq.up())
                                act.wait_ge(*ring.ready(t, ("v", m)))
                                nc.scalar.activation(V[s][:, i, :, 0:LD], ring.bank(("v", m))[:].rearrange("p (h d) -> p h d", h=LH), ACT.Copy).then_inc(*ring.out(("v", m)))
                            if m >= TLAG:
                                i, s = TILE_UNITS[m - TLAG]
                                for c in range(2):
                                    name = ("qkT", m - TLAG, c)
                                    act.wait_ge(*ring.ready(t, name))
                                    nc.scalar.activation(QKT[s][:, c * PAIRS_H:(c + 1) * PAIRS_H, i * P:(i + 1) * P],
                                                         ring.bank(name)[:].rearrange("p (h j) -> p h j", h=PAIRS_H), ACT.Copy).then_inc(*ring.out(name))
                        for k in range(U + PLAG):
                            if k < U:
                                for w in range(NT):
                                    if w % 2 == 0:
                                        act.wait_ge(*ring.moved(t, ("sim", k, w // 2)))
                                    own = slice(1 if w == 0 else 0, 2)
                                    x = SM[k % RB][:, w, own, :]
                                    ins = nc.scalar.activation(x, x, ACT.Exp, bias=nmax[k % RB][:, w:w + 1], scale=-1.0)
                                ins.then_inc(*probs.up())
                            if k >= PLAG:
                                name = ("pT", k - PLAG, 0)
                                act.wait_ge(*ring.ready(t, name))
                                part = ring.bank(name)[:, P:4 * P]
                                nc.scalar.activation(PT[(k - PLAG) % TR][:].rearrange("p w b j -> p (w b j)")[:, P:4 * P], part, ACT.Copy).then_inc(*ring.out(name))
                        for s in two:
                            for k in range(PAIRS_H):
                                act.wait_ge(*ring.ready(t, ("oT", s, k)))
                                nc.scalar.activation(OT[s][:, k, :], ring.bank(("oT", s, k))[:], ACT.Copy).then_inc(*o_high.up())
                        for s in two:
                            for k in range(KD):
                                act.wait_ge(*ring.moved(t, ("nT", s, k)))
                                nc.scalar.activation(hT(s, k)[0], AFF(s, k), ACT.Copy).then_inc(*n_high.up())

                        def hidden_high(n):
                            s, m = n // MH, n % MH
                            r = P if m < MH - 1 else TAIL
                            act.wait_ge(*ring.moved(t, ("a", s, m)))
                            nc.scalar.activation(HH[s][0:r, m, :], hidden(s, m)[0:r, :], ACT.Copy).then_inc(*hid_high.up())

                        for n in range(STREAMS * MH):
                            s, m = n // MH, n % MH
                            r = P if m < MH - 1 else TAIL
                            act.wait_ge(*ring.ready(t, ("g", s, m)))
                            if n >= RB:
                                act.wait_ge(*ring.moved(t, ("a", (n - RB) // MH, (n - RB) % MH)))
                            nc.scalar.activation(GL[n % RB][0:r, :], ring.bank(("g", s, m))[0:r, :], ACT.Gelu, bias=bg[0:r, m:m + 1])\
                                .then_inc(*ring.out(("g", s, m)))
                            if n:
                                hidden_high(n - 1)
                        hidden_high(STREAMS * MH - 1)
                        high_hT(t)
                        for s in two:
                            act.wait_ge(*ring.moved(t, ("w2", s, NT // 2 - 1)))
                            act.dma_start(yb[(t + PAIRS) * STREAMS + s], Z[s]).then_inc(stored[s].sem, 16)
                            act.wait_ge(*fin.at(t, s + 1))
                            act.dma_start(ob[p * STREAMS + s], X3[s]).then_inc(stored[s].sem, 16)
                        for x in (sq, probs, o_high, n_high, hid_high, ring.emptied["S"]):
                            x.close()
                for s in two:
                    act.wait_ge(*stored[s].at(LAYERS * PAIRS, 0))

            @block.tensor
            def _(pe):
                pe.wait_ge(consts, 4)
                pe.wait_ge(vones, 3 * STREAMS)

                def turn_y(t, fresh):
                    for s in two:
                        pe.wait_ge(*y_in[s].at(t + 1, 16))
                        for k in range(KD):
                            bank = ring.bank(("hT", s, k)) if fresh else ring.take(pe, t, ("hT", s, k))
                            for i in range(NT):
                                mm = nc.tensor.transpose(bank[:, i * P:(i + 1) * P], Y[s][:, i, k * P:(k + 1) * P], K.ident[:])
                            mm.then_inc(*ring.full.up())

                start_ring(pe, ring.full, hT_first, lambda: turn_y(-1, True))
                with pe.Fori(0, LAYERS) as l:
                    hold(pe, K.pe_passed, *w_split.at(l, 1))
                    with pe.Fori(0, PAIRS) as p:
                        t = l * PAIRS + p
                        full = lambda: ring.full.up()
                        for m in range(M8 + TLAG):
                            if m < M8:
                                i, s = TILE_UNITS[m]
                                if i == 0:
                                    pe.wait_ge(*ring.moved_before(t, ("hT", s, KD - 1)))
                                for c, name in enumerate("qkv"):
                                    bank = ring.take(pe, t, (name, m))
                                    for k in range(KD):
                                        mm = split_matmul(nc, bank[:], late(s, k, i), [x[:, k, c * INNER:(c + 1) * INNER] for x in Wqkv[0:2]],
                                                          start=(k == 0), stop=(k == KD - 1))
                                    mm.then_inc(*full())
                            if m >= TLAG:
                                u = m - TLAG
                                pe.wait_ge(*qk.at(t, u + 1))
                                for c in range(2):
                                    bank = ring.take(pe, t, ("qkT", u, c))
                                    src = T1[u % TB][:, c * LH:(c + 1) * LH, :].rearrange("p h d -> p (h d)")
                                    for g in range(PAIRS_H):
                                        mm = nc.tensor.transpose(bank[:, g * P:(g + 1) * P], src[:, g * P:(g + 1) * P], K.ident[:])
                                    mm.then_inc(*full())
                        for k in range(U + VLAG):
                            if k < U:
                                h, s = HEAD_UNITS[k]
                                if h == 0:
                                    pe.wait_ge(*ring.moved(t, ("qkT", M8 - STREAMS + s, 1)))
                                part, g = slice(h % 2 * LD, h % 2 * LD + LD), h // 2
                                for w in range(NT):
                                    if w % 2 == 0:
                                        bank = ring.take(pe, t, ("sim", k, w // 2))
                                    a = 1 if w == 0 else 0
                                    mm = nc.tensor.matmul(bank[:, (w % 2 * 2 + a) * P:(w % 2 * 2 + 2) * P], QKT[s][part, g, w * P:(w + 1) * P],
                                                          QKT[s][part, PAIRS_H + g, (w - 1 + a) * P:(w + 1) * P], start=True, stop=True)
                                    if w % 2:
                                        mm.then_inc(*full())
                            if PLAG <= k < U + PLAG:
                                u = k - PLAG
                                pe.wait_ge(*probs.at(t, u + 1))
                                for w in range(NT):
                                    if w % 2 == 0:
                                        bank = ring.take(pe, t, ("pT", u, w // 2))
                                    for a in range(1 if w == 0 else 0, 2):
                                        c = w % 2 * 2 + a
                                        mm = turned(nc, bank[:, c * P:(c + 1) * P], SM[u % RB][:, w, a, :], K.ident[:])
                                    if w % 2:
                                        mm.then_inc(*full())
                            if k >= VLAG:
                                u = k - VLAG
                                h, s = HEAD_UNITS[u]
                                pe.wait_ge(*ring.moved(t, ("pT", u, 0)))
                                pe.wait_ge(*ring.moved(t, ("pT", u, 1)))
                                bank = ring.take(pe, t, ("o", u))
                                for w in range(NT):
                                    for a in range(1 if w == 0 else 0, 2):
                                        mm = nc.tensor.matmul(bank[:, w * V1:(w + 1) * V1], PT[u % TR][:, w, a, :], V[s][:, w - 1 + a, h, :],
                                                              start=(a == 0 or w == 0), stop=(a == 1))
                                mm.then_inc(*full())
                        for s in two:
                            pe.wait_ge(*ring.moved(t, ("o", U - STREAMS + s)))
                            for k in range(PAIRS_H):
                                bank = ring.take(pe, t, ("oT", s, k))
                                for i in range(NT):
                                    mm = nc.tensor.transpose(bank[:, i * P:(i + 1) * P], O[s][:, i, k * P:(k + 1) * P], K.ident[:])
                                mm.then_inc(*full())
                        pe.wait_ge(*w_split.at(l, 2))
                        for s in two:
                            pe.wait_ge(*ring.moved(t, ("oT", s, PAIRS_H - 1)))
                            for g in range(NT // 2):
                                bank = ring.take(pe, t, ("wo", s, g))
                                for i in (2 * g, 2 * g + 1):
                                    for k in range(PAIRS_H):
                                        mm = split_matmul(nc, bank[:, i % 2 * D:(i % 2 + 1) * D], [x[s][:, k, i * P:(i + 1) * P] for x in (OT, OTL)],
                                                          [x[:, k, :] for x in Wo[0:2]], start=(k == 0), stop=(k == PAIRS_H - 1))
                                mm.then_inc(*full())
                        for s in two:
                            pe.wait_ge(*ring.moved(t, ("wo", s, NT // 2 - 1)))
                            bank = ring.take(pe, t, ("late", s))
                            for i in range(NT):
                                mm = nc.tensor.matmul(bank[:, i * P:(i + 1) * P], shift[:], Y[s][:, i, P:D], start=True, stop=(i == 0))
                                if i:
                                    mm = nc.tensor.matmul(bank[:, i * P:(i + 1) * P], carry[:], Y[s][:, i - 1, P:D], start=False, stop=True)
                            mm.then_inc(*full())
                        for s in two:
                            pe.wait_ge(*ring.moved(t, ("late", s)))
                            for k in range(KD):
                                bank = ring.take(pe, t, ("nT", s, k))
                                for i in range(NT):
                                    mm = turned(nc, bank[:, i * P:(i + 1) * P], O[s][:, i, k * P:(k + 1) * P], K.ident[:])
                                mm.then_inc(*full())
                        pe.wait_ge(*w_split.at(l, 3))
                        for s in two:
                            pe.wait_ge(*n_low.at(t, (s + 1) * KD))
                            for m in range(MH):
                                r = P if m < MH - 1 else TAIL
                                for name, at in (("g", HID), ("a", 0)):
                                    bank = ring.take(pe, t, (name, s, m))
                                    for k in range(KD):
                                        mm = split_matmul(nc, bank[0:r, :], [x[:, k, at + m * P:at + m * P + r] for x in W1[0:2]], hT(s, k),
                                                          start=(k == 0), stop=(k == KD - 1))
                                    mm.then_inc(*full())
                        turn_y(t, False)
                        pe.wait_ge(*w2_split.at(l, 4))
                        for s in two:
                            pe.wait_ge(*hid_low.at(t, (s + 1) * MH))
                            for g in range(NT // 2):
                                bank = ring.take(pe, t, ("w2", s, g))
                                for i in (2 * g, 2 * g + 1):
                                    for m in range(MH):
                                        r = P if m < MH - 1 else TAIL
                                        mm = split_matmul(nc, bank[:, i % 2 * D:(i % 2 + 1) * D],
                                                          (HH[s][0:r, m, i * P:(i + 1) * P], hidden(s, m, True)[0:r, i * P:(i + 1) * P]),
                                                          [x[0:r, m, :] for x in W2[0:2]], start=(m == 0), stop=(m == MH - 1))
                                mm.then_inc(*full())
                        ring.close_pe()


def program(nc, A):

    class K:
        keep = Store(nc, "keep")

    def scratch(name, shape, dt=FP):
        return nc.dram_tensor(name, shape, dt, kind="Internal").ap()

    K.xnT_d, K.ctxT_d = scratch("xnT", (B, P, KD, S)), scratch("ctxT", (B, P, KD, S))
    K.m_d = scratch("running_max", (B * H, S))
    K.x2_d, K.x3_d = scratch("x2", (N + CAP, D)), scratch("x3", (N, D))
    K.y_d = scratch("y", ((LAYERS + 1) * N, D))
    K.xg_d, K.slots_d = scratch("expert_rows", (N + CAP, ROW)), scratch("slots", (E_, CAP), I32)
    with K.keep.stack:
        setup(nc, A, K)
        first = Store(nc, "first")
        with nc.cleanup_on_exit(), first.stack:
            K.gates = first.sb("gates", [2, NT, B, H])
            K.acol, K.nlcol = first.sb("a_columns", [NT, B, H]), first.sb("exp_columns", [NT, B, H])
            normalize_phase(nc, A, K)
            scan_phase(nc, A, K)
            mlstm_phase(nc, A, K)
        second = Store(nc, "second")
        with second.stack:
            K.R = second.sb("priorities", [E_, B, NT])
            K.idx = second.sb("slot_tokens", [E_, SLOTS], I32)
            router_phase(nc, A, K)
            routing_phase(nc, A, K)
            expert_phase(nc, A, K)
        retrieval_phase(nc, A, K)
        layer_phase(nc, A, K)


_INS = ["x", "ctx_1024", "g_xattn", "g_ffn", "L0_xattn_ig_kernel", "L0_xattn_ig_bias", "L0_xattn_fg_kernel",
        "L0_xattn_fg_bias", "L0_xattn_outnorm_weight", "L1_ffn_wqkv", "L1_ffn_q_scale", "L1_ffn_k_scale",
        "L1_ffn_wo", "L1_ffn_ln_g", "L1_ffn_ln_b", "L1_ffn_w1", "L1_ffn_b1", "L1_ffn_w2", "L1_ffn_b2"]


def position_tables():
    f = np.float32
    half = np.arange(0, LD, 2).astype(f)
    inv_freq = f(1) / f(10000.0) ** (half / f(LD))
    pos = np.arange(S).astype(f)
    freqs = pos[:, None] * inv_freq[None]
    freqs = np.concatenate([freqs, freqs], -1)
    base = (half + f(0.4 * LD)) / f(1.4 * LD)
    scale = base[None] ** ((pos - f(S // 2)) / f(64))[:, None]
    scale = np.concatenate([scale, scale], -1)
    sign = np.where(np.arange(LD) < LD // 2, -1, 1).astype(f)
    c, s = np.cos(freqs), np.sin(freqs) * sign
    return np.stack([c * scale * f(8), c / scale], 1).astype(f), np.stack([s * scale * f(8), s / scale], 1).astype(f)


def kernel(**inputs):
    import numpy as _np
    import concourse.bacc as _bacc
    from concourse.bass_utils import run_bass_kernel_spmd as _run

    nc = _bacc.Bacc("TRN2", target_bir_lowering=False, num_devices=1)
    arrays = {name: _np.ascontiguousarray(inputs[name]) for name in _INS}
    arrays["gate_wT"] = _np.ascontiguousarray(inputs["L0_ffn_gate_w"].T)
    arrays["w1T"] = _np.ascontiguousarray(inputs["L0_ffn_w1"].transpose(0, 2, 1))
    arrays["w2T"] = _np.ascontiguousarray(inputs["L0_ffn_w2"].transpose(0, 2, 1))
    arrays["cos"], arrays["sin"] = position_tables()
    A = {n: nc.dram_tensor(n, a.shape, mybir.dt.from_np(a.dtype), kind="ExternalInput").ap() for n, a in arrays.items()}
    A["out"] = nc.dram_tensor("out", (B, S, D), FP, kind="ExternalOutput").ap()
    program(nc, A)
    return _run(nc, [arrays], core_ids=[0]).results[0]["out"]
```

```python
import concourse.bass as bass
from concourse import mybir
from contextlib import ExitStack
import numpy as np

FP = mybir.dt.float32
I32 = mybir.dt.int32
R32 = mybir.dt.float32r
ALU = mybir.AluOpType
ACT = mybir.ActivationFunctionType
AX = mybir.AxisListType.X

P = 128
B, S, D = 8, 512, 256
NT = S // P
KD = D // P
N = B * S
STREAMS = 2
PAIRS = B // STREAMS


class Sig:

    def __init__(self, sem, per, credit=0):
        self.sem, self.per, self.credit, self.n = sem, per, credit, 0

    def up(self, by=1):
        self.n += by
        return self.sem, by

    def at(self, turn, k):
        return self.sem, turn * self.per + (self.credit + k)

    def prev(self, turn, k):
        assert self.credit >= self.per and k > 0
        return self.sem, turn * self.per + (self.credit - self.per + k)

    def now(self, turn):
        return self.at(turn, self.n)

    def close(self):
        assert self.n == self.per, (self.sem.name, self.n, self.per)
        self.n = 0


class Ring:

    def __init__(self, banks, groups, full, emptied):
        self.banks, self.names = banks, [g for g, _ in groups]
        self.who = dict(groups)
        assert len(self.who) == len(groups)
        self.index = {g: i for i, g in enumerate(self.names)}
        count = {w: 0 for w in emptied}
        self.rank = {}
        for g, w in groups:
            count[w] += 1
            self.rank[g] = count[w]
        self.full = Sig(full, len(groups), len(groups))
        self.emptied = {w: Sig(emptied[w], count[w], count[w]) for w in emptied}
        self.taken = 0

    def bank(self, name):
        return self.banks[self.index[name] % 8]

    def take(self, pe, turn, name):
        i = self.index[name]
        assert i == self.taken, (name, self.names[self.taken])
        self.taken += 1
        if i >= 8:
            last, back = self.names[i - 8], 0
        else:
            last, back = self.names[max(j for j in range(len(self.names)) if j % 8 == i)], 1
        sig = self.emptied[self.who[last]]
        pe.wait_ge(sig.sem, turn * sig.per + (sig.credit - back * sig.per + self.rank[last]))
        return self.bank(name)

    def ready(self, turn, name):
        return self.full.at(turn, self.index[name] + 1)

    def used(self, turn, name):
        return self.full.prev(turn, self.index[name] + 1)

    def out(self, name):
        sig = self.emptied[self.who[name]]
        assert sig.n == self.rank[name] - 1, name
        return sig.up()

    def moved(self, turn, name):
        return self.emptied[self.who[name]].at(turn, self.rank[name])

    def moved_before(self, turn, name):
        return self.emptied[self.who[name]].prev(turn, self.rank[name])

    def close_pe(self):
        assert self.taken == len(self.names)
        self.taken = 0
        self.full.close()


def plain(ap):
    return ap.bitcast(FP)


def split_matmul(nc, out, weights, data, start, stop):
    (wh, wl), (dh, dl) = weights, data
    nc.tensor.matmul(out, wh, dh, start=start, stop=False)
    nc.tensor.matmul(out, wh, dl, start=False, stop=False)
    return nc.tensor.matmul(out, wl, dh, start=False, stop=stop)


def hold(engine, passed, sem, value):
    engine.wait_ge(sem, value)
    engine.sem_inc(passed, 1)


def credit(engine, *sigs):
    for sig in sigs:
        engine.sem_inc(sig.sem, sig.credit)
H = 4
DH = D // H


class Store:

    def __init__(self, nc, phase):
        self.nc, self.phase, self.stack, self.place = nc, phase, ExitStack(), {}

    def sb(self, name, shape, dt=FP):
        self.place[name] = -(-self.nc.sbuf_base // 32) * 32
        return self.stack.enter_context(self.nc.sbuf_tensor(f"{self.phase}_{name}", [P] + shape, dt))

    def rounded(self, name, shape):
        return self.nc.alloc_sbuf_tensor_at(f"{self.phase}_{name}_r", [P] + shape, R32, offset=self.place[name])

    def rows(self, name, shape, dt=FP):
        return self.stack.enter_context(self.nc.sbuf_tensor(f"{self.phase}_{name}", shape, dt))

    def banks(self):
        return [self.stack.enter_context(self.nc.psum_tensor(f"{self.phase}_bank{i}", [P, 512], FP)) for i in range(8)]

    def sem(self, name):
        return self.nc.alloc_semaphore(f"{self.phase}_{name}")


def tiles(ap):
    return ap.rearrange("(t p) d -> p t d", p=P)


def setup(nc, A, K):
    sem_zero, sem_ready = nc.alloc_semaphore("const_zero"), nc.alloc_semaphore("const_ready")
    K.ident = K.keep.sb("ident", [P])
    K.half = K.keep.sb("minus_half", [64])
    K.one = K.keep.sb("one", [1])
    K.v_passed, K.pool_passed, K.pe_passed, K.sp_passed = (nc.alloc_semaphore(f"{n}_waits") for n in ("vector", "pool", "tensor", "sync"))
    with nc.Block() as block:
        @block.gpsimd
        def _(pool):
            nc.gpsimd.memset(K.ident[:], 0.0).then_inc(sem_zero, 1)
            nc.gpsimd.memset(K.half[:], -0.5).then_inc(sem_ready, 1)
            nc.gpsimd.memset(K.one[:], 1.0).then_inc(sem_ready, 1)
            pool.wait_ge(sem_zero, 1)
            nc.gpsimd.affine_select(out=K.ident[:], in_=K.ident[:], compare_op=ALU.not_equal, fill=1.0,
                                    base=0, pattern=[[-1, P]], channel_multiplier=1).then_inc(sem_ready, 1)
            pool.wait_ge(sem_ready, 3)


def normalize_phase(nc, A, K):
    R = Store(nc, "nrm")
    FOUR, TURNS = 4, B // 4
    with R.stack:
        X = [R.sb(f"x{s}", [NT, D]) for s in range(FOUR)]
        C = [R.sb(f"ctx{s}", [NT, D]) for s in range(FOUR)]
        XN = [R.sb(f"xn{s}", [NT, D]) for s in range(FOUR)]
        XT = [R.sb(f"xT{s}", [KD, S]) for s in range(FOUR)]
        CT = [R.sb(f"cT{s}", [KD, S]) for s in range(FOUR)]
        halves = [R.sb(f"halves{s}", [NT, 6]) for s in range(FOUR)]
        stats = [R.sb(f"stats{s}", [NT, 2]) for s in range(FOUR)]
        vare = [R.sb(f"vare{s}", [NT]) for s in range(FOUR)]
        rstd = [R.sb(f"rstd{s}", [NT]) for s in range(FOUR)]
        kern = R.sb("kern", [3 * KD, 2, H])
        Wg = R.sb("Wg", [2 * KD, 2, H])
        bias = R.sb("bias", [2, H])
        groups = []
        for s in range(FOUR):
            groups += [(("cT", s, k), "S") for k in range(KD)]
        for s in range(FOUR):
            groups += [(("xT", s, k), "S") for k in range(KD)]
        for s in range(FOUR):
            groups += [(("gate", s), "V")]
        ring = Ring(R.banks(), groups, R.sem("bank_full"), {"V": R.sem("emptied_V"), "S": R.sem("emptied_S")})
        w_in = R.sem("weights_in")
        x_in = [Sig(R.sem(f"x_in{s}"), 16) for s in range(FOUR)]
        c_in = [Sig(R.sem(f"ctx_in{s}"), 16) for s in range(FOUR)]
        stored = [Sig(R.sem(f"stored{s}"), 32, 32) for s in range(FOUR)]
        step = Sig(R.sem("vector_step"), FOUR * NT)
        stat = Sig(R.sem("stats_ready"), FOUR * NT)
        normed = Sig(R.sem("x_normed"), FOUR * NT, FOUR * NT)
        pstep = Sig(R.sem("pool_step"), FOUR)
        rs = Sig(R.sem("rstd_ready"), FOUR)
        wg = R.sem("gate_weights")
        xb = A["x"].rearrange("b (t p) d -> b p t d", p=P)
        cb = A["ctx_1024"].rearrange("b (t p) d -> b p t d", p=P)
        with nc.Block() as block:
            @block.sync
            def _(sp):
                for i, name in enumerate(("ig", "fg")):
                    sp.dma_start(kern[:, :, i, :], A[f"L0_xattn_{name}_kernel"].rearrange("(k p) h -> p k h", p=P)).then_inc(w_in, 16)
                    sp.dma_start(bias[:, i, :], A[f"L0_xattn_{name}_bias"].partition_broadcast(P)).then_inc(w_in, 16)
                with sp.Fori(0, TURNS) as t:
                    for s in range(FOUR):
                        sp.wait_ge(*ring.used(t, ("cT", s, KD - 1)))
                        sp.dma_start(C[s][:], cb[t * FOUR + s]).then_inc(c_in[s].sem, 16)
                        sp.wait_ge(*normed.prev(t, NT * (s + 1)))
                        sp.dma_start(X[s][:], xb[t * FOUR + s]).then_inc(x_in[s].sem, 16)

            @block.vector
            def _(v):
                credit(v, normed, ring.emptied["V"])
                v.wait_ge(w_in, 64)
                nc.vector.tensor_copy(Wg[:, 0:KD], kern[:, 0:KD]).then_inc(wg, 1)
                nc.vector.tensor_tensor(Wg[:, KD:2 * KD], kern[:, KD:2 * KD], kern[:, 2 * KD:3 * KD], ALU.add).then_inc(wg, 1)
                with v.Fori(0, TURNS) as t:
                    for s in range(FOUR):
                        v.wait_ge(*x_in[s].at(t, 16))
                        for i in range(NT):
                            nc.vector.bn_stats(halves[s][:, i, :], X[s][:, i, :]).then_inc(*step.up())
                        hold(v, K.v_passed, *step.at(t, (s + 1) * NT))
                        for i in range(NT):
                            nc.vector.bn_aggr(stats[s][:, i, :], halves[s][:, i, :]).then_inc(*stat.up())
                    for s in range(FOUR):
                        v.wait_ge(*rs.at(t, s + 1))
                        for i in range(NT):
                            nc.vector.tensor_scalar(XN[s][:, i, :], X[s][:, i, :], stats[s][:, i, 0:1], rstd[s][:, i:i + 1],
                                                    ALU.subtract, ALU.mult).then_inc(*normed.up())
                    for s in range(FOUR):
                        v.wait_ge(*ring.ready(t, ("gate", s)))
                        psum = ring.bank(("gate", s))[:, 0:NT * 2 * H].rearrange("p (t g h) -> p g t h", t=NT, g=2)
                        nc.vector.tensor_tensor(K.gates[:, :, :, t * FOUR + s, :], psum,
                                                bias[:].unsqueeze(2).broadcast_to([P, 2, NT, H]), ALU.add).then_inc(*ring.out(("gate", s)))
                    step.close(), stat.close(), normed.close(), ring.emptied["V"].close()

            @block.gpsimd
            def _(pool):
                with pool.Fori(0, TURNS) as t:
                    for s in range(FOUR):
                        hold(pool, K.pool_passed, *stat.at(t, (s + 1) * NT))
                        nc.gpsimd.tensor_scalar(vare[s][:], stats[s][:, :, 1], 1e-5, None, ALU.add).then_inc(*pstep.up())
                        pool.wait_ge(*pstep.now(t))
                        nc.gpsimd.tensor_tensor(rstd[s][:], vare[s][:], K.half[:, 0:NT], ALU.pow).then_inc(*rs.up())
                    pstep.close(), rs.close()

            @block.scalar
            def _(act):
                credit(act, ring.emptied["S"], *stored)
                with act.Fori(0, TURNS) as t:
                    for name, T, scratch in (("cT", CT, K.ctxT_d), ("xT", XT, K.xnT_d)):
                        for s in range(FOUR):
                            act.wait_ge(*stored[s].at(t, 0))
                            for k in range(KD):
                                act.wait_ge(*ring.ready(t, (name, s, k)))
                                nc.scalar.activation(T[s][:, k, :], ring.bank((name, s, k))[:], ACT.Copy).then_inc(*ring.out((name, s, k)))
                    for name, T, scratch in (("cT", CT, K.ctxT_d), ("xT", XT, K.xnT_d)):
                        for s in range(FOUR):
                            act.wait_ge(*ring.moved(t, (name, s, KD - 1)))
                            act.dma_start(scratch[t * FOUR + s], T[s][:]).then_inc(stored[s].sem, 16)
                    ring.emptied["S"].close()
                for s in range(FOUR):
                    act.wait_ge(*stored[s].at(TURNS, 0))

            @block.tensor
            def _(pe):
                pe.wait_ge(wg, 2)
                credit(pe, ring.full)
                with pe.Fori(0, TURNS) as t:
                    for name, src, sig in (("cT", C, c_in), ("xT", XN, None)):
                        for s in range(FOUR):
                            if sig:
                                pe.wait_ge(*sig[s].at(t, 16))
                            else:
                                pe.wait_ge(*normed.at(t, NT * (s + 1)))
                            for k in range(KD):
                                bank = ring.take(pe, t, (name, s, k))
                                for i in range(NT):
                                    mm = nc.tensor.transpose(bank[:, i * P:(i + 1) * P], src[s][:, i, k * P:(k + 1) * P], K.ident[:])
                                mm.then_inc(*ring.full.up())
                    for s in range(FOUR):
                        pe.wait_ge(*ring.moved(t, ("xT", s, KD - 1)))
                        bank = ring.take(pe, t, ("gate", s))
                        for i in range(NT):
                            for k in range(2 * KD):
                                T = (XT if k < KD else CT)[s]
                                mm = nc.tensor.matmul(bank[:, i * 2 * H:(i + 1) * 2 * H], T[:, k % KD, i * P:(i + 1) * P],
                                                      Wg[:, k].rearrange("p g h -> p (g h)"), start=(k == 0), stop=(k == 2 * KD - 1))
                        mm.then_inc(*ring.full.up())
                    ring.close_pe()


def scan_phase(nc, A, K):
    R = Store(nc, "scan")
    BH = B * H
    with R.stack:
        row = lambda name: R.rows(name, [BH, S])
        f, nf, nabs, e, l, minf, lf, F, a, m, Fm, nl, ones = map(row, "f nf nabs e l minf lf F a m Fm nl ones".split())
        banks = R.banks()
        turned, step, sstep = R.sem("gates_turned"), Sig(R.sem("vector_step"), 0), Sig(R.sem("scalar_step"), 0)
        rows_ready, back, kept = R.sem("rows_ready"), R.sem("columns_turned"), R.sem("m_stored")
        with nc.Block() as block:
            @block.tensor
            def _(pe):
                for kind in range(2):
                    for i in range(NT):
                        mm = nc.tensor.transpose(banks[kind][0:BH, i * P:(i + 1) * P],
                                                 K.gates[:, kind, i].rearrange("p b h -> p (b h)"), K.ident[:])
                    mm.then_inc(turned, 1)
                pe.wait_ge(rows_ready, 1)
                for i in range(NT):
                    mm = nc.tensor.transpose(banks[2][:, i * BH:(i + 1) * BH], a[:, i * P:(i + 1) * P], K.ident[0:BH, 0:BH])
                mm.then_inc(back, 1)
                pe.wait_ge(rows_ready, 2)
                for i in range(NT):
                    mm = nc.tensor.transpose(banks[3][:, i * BH:(i + 1) * BH], nl[:, i * P:(i + 1) * P], K.ident[0:BH, 0:BH])
                mm.then_inc(back, 1)

            @block.vector
            def _(v):
                def then(ins):
                    ins.then_inc(*step.up())
                    v.wait_ge(*step.now(0))
                then(nc.vector.memset(ones[:], 1.0))
                v.wait_ge(turned, 2)
                then(nc.vector.tensor_copy(f[:], banks[1][0:BH, :]))
                then(nc.vector.tensor_scalar(nf[:], f[:], -1.0, None, ALU.mult))
                then(nc.vector.tensor_tensor(nabs[:], f[:], nf[:], ALU.min))
                then(nc.vector.tensor_scalar(minf[:], f[:], 0.0, None, ALU.min))
                v.wait_ge(*sstep.at(0, 2))
                then(nc.vector.tensor_tensor(lf[:], minf[:], l[:], ALU.subtract))
                then(nc.vector.tensor_tensor_scan(F[:], ones[:], lf[:], 0.0, ALU.mult, ALU.add))
                then(nc.vector.tensor_tensor(a[:], banks[0][0:BH, :], F[:], ALU.subtract))
                then(nc.vector.tensor_tensor_scan(m[:], a[:], a[:], -3.0e38, ALU.max, ALU.max))
                nc.vector.tensor_tensor(Fm[:], F[:], m[:], ALU.add).then_inc(rows_ready, 1)
                v.wait_ge(back, 1)
                nc.vector.tensor_copy(K.acol[:].rearrange("p t b h -> p (t b h)"), banks[2][:, 0:NT * BH]).then_inc(*step.up())
                v.wait_ge(back, 2)
                nc.vector.tensor_scalar(K.nlcol[:].rearrange("p t b h -> p (t b h)"), banks[3][:, 0:NT * BH], 1e-6, None, ALU.add).then_inc(*step.up())

            @block.scalar
            def _(act):
                act.wait_ge(*step.at(0, 4))
                nc.scalar.activation(e[:], nabs[:], ACT.Exp).then_inc(*sstep.up())
                act.wait_ge(*sstep.now(0))
                nc.scalar.activation(l[:], e[:], ACT.Ln, bias=K.one[0:BH, :]).then_inc(*sstep.up())
                act.wait_ge(rows_ready, 1)
                nc.scalar.activation(nl[:], Fm[:], ACT.Exp, scale=-1.0).then_inc(rows_ready, 1)

            @block.sync
            def _(sp):
                sp.wait_ge(rows_ready, 1)
                sp.dma_start(K.m_d[:, :], m[:]).then_inc(kept, 16)
                sp.wait_ge(kept, 16)


def mlstm_phase(nc, A, K):
    R = Store(nc, "mlstm")
    UNITS = [(h, s) for h in range(H) for s in range(STREAMS)]
    U, RB, LAG = len(UNITS), 4, 2
    HLAG, NLAG = LAG, LAG + 1
    W = DH + 1
    with R.stack:
        X = [R.sb(f"x{s}", [NT, D]) for s in range(STREAMS)]
        XT = [R.sb(f"xT{s}", [KD, 2, S]) for s in range(STREAMS)]
        CT = [R.sb(f"cT{s}", [KD, S]) for s in range(STREAMS)]
        VE = [R.sb(f"v{s}", [NT, H, W]) for s in range(STREAMS)]
        MB = [R.sb(f"m{s}", [H, S]) for s in range(STREAMS)]
        DT = [R.sb(f"decay{i}", [NT, S]) for i in range(RB)]
        CM = [R.sb(f"weights{i}", [NT, S]) for i in range(RB)]
        hh = [R.sb(f"hh{i}", [NT, DH]) for i in range(RB)]
        halves = [R.sb(f"halves{i}", [NT, 6]) for i in range(RB)]
        stats = [R.sb(f"stats{i}", [NT, 2]) for i in range(RB)]
        den, rden, vare, rstd = ([R.sb(f"{n}{i}", [NT]) for i in range(RB)] for n in "den rden vare rstd".split())
        gb, tg, wb, wt = R.sb("g", [2]), R.sb("tanh_g", [2]), R.sb("w", [D]), R.sb("w_tanh", [D])
        groups = []
        for k in range(U + LAG):
            if k < U:
                groups += [(("qk", k, j), "V") for j in range(3)]
            if k >= LAG:
                groups += [(("pv", k - LAG), "S")]
        ring = Ring(R.banks(), groups, R.sem("bank_full"), {"V": R.sem("scores_emptied"), "S": R.sem("sums_emptied")})
        par_in = R.sem("params_in")
        names = ("xT", "cT", "v", "m", "x")
        loaded = {n: [Sig(R.sem(f"{n}_in{s}"), {"v": 16 * NT, "xT": 32}.get(n, 16)) for s in range(STREAMS)] for n in names}
        stored = [Sig(R.sem(f"stored{s}"), 16, 16) for s in range(STREAMS)]
        ones = R.sem("ones_set")
        tgs, wts = R.sem("tanh_ready"), R.sem("w_ready")
        decay = Sig(R.sem("decay_ready"), U, U)
        masked = Sig(R.sem("decay_masked"), U)
        step = Sig(R.sem("vector_step"), U * (4 + NT + 2))
        stat = Sig(R.sem("stats_ready"), U * NT)
        pstep = Sig(R.sem("pool_step"), U)
        rs = Sig(R.sem("rstd_ready"), U)
        x1 = Sig(R.sem("x1_ready"), U)
        xb = A["x"].rearrange("b (t p) d -> b p t d", p=P)
        vb = A["ctx_1024"].rearrange("b (t p) (h d) -> b t p h d", p=P, h=H)
        mb = K.m_d[:, :].rearrange("(b h) s -> b (h s)", h=H)
        ob = K.x2_d[0:N, :].rearrange("(b t p) d -> b p t d", p=P, t=NT)
        with nc.Block() as block:
            @block.sync
            def _(sp):
                sp.dma_start(gb[:, 0:1], A["g_xattn"][0:1].partition_broadcast(P)).then_inc(par_in, 16)
                sp.dma_start(wb[:], A["L0_xattn_outnorm_weight"].rearrange("h d -> (h d)").partition_broadcast(P)).then_inc(par_in, 16)
                sp.wait_ge(ones, 3 * STREAMS)
                with sp.Fori(0, PAIRS) as t:
                    for s in range(STREAMS):
                        sp.wait_ge(*ring.used(t, ("qk", U - STREAMS + s, 2)))
                        for i in range(2):
                            rows = slice(i * DH, (i + 1) * DH)
                            sp.dma_start(XT[s][rows, :, i, :], K.xnT_d[t * STREAMS + s][rows]).then_inc(loaded["xT"][s].sem, 16)
                        sp.dma_start(CT[s][:], K.ctxT_d[t * STREAMS + s]).then_inc(loaded["cT"][s].sem, 16)
                        sp.wait_ge(*decay.prev(t, U - STREAMS + s + 1))
                        sp.dma_start(MB[s][:], mb[t * STREAMS + s].partition_broadcast(P)).then_inc(loaded["m"][s].sem, 16)
                    for s in range(STREAMS):
                        sp.wait_ge(*ring.used(t, ("pv", U - STREAMS + s)))
                        for i in range(NT):
                            sp.dma_start(VE[s][:, i, :, 0:DH], vb[t * STREAMS + s, i]).then_inc(loaded["v"][s].sem, 16)
                    for s in range(STREAMS):
                        sp.wait_ge(*stored[s].at(t, 0))
                        sp.dma_start(X[s][:], xb[t * STREAMS + s]).then_inc(loaded["x"][s].sem, 16)

            @block.scalar
            def _(act):
                act.wait_ge(par_in, 32)
                nc.scalar.activation(tg[:, 0:1], gb[:, 0:1], ACT.Tanh).then_inc(tgs, 1)
                credit(act, decay, *stored)

                def store(t):
                    for s in range(STREAMS):
                        act.wait_ge(*x1.at(t, U - STREAMS + s + 1))
                        act.dma_start(ob[t * STREAMS + s], X[s][:]).then_inc(stored[s].sem, 16)

                def turn(t, earlier):
                    for k in range(U):
                        h, s = UNITS[k]
                        if h == 0:
                            act.wait_ge(*loaded["m"][s].at(t, 16))
                        act.wait_ge(*(ring.moved(t, ("qk", k - RB, 2)) if k >= RB else ring.moved_before(t, ("qk", U + k - RB, 2))))
                        for j in range(NT):
                            bcol = K.acol[:, j, t * STREAMS + s, h:h + 1]
                            e = nc.scalar.activation(DT[k % RB][:, j, 0:S - j * P], MB[s][:, h, j * P:S], ACT.Exp, bias=bcol, scale=-1.0)
                        e.then_inc(*decay.up())
                        if earlier is not None and k == RB - 1:
                            store(earlier)
                    decay.close()

                turn(0, None)
                with act.Fori(1, PAIRS) as t:
                    turn(t, t - 1)
                store(PAIRS - 1)
                for s in range(STREAMS):
                    act.wait_ge(*stored[s].at(PAIRS, 0))

            @block.gpsimd
            def _(pool):
                for s in range(STREAMS):
                    nc.gpsimd.memset(VE[s][:, :, :, DH:W], 1.0).then_inc(ones, 1)
                with pool.Fori(0, PAIRS) as t:
                    for k in range(U + NLAG):
                        if k < U:
                            hold(pool, K.pool_passed, *decay.at(t, k + 1))
                            diag = DT[k % RB][:, :, 0:P]
                            nc.gpsimd.affine_select(out=diag, in_=diag, compare_op=ALU.is_ge, fill=0.0, base=0,
                                                    pattern=[[0, NT], [1, P]], channel_multiplier=-1).then_inc(*masked.up())
                        if k >= NLAG:
                            i = (k - NLAG) % RB
                            hold(pool, K.pool_passed, *stat.at(t, (k - NLAG + 1) * NT))
                            nc.gpsimd.tensor_scalar(vare[i][:], stats[i][:, :, 1], 1e-6, None, ALU.add).then_inc(*pstep.up())
                            pool.wait_ge(*pstep.now(t))
                            nc.gpsimd.tensor_tensor(rstd[i][:], vare[i][:], K.half[:, 0:NT], ALU.pow).then_inc(*rs.up())
                    masked.close(), pstep.close(), rs.close()

            @block.vector
            def _(v):
                for s in range(STREAMS):
                    nc.vector.memset(XT[s][DH:P, :, 0, :], 0.0).then_inc(ones, 1)
                    nc.vector.memset(XT[s][0:DH, :, 1, :], 0.0).then_inc(ones, 1)
                v.wait_ge(tgs, 1)
                nc.vector.tensor_scalar(wt[:], wb[:], tg[:, 0:1], None, ALU.mult).then_inc(wts, 1)
                v.wait_ge(wts, 1)
                credit(v, ring.emptied["V"], ring.emptied["S"])

                def then(t, ins):
                    ins.then_inc(*step.up())
                    v.wait_ge(*step.now(t))

                over = lambda x: x[:].unsqueeze(2).broadcast_to([P, NT, DH])
                with v.Fori(0, PAIRS) as t:
                    for k in range(U + NLAG):
                        if k < U:
                            v.wait_ge(*masked.at(t, k + 1))
                            for g, js in enumerate(((0,), (1, 3), (2,))):
                                v.wait_ge(*ring.ready(t, ("qk", k, g)))
                                at = 0
                                for j in js:
                                    n = S - j * P
                                    ins = nc.vector.scalar_tensor_tensor(out=CM[k % RB][:, j, 0:n], in0=ring.bank(("qk", k, g))[:, at:at + n],
                                                                         scalar=float(DH) ** -0.5, in1=DT[k % RB][:, j, 0:n],
                                                                         op0=ALU.mult, op1=ALU.mult)
                                    at += n
                                ins.then_inc(*ring.out(("qk", k, g)))
                        if HLAG <= k < U + HLAG:
                            u = k - HLAG
                            (h, s), i, name = UNITS[u], u % RB, ("pv", u)
                            v.wait_ge(*ring.ready(t, name))
                            sums = ring.bank(name)[:, 0:NT * W].rearrange("p (t w) -> p t w", t=NT)
                            then(t, nc.vector.tensor_scalar(den[i][:], sums[:, :, DH], -1.0, None, ALU.mult))
                            then(t, nc.vector.tensor_tensor(den[i][:], sums[:, :, DH], den[i][:], ALU.max))
                            then(t, nc.vector.scalar_tensor_tensor(out=den[i][:], in0=den[i][:], scalar=1e-6, in1=K.nlcol[:, :, t * STREAMS + s, h], op0=ALU.add, op1=ALU.max))
                            then(t, nc.vector.reciprocal(rden[i][:], den[i][:]))
                            nc.vector.tensor_tensor(hh[i][:], sums[:, :, 0:DH], over(rden[i]), ALU.mult).then_inc(*ring.out(name))
                            v.wait_ge(*ring.moved(t, name))
                            for j in range(NT):
                                nc.vector.bn_stats(halves[i][:, j, :], hh[i][:, j, :]).then_inc(*step.up())
                            hold(v, K.v_passed, *step.now(t))
                            for j in range(NT):
                                nc.vector.bn_aggr(stats[i][:, j, :], halves[i][:, j, :]).then_inc(*stat.up())
                        if k >= NLAG:
                            u = k - NLAG
                            (h, s), i = UNITS[u], u % RB
                            if h == 0:
                                v.wait_ge(*loaded["x"][s].at(t, 16))
                            v.wait_ge(*rs.at(t, u + 1))
                            for j in range(NT):
                                ins = nc.vector.tensor_scalar(hh[i][:, j, :], hh[i][:, j, :], stats[i][:, j, 0:1], rstd[i][:, j:j + 1], ALU.subtract, ALU.mult)
                            then(t, ins)
                            head = slice(h * DH, (h + 1) * DH)
                            then(t, nc.vector.tensor_tensor(hh[i][:], hh[i][:], wt[:, head].unsqueeze(1).broadcast_to([P, NT, DH]), ALU.mult))
                            nc.vector.tensor_tensor(X[s][:, :, head], X[s][:, :, head], hh[i][:], ALU.add).then_inc(*x1.up())
                    step.close(), stat.close(), x1.close(), ring.emptied["V"].close(), ring.emptied["S"].close()

            @block.tensor
            def _(pe):
                credit(pe, ring.full)
                pe.wait_ge(ones, 3 * STREAMS)
                with pe.Fori(0, PAIRS) as t:
                    for k in range(U + LAG):
                        scores = {("qk", k, g): ring.take(pe, t, ("qk", k, g)) for g in range(3)} if k < U else {}
                        sums = ring.take(pe, t, ("pv", k - LAG)) if k >= LAG else None
                        for g, js in enumerate(((0,), (1, 3), (2,))):
                            if k < U:
                                h, s = UNITS[k]
                                if h == 0 and g == 0:
                                    pe.wait_ge(*loaded["xT"][s].at(t, 32))
                                    pe.wait_ge(*loaded["cT"][s].at(t, 16))
                                kd = h // 2
                                at = 0
                                for j in js:
                                    n = S - j * P
                                    mm = nc.tensor.matmul(scores["qk", k, g][:, at:at + n], CT[s][:, kd, j * P:(j + 1) * P], XT[s][:, kd, h % 2, j * P:S],
                                                          start=True, stop=True)
                                    at += n
                                mm.then_inc(*ring.full.up())
                            if k >= LAG:
                                h, s = UNITS[k - LAG]
                                if g == 0:
                                    if h == 0:
                                        pe.wait_ge(*loaded["v"][s].at(t, 16 * NT))
                                    pe.wait_ge(*ring.moved(t, ("qk", k - LAG, 2)))
                                for i in ((0, 1), (2,), (3,))[g]:
                                    for j in range(i + 1):
                                        mm = nc.tensor.matmul(sums[:, i * W:(i + 1) * W], CM[(k - LAG) % RB][:, j, (i - j) * P:(i - j + 1) * P],
                                                              VE[s][:, j, h, :], start=(j == 0), stop=(j == i))
                        if k >= LAG:
                            mm.then_inc(*ring.full.up())
                    ring.close_pe()
E_ = 8
F_ = 256
KF = F_ // P
CAP = N // E_
SLOTS = CAP // P
ROW = D + E_
COLS = N // P


def layernorm_stats(nc, v, t, K, src, halves, stats, step, stat):
    first = step.n
    for i in range(NT):
        nc.vector.bn_stats(halves[:, i, :], src[:, i, :]).then_inc(*step.up())
    hold(v, K.v_passed, *step.at(t, first + NT))
    for i in range(NT):
        nc.vector.bn_aggr(stats[:, i, :], halves[:, i, :]).then_inc(*stat.up())


def rstd_on_pool(nc, pool, t, K, stats, vare, rstd, eps, stat, pstep, rs):
    hold(pool, K.pool_passed, *stat.at(t, (rs.n + 1) * NT))
    nc.gpsimd.tensor_scalar(vare[:], stats[:, :, 1], eps, None, ALU.add).then_inc(*pstep.up())
    pool.wait_ge(*pstep.now(t))
    nc.gpsimd.tensor_tensor(rstd[:], vare[:], K.half[:, 0:NT], ALU.pow).then_inc(*rs.up())


def router_phase(nc, A, K):
    R = Store(nc, "router")
    with R.stack:
        FOUR, TURNS = 4, B // 4
        streams = range(FOUR)
        X = [R.sb(f"x{s}", [NT, D]) for s in streams]
        T4 = FOUR * NT
        rows4 = R.sb("row", [T4, ROW])
        XG = [rows4[:, s * NT:(s + 1) * NT, :] for s in streams]
        XT = [R.sb(f"xT{s}", [KD, S]) for s in streams]
        halves = [R.sb(f"halves{s}", [NT, 6]) for s in streams]
        stats = [R.sb(f"stats{s}", [NT, 2]) for s in streams]
        vare, rstd = ([R.sb(f"{n}{s}", [NT]) for s in streams] for n in ("vare", "rstd"))
        lg, zz, ex, rank, prec, sel, q = (R.sb(n, [T4, E_]) for n in "logits shifted exps rank before selected priority".split())
        mx, sm, rc = (R.sb(n, [T4]) for n in "max sum inverse".split())
        gt, eq, bp = (R.sb(n, [T4, E_, E_]) for n in "greater equal before_by".split())
        gw = R.sb("gate_w", [KD, E_])
        tri = R.sb("earlier", [E_, E_])
        zero = R.sb("zero", [SLOTS, ROW])
        groups = [(("xT", s, k), "S") for s in streams for k in range(KD)] + [(("logits", s), "V") for s in streams]
        ring = Ring(R.banks(), groups, R.sem("bank_full"), {"V": R.sem("emptied_V"), "S": R.sem("emptied_S")})
        w_in, tri_ready, zeroed, dummies = R.sem("gate_in"), R.sem("tri_ready"), R.sem("zeroed"), R.sem("dummy_rows")
        x_in = [Sig(R.sem(f"x_in{s}"), 16) for s in streams]
        stored = [Sig(R.sem(f"stored{s}"), 16, 16) for s in streams]
        step = Sig(R.sem("vector_step"), FOUR * NT + 16)
        stat = Sig(R.sem("stats_ready"), FOUR * NT)
        normed = Sig(R.sem("x_normed"), FOUR * NT, FOUR * NT)
        pstep = Sig(R.sem("pool_step"), FOUR)
        rs = Sig(R.sem("rstd_ready"), FOUR)
        shifted = Sig(R.sem("logits_shifted"), 1)
        expd = Sig(R.sem("exp_ready"), 1)
        rows_ready = Sig(R.sem("rows_ready"), 1)
        xb = K.x2_d[0:N, :].rearrange("(b t p) d -> b p t d", p=P, t=NT)
        gb = K.xg_d[0:N, :].rearrange("(b t p) d -> b p t d", p=P, t=NT)
        with nc.Block() as block:
            @block.sync
            def _(sp):
                sp.dma_start(gw[:], A["gate_wT"].rearrange("(k p) e -> p k e", p=P)).then_inc(w_in, 16)
                with sp.Fori(0, TURNS) as t:
                    for s in streams:
                        sp.wait_ge(*normed.prev(t, NT * (s + 1)))
                        sp.dma_start(X[s][:], xb[t * FOUR + s]).then_inc(x_in[s].sem, 16)
                sp.wait_ge(zeroed, 1)
                sp.dma_start(K.xg_d[N:N + CAP, :].rearrange("(t p) d -> p t d", p=P), zero[:]).then_inc(dummies, 16)
                sp.dma_start(K.x2_d[N:N + CAP, :].rearrange("(t p) d -> p t d", p=P), zero[:, :, 0:D]).then_inc(dummies, 16)
                sp.wait_ge(dummies, 32)

            @block.gpsimd
            def _(pool):
                nc.gpsimd.memset(zero[:], 0.0).then_inc(zeroed, 1)
                nc.gpsimd.memset(tri[:], 1.0).then_inc(tri_ready, 1)
                pool.wait_ge(tri_ready, 1)
                nc.gpsimd.affine_select(out=tri[:], in_=tri[:], compare_op=ALU.is_gt, fill=0.0, base=0,
                                        pattern=[[1, E_], [-1, E_]], channel_multiplier=0).then_inc(tri_ready, 1)
                with pool.Fori(0, TURNS) as t:
                    for s in streams:
                        rstd_on_pool(nc, pool, t, K, stats[s], vare[s], rstd[s], 1e-5, stat, pstep, rs)
                    pstep.close(), rs.close()

            @block.vector
            def _(v):
                credit(v, normed, ring.emptied["V"])
                v.wait_ge(tri_ready, 2)

                with v.Fori(0, TURNS) as t:
                    def then(ins):
                        ins.then_inc(*step.up())
                        v.wait_ge(*step.now(t))

                    for s in streams:
                        v.wait_ge(*x_in[s].at(t, 16))
                        layernorm_stats(nc, v, t, K, X[s], halves[s], stats[s], step, stat)
                    for s in streams:
                        v.wait_ge(*rs.at(t, s + 1))
                        v.wait_ge(*stored[s].at(t, 0))
                        for i in range(NT):
                            nc.vector.tensor_scalar(XG[s][:, i, 0:D], X[s][:, i, :], stats[s][:, i, 0:1], rstd[s][:, i:i + 1],
                                                    ALU.subtract, ALU.mult).then_inc(*normed.up())
                    over = lambda x: x[:].unsqueeze(2).broadcast_to([P, T4, E_])
                    pairs = lambda x: x.broadcast_to([P, T4, E_, E_])
                    for s in streams:
                        v.wait_ge(*ring.ready(t, ("logits", s)))
                        nc.vector.tensor_copy(lg[:, s * NT:(s + 1) * NT, :], ring.bank(("logits", s))[:, 0:NT * E_].rearrange("p (t e) -> p t e", t=NT))\
                            .then_inc(*ring.out(("logits", s)))
                    v.wait_ge(*ring.moved(t, ("logits", FOUR - 1)))
                    then(nc.vector.tensor_reduce(mx[:], lg[:], AX, ALU.max))
                    nc.vector.tensor_tensor(zz[:], lg[:], over(mx), ALU.subtract).then_inc(*shifted.up())
                    v.wait_ge(*expd.at(t, 1))
                    then(nc.vector.tensor_reduce(sm[:], ex[:], AX, ALU.add))
                    then(nc.vector.reciprocal(rc[:], sm[:]))
                    prob = rows4[:, :, D:ROW]
                    nc.vector.tensor_tensor(prob, ex[:], over(rc), ALU.mult).then_inc(*rows_ready.up())
                    v.wait_ge(*rows_ready.now(t))
                    other, own = pairs(prob.unsqueeze(2)), pairs(prob.unsqueeze(3))
                    nc.vector.tensor_tensor(gt[:], other, own, ALU.is_gt).then_inc(*step.up())
                    then(nc.vector.tensor_tensor(eq[:], other, own, ALU.is_equal))
                    then(nc.vector.tensor_tensor(eq[:], eq[:], tri[:].unsqueeze(1).broadcast_to([P, T4, E_, E_]), ALU.mult))
                    then(nc.vector.tensor_tensor(gt[:], gt[:], eq[:], ALU.add))
                    nc.vector.tensor_reduce(rank[:], gt[:], AX, ALU.add).then_inc(*step.up())
                    then(nc.vector.tensor_tensor(bp[:], gt[:], other, ALU.mult))
                    then(nc.vector.tensor_reduce(prec[:], bp[:], AX, ALU.add))
                    then(nc.vector.tensor_scalar(sel[:], prec[:], 0.9, None, ALU.is_lt))
                    then(nc.vector.tensor_scalar(rank[:], rank[:], -1.0, -1.0, ALU.mult, ALU.add))
                    then(nc.vector.tensor_tensor(q[:], prob, rank[:], ALU.add))
                    then(nc.vector.tensor_tensor(q[:], q[:], sel[:], ALU.mult))
                    nc.vector.tensor_scalar(sel[:], sel[:], 1.0e9, -1.0e9, ALU.mult, ALU.add).then_inc(*step.up())
                    v.wait_ge(*step.now(t))
                    turn_R = K.R[:].rearrange("p e (g b) t -> p g (b t) e", g=TURNS)[:, t]
                    nc.vector.tensor_tensor(turn_R, q[:], sel[:], ALU.add).then_inc(*step.up())
                    step.close(), stat.close(), normed.close(), shifted.close(), rows_ready.close(), ring.emptied["V"].close()

            @block.scalar
            def _(act):
                credit(act, ring.emptied["S"], *stored)
                with act.Fori(0, TURNS) as t:
                    for s in streams:
                        for k in range(KD):
                            act.wait_ge(*ring.ready(t, ("xT", s, k)))
                            nc.scalar.activation(XT[s][:, k, :], ring.bank(("xT", s, k))[:], ACT.Copy).then_inc(*ring.out(("xT", s, k)))
                    act.wait_ge(*shifted.at(t, 1))
                    nc.scalar.activation(ex[:], zz[:], ACT.Exp).then_inc(*expd.up())
                    act.wait_ge(*rows_ready.at(t, 1))
                    for s in streams:
                        act.dma_start(gb[t * FOUR + s], XG[s]).then_inc(stored[s].sem, 16)
                    expd.close(), ring.emptied["S"].close()
                for s in streams:
                    act.wait_ge(*stored[s].at(TURNS, 0))

            @block.tensor
            def _(pe):
                credit(pe, ring.full)
                pe.wait_ge(w_in, 16)
                with pe.Fori(0, TURNS) as t:
                    for s in streams:
                        pe.wait_ge(*normed.at(t, NT * (s + 1)))
                        for k in range(KD):
                            bank = ring.take(pe, t, ("xT", s, k))
                            for i in range(NT):
                                mm = nc.tensor.transpose(bank[:, i * P:(i + 1) * P], XG[s][:, i, k * P:(k + 1) * P], K.ident[:])
                            mm.then_inc(*ring.full.up())
                    for s in streams:
                        pe.wait_ge(*ring.moved(t, ("xT", s, KD - 1)))
                        bank = ring.take(pe, t, ("logits", s))
                        for i in range(NT):
                            for k in range(KD):
                                mm = nc.tensor.matmul(bank[:, i * E_:(i + 1) * E_], XT[s][:, k, i * P:(i + 1) * P], gw[:, k, :],
                                                      start=(k == 0), stop=(k == KD - 1))
                        mm.then_inc(*ring.full.up())
                    ring.close_pe()


def routing_phase(nc, A, K):
    R = Store(nc, "route")
    BF = mybir.dt.bfloat16
    LO, HI = 32, CAP // 32
    TRY = 3
    with R.stack:
        T, cnt, ok, stepc, left, raised = (R.sb(n, [E_]) for n in "T cnt ok step left raised".split())
        Tn, ahead, cnt3, ok3 = (R.sb(n, [E_, TRY]) for n in "tried ahead counts reached".split())
        cmp3 = R.sb("at_least", [E_, TRY, COLS])
        cmp_, gtm, eqm, within, tot, M, pos, lo, hi, posf = (R.sb(n, [E_, COLS]) for n in "cmp gtm eqm within tot M pos lo hi posf".split())
        posi, hii, loi = (R.sb(n, [E_, COLS], I32) for n in "posi hii loi".split())
        keep1 = R.sb("segments", [E_, COLS])
        ones, before = R.sb("ones", [P]), R.sb("before", [P])
        hiota, liota = R.sb("hi_iota", [HI]), R.sb("lo_iota", [LO])
        ciota, piota = R.sb("col_iota", [COLS]), R.sb("part_iota", [1])
        LH = R.sb("hot_hi", [E_, COLS, 96], BF)
        RL = R.sb("hot_lo", [E_, COLS, LO], BF)
        vacant = R.rows("vacant", [HI, E_, LO])
        i1, i2, un = (R.rows(n, [HI, E_, LO]) for n in ("i1", "i2", "un"))
        slots = R.rows("slots", [HI, E_, LO], I32)
        banks = R.banks()
        const = R.sem("consts")
        step = Sig(R.sem("vector_step"), 5)
        counted = Sig(R.sem("counted"), 1)
        partial = Sig(R.sem("partial_counts"), 1)
        st2 = Sig(R.sem("tail_step"), 0)
        masks, sums = R.sem("mask_ready"), R.sem("mask_summed")
        hot, made, listed, listed_in, out_ready = R.sem("hot_ready"), R.sem("lists_made"), R.sem("list_stored"), R.sem("list_in"), R.sem("slots_ready")
        cs, cs2 = Sig(R.sem("const_step"), 0), Sig(R.sem("start_step"), 0)
        steps_on = Sig(R.sem("steps_made"), 2)
        ITER = 15
        over = lambda x: x[:].unsqueeze(2).broadcast_to([P, E_, COLS])
        flat = lambda x: x[:].rearrange("p e c -> p (e c)")
        with nc.Block() as block:
            @block.gpsimd
            def _(pool):
                nc.gpsimd.memset(ones[:], 1.0).then_inc(const, 1)
                nc.gpsimd.memset(before[:], 1.0).then_inc(*cs.up())
                pool.wait_ge(*cs.now(0))
                nc.gpsimd.affine_select(out=before[:], in_=before[:], compare_op=ALU.is_gt, fill=0.0, base=0,
                                        pattern=[[1, P]], channel_multiplier=-1).then_inc(const, 1)
                nc.gpsimd.memset(keep1[:], 1.0).then_inc(*cs.up())
                pool.wait_ge(*cs.now(0))
                nc.gpsimd.memset(keep1[:, :, 0:1], 0.0).then_inc(const, 1)
                nc.gpsimd.iota(hiota[:], [[1, HI]], 0, 0, allow_small_or_imprecise_dtypes=True).then_inc(const, 1)
                nc.gpsimd.iota(liota[:], [[1, LO]], 0, 0, allow_small_or_imprecise_dtypes=True).then_inc(const, 1)
                nc.gpsimd.iota(ciota[:], [[1, COLS]], 0, 0, allow_small_or_imprecise_dtypes=True).then_inc(const, 1)
                nc.gpsimd.iota(piota[:], [[1, 1]], 0, 1, allow_small_or_imprecise_dtypes=True).then_inc(const, 1)
                nc.gpsimd.iota(vacant[:], [[0, E_], [1, LO]], N, LO, allow_small_or_imprecise_dtypes=True).then_inc(const, 1)
                nc.gpsimd.memset(LH[:], 0.0).then_inc(const, 1)

            @block.vector
            def _(v):
                nc.vector.memset(T[:], -8.0).then_inc(*cs2.up())
                for k in range(TRY):
                    nc.vector.memset(ahead[:, :, k:k + 1], 2.0 * (k + 1)).then_inc(*cs2.up())
                v.wait_ge(*cs2.now(0))
                v.wait_ge(const, 2)
                with v.Fori(0, ITER) as t:
                    def then(ins):
                        ins.then_inc(*step.up())
                        v.wait_ge(*step.now(t))
                    then(nc.vector.tensor_tensor(Tn[:], T[:].unsqueeze(2).broadcast_to([P, E_, TRY]), ahead[:], ALU.add))
                    then(nc.vector.tensor_tensor(cmp3[:], K.R[:].rearrange("p e b t -> p e (b t)").unsqueeze(2).broadcast_to([P, E_, TRY, COLS]),
                                                 Tn[:].unsqueeze(3).broadcast_to([P, E_, TRY, COLS]), ALU.is_ge))
                    nc.vector.tensor_reduce(cnt3[:], cmp3[:], AX, ALU.add).then_inc(*partial.up())
                    nc.vector.tensor_copy(stepc[:], ahead[:, :, 0]).then_inc(*steps_on.up())
                    v.wait_ge(*steps_on.now(t))
                    nc.vector.tensor_scalar(ahead[:], ahead[:], 0.25, None, ALU.mult).then_inc(*steps_on.up())
                    v.wait_ge(*counted.at(t, 1))
                    then(nc.vector.scalar_tensor_tensor(out=ok3[:], in0=banks[0][:, 0:E_ * TRY].rearrange("p (e k) -> p e k", k=TRY), scalar=float(CAP) - 0.5,
                                                        in1=stepc[:].unsqueeze(2).broadcast_to([P, E_, TRY]), op0=ALU.is_gt, op1=ALU.mult))
                    then(nc.vector.tensor_reduce(raised[:], ok3[:], AX, ALU.add))
                    v.wait_ge(*steps_on.now(t))
                    then(nc.vector.tensor_tensor(T[:], T[:], raised[:], ALU.add))
                    step.close(), partial.close(), steps_on.close()

                def then2(ins):
                    ins.then_inc(*st2.up())
                    v.wait_ge(*st2.now(0))

                Rv = K.R[:].rearrange("p e b t -> p e (b t)")
                def prefix(base):
                    then2(nc.vector.tensor_copy(flat(tot), banks[base + 1][:, 0:E_ * COLS]))
                    then2(nc.vector.tensor_tensor_scan(flat(pos), flat(keep1), flat(tot), 0.0, ALU.mult, ALU.add))
                    then2(nc.vector.tensor_tensor(pos[:], pos[:], tot[:], ALU.subtract))
                    then2(nc.vector.tensor_tensor(flat(pos), banks[base][:, 0:E_ * COLS], flat(pos), ALU.add))

                v.wait_ge(const, 9)
                then2(nc.vector.tensor_tensor(gtm[:], Rv, over(T), ALU.is_gt))
                nc.vector.tensor_tensor(eqm[:], Rv, over(T), ALU.is_equal).then_inc(masks, 1)
                then2(nc.vector.tensor_reduce(cnt[:], gtm[:], AX, ALU.add))
                nc.vector.tensor_copy(ok[:], cnt[:]).then_inc(masks, 1)
                v.wait_ge(sums, 1)
                prefix(1)
                v.wait_ge(sums, 2)
                then2(nc.vector.tensor_scalar(left[:], banks[0][:, 0:E_], -1.0, float(CAP), ALU.mult, ALU.add))
                then2(nc.vector.tensor_tensor(M[:], pos[:], over(left), ALU.is_lt))
                then2(nc.vector.tensor_tensor(M[:], M[:], eqm[:], ALU.mult))
                nc.vector.tensor_tensor(M[:], M[:], gtm[:], ALU.add).then_inc(masks, 1)
                v.wait_ge(masks, 3)
                v.wait_ge(sums, 3)
                prefix(3)
                then2(nc.vector.tensor_copy(posi[:], pos[:]))
                then2(nc.vector.tensor_scalar(hii[:], posi[:], 5, None, ALU.arith_shift_right))
                then2(nc.vector.tensor_scalar(loi[:], posi[:], LO - 1, None, ALU.bitwise_and))
                then2(nc.vector.tensor_copy(hi[:], hii[:]))
                then2(nc.vector.tensor_copy(lo[:], loi[:]))
                then2(nc.vector.tensor_scalar(cmp_[:], M[:], 1000.0, -1000.0, ALU.mult, ALU.add))
                then2(nc.vector.tensor_tensor(hi[:], hi[:], cmp_[:], ALU.add))
                for e in range(E_):
                    wide = lambda x, n: x[:, e, :].unsqueeze(2).broadcast_to([P, COLS, n])
                    hot_hi = LH[:, e, :, 0:HI]
                    nc.vector.tensor_tensor(RL[:, e], wide(lo, LO), liota[:].unsqueeze(1).broadcast_to([P, COLS, LO]), ALU.is_equal).then_inc(*st2.up())
                    then2(nc.vector.tensor_tensor(hot_hi, wide(hi, HI), hiota[:].unsqueeze(1).broadcast_to([P, COLS, HI]), ALU.is_equal))
                    nc.vector.tensor_scalar(LH[:, e, :, 32:32 + HI], hot_hi, piota[:, 0:1], None, ALU.mult).then_inc(*st2.up())
                    nc.vector.tensor_tensor(LH[:, e, :, 64:64 + HI], hot_hi, ciota[:].unsqueeze(2).broadcast_to([P, COLS, HI]), ALU.mult).then_inc(hot, 1)
                v.wait_ge(made, 1)
                L = banks[5]
                fl = lambda x: x[:].rearrange("p e l -> p (e l)")
                then2(nc.vector.tensor_scalar(fl(i1), L[64:64 + HI, 0:E_ * LO], float(P), None, ALU.mult))
                then2(nc.vector.tensor_tensor(fl(i2), L[32:32 + HI, 0:E_ * LO], fl(i1), ALU.add))
                then2(nc.vector.tensor_scalar(fl(un), L[0:HI, 0:E_ * LO], -1.0, 1.0, ALU.mult, ALU.add))
                then2(nc.vector.tensor_tensor(un[:], un[:], vacant[:], ALU.mult))
                nc.vector.tensor_tensor(slots[:], i2[:], un[:], ALU.add).then_inc(out_ready, 1)

            @block.tensor
            def _(pe):
                pe.wait_ge(const, 2)
                with pe.Fori(0, ITER) as t:
                    pe.wait_ge(*partial.at(t, 1))
                    nc.tensor.matmul(banks[0][:, 0:E_ * TRY], ones[:], cnt3[:].rearrange("p e k -> p (e k)"), start=True, stop=True).then_inc(*counted.up())
                    counted.close()
                pe.wait_ge(masks, 1)
                nc.tensor.matmul(banks[1][:, 0:E_ * COLS], before[:], flat(eqm), start=True, stop=True)
                nc.tensor.matmul(banks[2][:, 0:E_ * COLS], ones[:], flat(eqm), start=True, stop=True).then_inc(sums, 1)
                pe.wait_ge(masks, 2)
                nc.tensor.matmul(banks[0][:, 0:E_], ones[:], ok[:], start=True, stop=True).then_inc(sums, 1)
                pe.wait_ge(masks, 3)
                nc.tensor.matmul(banks[3][:, 0:E_ * COLS], before[:], flat(M), start=True, stop=True)
                nc.tensor.matmul(banks[4][:, 0:E_ * COLS], ones[:], flat(M), start=True, stop=True).then_inc(sums, 1)
                for e in range(E_):
                    pe.wait_ge(hot, e + 1)
                    for c in range(COLS):
                        mm = nc.tensor.matmul(banks[5][0:96, e * LO:(e + 1) * LO], LH[:, e, c, :], RL[:, e, c, :],
                                              start=(c == 0), stop=(c == COLS - 1))
                mm.then_inc(made, 1)

            @block.sync
            def _(sp):
                sp.wait_ge(out_ready, 1)
                sp.dma_start(K.slots_d[:, :].rearrange("e (h l) -> h e l", h=HI), slots[:]).then_inc(listed, 16)
                sp.wait_ge(listed, 16)
                sp.dma_start(K.idx[:], K.slots_d[:, :].rearrange("e (t p) -> p e t", p=P), allow_slow_non_contiguous=True).then_inc(listed_in, 16)
                sp.wait_ge(listed_in, 16)


def expert_phase(nc, A, K):
    R = Store(nc, "expert")
    FOUR = 4
    TURNS = E_ // FOUR
    with R.stack:
        streams = range(FOUR)
        W1 = [R.sb(f"w1{s}", [KD, F_]) for s in streams]
        W2 = [R.sb(f"w2{s}", [KF, D]) for s in streams]
        GX = [R.sb(f"rows{s}", [SLOTS, ROW]) for s in streams]
        XT = [R.sb(f"xT{s}", [KD, CAP]) for s in streams]
        HT = [R.sb(f"hT{s}", [KF, CAP]) for s in streams]
        Y = [R.sb(f"y{s}", [SLOTS, D]) for s in streams]
        sc = [R.sb(f"share{s}", [SLOTS]) for s in streams]
        ig, ia = ([R.sb(f"{n}{s}", [SLOTS], I32) for s in streams] for n in ("gather_idx", "add_idx"))
        gb, tg = R.sb("g", [1]), R.sb("tanh_g", [1])
        STEPS = FOUR + 2
        has = lambda s: 0 <= s < FOUR
        groups = []
        for k in range(STEPS):
            groups += [(("xT", k, i), "S") for i in range(KD) if has(k)]
            groups += [(("hT", k - 1, i), "S") for i in range(KF) if has(k - 1)]
            groups += [(("y", k - 2, i), "V") for i in range(SLOTS // 2) if has(k - 2)]
        ring = Ring(R.banks(), groups, R.sem("bank_full"), {"V": R.sem("emptied_V"), "S": R.sem("emptied_S")})
        g_in, tgs = R.sem("g_in"), R.sem("tanh_ready")
        w_in = [Sig(R.sem(f"weights_in{s}"), 32) for s in streams]
        copied, copied2 = Sig(R.sem("gather_idx_copied"), FOUR), Sig(R.sem("add_idx_copied"), FOUR)
        rows_in = [Sig(R.sem(f"rows_in{s}"), 16 * SLOTS) for s in streams]
        share = Sig(R.sem("share_ready"), FOUR)
        added = [Sig(R.sem(f"rows_added{s}"), 16 * SLOTS) for s in streams]
        y_free = Sig(R.sem("y_free"), FOUR, FOUR)
        w1 = A["w1T"].rearrange("e (k p) f -> e p k f", p=P)
        w2 = A["w2T"].rearrange("e (k p) d -> e p k d", p=P)
        with nc.Block() as block:
            @block.sync
            def _(sp):
                sp.dma_start(gb[:], A["g_ffn"][0:1].partition_broadcast(P)).then_inc(g_in, 16)
                with sp.Fori(0, TURNS) as t:
                    for s in streams:
                        sp.wait_ge(*ring.used(t, ("y", s, SLOTS // 2 - 1)))
                        sp.dma_start(W1[s][:], w1[t * FOUR + s]).then_inc(w_in[s].sem, 16)
                        sp.dma_start(W2[s][:], w2[t * FOUR + s]).then_inc(w_in[s].sem, 16)

            @block.gpsimd
            def _(pool):
                def add_rows(t, s):
                    nc.gpsimd.tensor_copy(ia[s][:], K.idx[:, t * FOUR + s, :]).then_inc(copied2.sem, 1)
                    hold(pool, K.pool_passed, *copied2.at(t, s + 1))
                    for i in range(SLOTS):
                        hold(pool, K.pool_passed, *ring.moved(t, ("y", s, i // 2)))
                        pool.indirect_dma_start(K.x2_d[:, :], bass.IndirectOffsetOnAxis(ap=ia[s][:, i:i + 1], axis=0),
                                                Y[s][:, i, :], None, compute_op=ALU.add).then_inc(added[s].sem, 16)

                def rows_added(t, s):
                    pool.wait_ge(*added[s].at(t, 16 * SLOTS))
                    pool.sem_inc(y_free.sem, 1)

                def gather(t, s):
                    nc.gpsimd.tensor_copy(ig[s][:], K.idx[:, t * FOUR + s, :]).then_inc(copied.sem, 1)
                    hold(pool, K.pool_passed, *copied.at(t, s + 1))
                    for i in range(SLOTS):
                        pool.indirect_dma_start(GX[s][:, i, :], None, K.xg_d[:, :],
                                                bass.IndirectOffsetOnAxis(ap=ig[s][:, i:i + 1], axis=0)).then_inc(rows_in[s].sem, 16)

                credit(pool, y_free)
                for s in streams:
                    gather(0, s)
                with pool.Fori(1, TURNS) as t:
                    for s in streams:
                        add_rows(t - 1, s)
                        hold(pool, K.pool_passed, *rows_in[s].at(t, 0))
                        hold(pool, K.pool_passed, *ring.used(t, ("xT", s, KD - 1)))
                        hold(pool, K.pool_passed, *share.at(t, s - FOUR + 1))
                        gather(t, s)
                        rows_added(t - 1, s)
                for s in streams:
                    add_rows(TURNS - 1, s)
                    rows_added(TURNS - 1, s)

            @block.scalar
            def _(act):
                act.wait_ge(g_in, 16)
                nc.scalar.activation(tg[:], gb[:], ACT.Tanh).then_inc(tgs, 1)
                credit(act, ring.emptied["S"])
                with act.Fori(0, TURNS) as t:
                    for step in range(STEPS):
                        if has(step):
                            for k in range(KD):
                                name = ("xT", step, k)
                                act.wait_ge(*ring.ready(t, name))
                                nc.scalar.activation(XT[step][:, k, :], ring.bank(name)[:], ACT.Copy).then_inc(*ring.out(name))
                        if has(step - 1):
                            for m in range(KF):
                                name = ("hT", step - 1, m)
                                act.wait_ge(*ring.ready(t, name))
                                nc.scalar.activation(HT[step - 1][:, m, :], ring.bank(name)[:], ACT.Gelu).then_inc(*ring.out(name))
                    ring.emptied["S"].close()

            @block.vector
            def _(v):
                credit(v, ring.emptied["V"])
                v.wait_ge(tgs, 1)
                with v.Fori(0, TURNS) as t:
                    v.wait_ge(*ring.moved_before(t, ("y", FOUR - 1, SLOTS // 2 - 1)))
                    for step in range(STEPS):
                        if has(step):
                            s = step
                            v.wait_ge(*rows_in[s].at(t, 16 * SLOTS))
                            nc.vector.tensor_scalar(sc[s][:], GX[s][:, :, D + t * FOUR + s], tg[:, 0:1], None, ALU.mult).then_inc(*share.up())
                        if has(step - 2):
                            s = step - 2
                            v.wait_ge(*share.at(t, s + 1))
                            v.wait_ge(*y_free.prev(t, s + 1))
                            for i in range(SLOTS):
                                name = ("y", s, i // 2)
                                if i % 2 == 0:
                                    v.wait_ge(*ring.ready(t, name))
                                ins = nc.vector.tensor_scalar(Y[s][:, i, :], ring.bank(name)[:, i % 2 * D:(i % 2 + 1) * D], sc[s][:, i:i + 1], None, ALU.mult)
                                if i % 2:
                                    ins.then_inc(*ring.out(name))
                    share.close(), ring.emptied["V"].close()

            @block.tensor
            def _(pe):
                credit(pe, ring.full)
                with pe.Fori(0, TURNS) as t:
                    for step in range(STEPS):
                        if has(step):
                            s = step
                            pe.wait_ge(*rows_in[s].at(t, 16 * SLOTS))
                            for k in range(KD):
                                bank = ring.take(pe, t, ("xT", s, k))
                                for i in range(SLOTS):
                                    mm = nc.tensor.transpose(bank[:, i * P:(i + 1) * P], GX[s][:, i, k * P:(k + 1) * P], K.ident[:])
                                mm.then_inc(*ring.full.up())
                        if has(step - 1):
                            s = step - 1
                            pe.wait_ge(*w_in[s].at(t, 32))
                            pe.wait_ge(*ring.moved(t, ("xT", s, KD - 1)))
                            for m in range(KF):
                                bank = ring.take(pe, t, ("hT", s, m))
                                for k in range(KD):
                                    mm = nc.tensor.matmul(bank[:], W1[s][:, k, m * P:(m + 1) * P], XT[s][:, k, :], start=(k == 0), stop=(k == KD - 1))
                                mm.then_inc(*ring.full.up())
                        if has(step - 2):
                            s = step - 2
                            pe.wait_ge(*ring.moved(t, ("hT", s, KF - 1)))
                            for g in range(SLOTS // 2):
                                bank = ring.take(pe, t, ("y", s, g))
                                for i in range(2):
                                    for m in range(KF):
                                        mm = nc.tensor.matmul(bank[:, i * D:(i + 1) * D], HT[s][:, m, (2 * g + i) * P:(2 * g + i + 1) * P], W2[s][:, m, :],
                                                              start=(m == 0), stop=(m == KF - 1))
                                mm.then_inc(*ring.full.up())
                    ring.close_pe()


def retrieval_phase(nc, A, K):
    R = Store(nc, "retr")
    FOUR, TURNS = 4, B // 4
    streams = range(FOUR)
    PARTS = ((0,), (1, 3), (2,))
    with R.stack:
        X, Q, C, ST, Z = ([R.sb(f"{n}{s}", shape) for s in streams] for n, shape in
                          (("x", [NT, D]), ("q", [NT, D]), ("cT", [KD, S]), ("scores", [NT, S]), ("y", [NT, D])))
        halves = [R.sb(f"halves{s}", [NT, 6]) for s in streams]
        stats = [R.sb(f"stats{s}", [NT, 2]) for s in streams]
        vare, rstd = ([R.sb(f"{n}{s}", [NT]) for s in streams] for n in ("vare", "rstd"))
        gb, tg = R.sb("g", [1]), R.sb("tanh_g", [1])
        groups = [(("s", s, j), "S") for s in streams for j in range(len(PARTS))] + [(("p", s, g), "V") for s in streams for g in range(NT // 2)]
        ring = Ring(R.banks(), groups, R.sem("bank_full"), {"V": R.sem("emptied_V"), "S": R.sem("emptied_S")})
        g_in, tgs = R.sem("g_in"), R.sem("tanh_ready")
        x_in = [Sig(R.sem(f"x_in{s}"), 16) for s in streams]
        c_in = [Sig(R.sem(f"ctx_in{s}"), 16) for s in streams]
        stored = [Sig(R.sem(f"stored{s}"), 32, 32) for s in streams]
        step = Sig(R.sem("vector_step"), FOUR * 2 * NT)
        stat = Sig(R.sem("stats_ready"), 2 * FOUR * NT)
        normed = Sig(R.sem("x_normed"), FOUR)
        masked = Sig(R.sem("scores_masked"), FOUR)
        x3 = Sig(R.sem("x3_ready"), FOUR)
        y0 = Sig(R.sem("y_ready"), FOUR)
        pstep = Sig(R.sem("pool_step"), 2 * FOUR)
        rs = Sig(R.sem("rstd_ready"), 2 * FOUR)
        rows = lambda d: d.rearrange("(b t p) d -> b p t d", p=P, t=NT)
        xb, x3b, yb = rows(K.x2_d[0:N, :]), rows(K.x3_d[:, :]), rows(K.y_d[0:N, :])
        with nc.Block() as block:
            @block.sync
            def _(sp):
                sp.dma_start(gb[:], A["g_xattn"][1:2].partition_broadcast(P)).then_inc(g_in, 16)
                with sp.Fori(0, TURNS) as t:
                    for s in streams:
                        sp.wait_ge(*ring.used(t, ("s", s, 2)))
                        sp.dma_start(C[s][:], K.ctxT_d[t * FOUR + s]).then_inc(c_in[s].sem, 16)
                        sp.wait_ge(*stored[s].at(t, 0))
                        sp.dma_start(X[s][:], xb[t * FOUR + s]).then_inc(x_in[s].sem, 16)

            @block.gpsimd
            def _(pool):
                with pool.Fori(0, TURNS) as t:
                    for s in streams:
                        rstd_on_pool(nc, pool, t, K, stats[s], vare[s], rstd[s], 1e-5, stat, pstep, rs)
                    for s in streams:
                        hold(pool, K.pool_passed, *ring.moved(t, ("s", s, 2)))
                        diag = ST[s][:, :, 0:P]
                        nc.gpsimd.affine_select(out=diag, in_=diag, compare_op=ALU.is_ge, fill=0.0, base=0,
                                                pattern=[[0, NT], [1, P]], channel_multiplier=-1).then_inc(*masked.up())
                    for s in streams:
                        rstd_on_pool(nc, pool, t, K, stats[s], vare[s], rstd[s], 1e-5, stat, pstep, rs)
                    pstep.close(), rs.close(), masked.close()

            @block.vector
            def _(v):
                credit(v, ring.emptied["V"])
                v.wait_ge(tgs, 1)
                with v.Fori(0, TURNS) as t:
                    for s in streams:
                        v.wait_ge(*x_in[s].at(t, 16))
                        layernorm_stats(nc, v, t, K, X[s], halves[s], stats[s], step, stat)
                    for s in streams:
                        v.wait_ge(*rs.at(t, s + 1))
                        for i in range(NT):
                            ins = nc.vector.tensor_scalar(Q[s][:, i, :], X[s][:, i, :], stats[s][:, i, 0:1], rstd[s][:, i:i + 1], ALU.subtract, ALU.mult)
                        ins.then_inc(*normed.up())
                    for s in streams:
                        v.wait_ge(*stored[s].at(t, 0))
                        for g in range(NT // 2):
                            name, rows2 = ("p", s, g), slice(2 * g, 2 * g + 2)
                            v.wait_ge(*ring.ready(t, name))
                            psum = ring.bank(name)[:].rearrange("p (t d) -> p t d", t=2)
                            nc.vector.tensor_tensor(Z[s][:, rows2, :], psum, Q[s][:, rows2, :], ALU.add).then_inc(*ring.out(name))
                        v.wait_ge(*ring.moved(t, ("p", s, NT // 2 - 1)))
                        nc.vector.scalar_tensor_tensor(out=X[s][:], in0=Z[s][:], scalar=tg[:, 0:1], in1=X[s][:], op0=ALU.mult, op1=ALU.add).then_inc(*x3.up())
                        v.wait_ge(*x3.now(t))
                        layernorm_stats(nc, v, t, K, X[s], halves[s], stats[s], step, stat)
                    for s in streams:
                        v.wait_ge(*rs.at(t, FOUR + s + 1))
                        for i in range(NT):
                            ins = nc.vector.tensor_scalar(Z[s][:, i, :], X[s][:, i, :], stats[s][:, i, 0:1], rstd[s][:, i:i + 1], ALU.subtract, ALU.mult)
                        ins.then_inc(*y0.up())
                    step.close(), stat.close(), normed.close(), x3.close(), y0.close(), ring.emptied["V"].close()

            @block.scalar
            def _(act):
                act.wait_ge(g_in, 16)
                nc.scalar.activation(tg[:], gb[:], ACT.Tanh).then_inc(tgs, 1)
                credit(act, ring.emptied["S"], *stored)
                with act.Fori(0, TURNS) as t:
                    for s in streams:
                        for g, js in enumerate(PARTS):
                            act.wait_ge(*ring.ready(t, ("s", s, g)))
                            at = 0
                            for j in js:
                                n = S - j * P
                                ins = nc.scalar.activation(ST[s][:, j, 0:n], ring.bank(("s", s, g))[:, at:at + n], ACT.Copy)
                                at += n
                            ins.then_inc(*ring.out(("s", s, g)))
                    for s in streams:
                        act.wait_ge(*x3.at(t, s + 1))
                        act.dma_start(x3b[t * FOUR + s], X[s][:]).then_inc(stored[s].sem, 16)
                        act.wait_ge(*y0.at(t, s + 1))
                        act.dma_start(yb[t * FOUR + s], Z[s][:]).then_inc(stored[s].sem, 16)
                    ring.emptied["S"].close()
                for s in streams:
                    act.wait_ge(*stored[s].at(TURNS, 0))

            @block.tensor
            def _(pe):
                credit(pe, ring.full)
                with pe.Fori(0, TURNS) as t:
                    for s in streams:
                        pe.wait_ge(*c_in[s].at(t, 16))
                        for g, js in enumerate(PARTS):
                            bank = ring.take(pe, t, ("s", s, g))
                            at = 0
                            for j in js:
                                n = S - j * P
                                for k in range(KD):
                                    mm = nc.tensor.matmul(bank[:, at:at + n], C[s][:, k, j * P:(j + 1) * P], C[s][:, k, j * P:S], start=(k == 0), stop=(k == KD - 1))
                                at += n
                            mm.then_inc(*ring.full.up())
                    for s in streams:
                        pe.wait_ge(*normed.at(t, s + 1))
                        pe.wait_ge(*masked.at(t, s + 1))
                        for g in range(NT // 2):
                            bank = ring.take(pe, t, ("p", s, g))
                            for i in (2 * g, 2 * g + 1):
                                for j in range(i + 1):
                                    mm = nc.tensor.matmul(bank[:, i % 2 * D:(i % 2 + 1) * D], ST[s][:, j, (i - j) * P:(i - j + 1) * P], Q[s][:, j, :],
                                                          start=(j == 0), stop=(j == i))
                            mm.then_inc(*ring.full.up())
                    ring.close_pe()
LAYERS = 2
LH = 8
LD = 64
INNER = LH * LD
HID = 682
MH = -(-HID // P)
TAIL = HID - (MH - 1) * P
PAIRS_H = INNER // P
SMALL, TABLES = 16 * 7, 16 * 4
FAR = -3.0e38


def start_ring(engine, sig, before, work):
    engine.sem_inc(sig.sem, before)
    sig.n = before
    work()
    engine.wait_ge(sig.sem, sig.n)
    engine.sem_inc(sig.sem, sig.per - sig.n)
    sig.n = 0


def layer_phase(nc, A, K):
    R = Store(nc, "layer")
    two = range(STREAMS)
    TILE_UNITS = [(i, s) for s in two for i in range(NT)]
    HEAD_UNITS = [(h, s) for s in two for h in range(LH)]
    TURN_AT = {1: len(TILE_UNITS) - 2, 2: len(TILE_UNITS) - 1}
    OT_AT, WO_AT, LATE_AT, NORM_AT, NT_AT = 12, 13, 15, 16, 18
    HIDDEN_PARTS = (0,), (1,), (2, 3), (4, 5)
    U, V1 = len(HEAD_UNITS), LD + 1
    TLAG, PLAG, VLAG, RB, TR, TB = 2, 2, 4, 4, 3, 2
    with R.stack:
        weight = lambda n, shape: [R.sb(f"{n}_high", shape, R32), R.sb(f"{n}_low", shape)]
        Wqkv, Wo, W1, W2 = (weight(n, shape) for n, shape in (("wqkv", [KD, 3 * INNER]), ("wo", [PAIRS_H, D]), ("w1", [KD, 2 * HID]), ("w2", [MH, D])))
        Wqkv, Wo, W1, W2 = ((x[0], R.rounded(f"{n}_low", list(x[1].shape[1:])), x[1]) for n, x in (("wqkv", Wqkv), ("wo", Wo), ("w1", W1), ("w2", W2)))
        ba, bg, b2 = R.sb("b1_a", [MH]), R.sb("b1_g", [MH]), R.sb("b2", [D])
        lng, lnb = R.sb("ln_g", [KD]), R.sb("ln_b", [KD])
        qks = R.sb("qk_scale", [2, LD])
        At, Bt = R.sb("along", [NT, 2, LD]), R.sb("across", [NT, 2, LD])
        gb, tg = R.sb("g", [1]), R.sb("tanh_g", [1])
        mask = R.sb("mask", [2, P])
        shift, carry = R.sb("shift", [P]), R.sb("carry", [P])
        Y = [R.sb(f"y{s}", [NT, D]) for s in two]
        HT = [R.sb(f"hT{s}", [KD, S + 1], R32) for s in two]
        V = [R.sb(f"v{s}", [NT, LH, V1]) for s in two]
        QKT = [R.sb(f"qkT{s}", [2 * PAIRS_H, S]) for s in two]
        O = [R.sb(f"o{s}", [NT, INNER]) for s in two]
        OB = [R.sb(f"oT{s}", [2 + PAIRS_H * S], R32) for s in two]
        T1 = [R.sb(f"along_t{i}", [2 * LH, LD]) for i in range(TB)]
        ss, norm, rn = ([R.sb(f"{n}{i}", [2 * LH]) for i in range(TB)] for n in ("ss", "norm", "rn"))
        SM, PT = ([R.sb(f"{n}{i}", [NT, 2, P]) for i in range(c)] for n, c in (("scores", RB), ("probsT", TR)))
        nmax, rden = ([R.sb(f"{n}{i}", [NT]) for i in range(RB)] for n in ("nmax", "rden"))
        halves = [R.sb(f"halves{s}", [NT, 2, 6]) for s in two]
        stats = [R.sb(f"stats{s}", [NT, 2]) for s in two]
        vare, rstd = ([R.sb(f"{n}{s}", [NT]) for s in two] for n in ("vare", "rstd"))

        flat3 = lambda x: x[:].rearrange("p w b j -> p (w b j)")
        SQ, T2 = ([flat3(x).rearrange("p (h d) -> p h d", d=LD) for x in part] for part in (SM[0:TB], SM[TB:2 * TB]))
        GL = [flat3(SM[i // 2])[:, i % 2 * S:(i % 2 + 1) * S] for i in range(RB)]
        X3 = [x[:].rearrange("p (t a) d -> p t (a d)", t=NT) for x in T1]
        Z = [x[:, :, 0:D] for x in O]
        OT = [x[:, 2:2 + PAIRS_H * S].rearrange("p (k n) -> p k n", n=S) for x in OB]
        QKR = [R.rounded(f"qkT{s}", [2 * PAIRS_H, S]) for s in two]
        OTL = [x[:, 0:PAIRS_H, :] for x in QKR]
        HH = [x[:, 0:MH, :] for x in QKR]
        SPARE = [flat3(x) for x in PT[0:3] + SM[2:3]]
        SPARER = [flat3(R.rounded(n, [NT, 2, P])) for n in ("probsT0", "probsT1", "probsT2", "scores2")]
        AFF = lambda s, k: SPARE[2 + k][:, 0:S] if s else flat3(SM[3])[:, k * S:(k + 1) * S]

        def hidden(s, m, low=False):
            if m < 2:
                return (QKR if low else QKT)[s][:, MH + m, :]
            return (SPARER if low else SPARE)[2 * s + (m - 2) // 2][:, m % 2 * S:(m % 2 + 1) * S]

        def hT(s, k, at=0, n=S):
            low = OB[s][:, 1 + at:1 + at + n] if k else OB[s][:, S + 2 + at:S + 2 + at + n]
            return HT[s][:, k, k + at:k + at + n], low

        def late(s, k, i):
            return hT(s, k, i * P - k, P)

        groups = []
        oT_groups = lambda s: [(("oT", s, k), "V") for k in range(PAIRS_H)]
        wo_groups = lambda s: [(("wo", s, g), "V") for g in range(NT // 2)]
        nT_groups = lambda s: [(("nT", s, k), "V") for k in range(KD)]
        hidden_groups = lambda s, ms: [((n, s, m), w) for m in ms for n, w in (("g", "S"), ("a", "V"))]
        for m in range(len(TILE_UNITS)):
            groups += [(("q", m), "V"), (("k", m), "V"), (("v", m), "S")]
            if m >= TLAG:
                groups += [(("qkT", m - TLAG, c), "S") for c in range(2)]
        for k in range(U + VLAG):
            if k < U:
                groups += [(("sim", k, g), "V") for g in range(NT // 2)]
            if k in TURN_AT:
                groups += [(("qkT", TURN_AT[k], c), "S") for c in range(2)]
            if PLAG <= k < U + PLAG:
                groups += [(("pT", k - PLAG, 0), "S"), (("pT", k - PLAG, 1), "V")]
            if k >= VLAG:
                groups += [(("o", k - VLAG), "V")]
            if k == OT_AT:
                groups += oT_groups(0)
            if k == WO_AT:
                groups += wo_groups(0)
            if k == LATE_AT:
                groups += [(("late", 0), "late")]
            if k == NT_AT:
                groups += nT_groups(0)
        groups += oT_groups(1)
        groups += hidden_groups(0, HIDDEN_PARTS[0]) + wo_groups(1)
        groups += hidden_groups(0, HIDDEN_PARTS[1]) + [(("late", 1), "late")]
        w2_groups = lambda s: [(("w2", s, g), "V") for g in range(NT // 2)]
        groups += hidden_groups(0, HIDDEN_PARTS[2] + HIDDEN_PARTS[3]) + nT_groups(1) + w2_groups(0) + hidden_groups(1, range(MH))
        hT_first = len(groups)
        groups += [(("hT", s, k), "V") for s in two for k in range(KD)]
        groups += w2_groups(1)
        ring = Ring(R.banks(), groups, R.sem("bank_full"), {"V": R.sem("emptied_V"), "S": R.sem("emptied_S"), "late": R.sem("late_emptied")})

        g_in, consts, mset, tgs, vones = R.sem("g_in"), R.sem("consts"), R.sem("mask_step"), R.sem("tanh_ready"), R.sem("ones_set")
        win = {n: R.sem(f"{n}_in") for n in "wqkv wo w1 w2 small tables".split()}
        weights = (("wqkv", Wqkv), ("wo", Wo), ("w1", W1))
        w_high, w_split, w2_split = (Sig(R.sem(n), c) for n, c in (("weights_high", 3), ("weights_split", 3), ("w2_split", 4)))
        tabs = Sig(R.sem("scaled_tables"), 4)
        y_in = [Sig(R.sem(f"y_in{s}"), 16) for s in two]
        x3_in = [Sig(R.sem(f"x3_in{s}"), 16) for s in two]
        stored = [Sig(R.sem(f"stored{s}"), 32, 32) for s in two]
        h_high = Sig(R.sem("hT_high"), STREAMS * KD, STREAMS * KD)
        o_high = Sig(R.sem("oT_high"), STREAMS * PAIRS_H)
        n_high, n_low = Sig(R.sem("nT_high"), STREAMS * KD), Sig(R.sem("nT_low"), STREAMS * KD)
        hid_high, hid_low = Sig(R.sem("hidden_high"), STREAMS * MH), Sig(R.sem("hidden_low"), STREAMS * MH)
        M8 = len(TILE_UNITS)
        sq = Sig(R.sem("squares_ready"), M8)
        ssum = Sig(R.sem("square_sums"), M8)
        pstep = Sig(R.sem("pool_step"), STREAMS)
        root = Sig(R.sem("norms"), M8)
        clipped = Sig(R.sem("norms_clipped"), M8)
        roped = Sig(R.sem("rotated"), M8)
        rnorm = Sig(R.sem("norm_ready"), M8)
        q_ready, k_ready = Sig(R.sem("q_ready"), M8, M8), Sig(R.sem("k_ready"), M8)
        smax = Sig(R.sem("scores_ready"), U)
        probs = Sig(R.sem("probs_ready"), U)
        rd = Sig(R.sem("sums_inverted"), U)
        stat = Sig(R.sem("stats_ready"), STREAMS * NT)
        step = Sig(R.sem("vector_step"), STREAMS * 2 * NT)
        rs = Sig(R.sem("rstd_ready"), STREAMS)
        yb2 = Sig(R.sem("bias_added"), STREAMS)
        fin = Sig(R.sem("out_ready"), STREAMS)
        rows = lambda d: d.rearrange("(b t p) d -> b p t d", p=P, t=NT)
        x3b, ob = rows(K.x3_d[:, :]), A["out"].rearrange("b (t p) d -> b p t d", p=P)
        yb = rows(K.y_d[:, :])

        with nc.Block() as block:
            @block.sync
            def _(sp):
                sp.dma_start(gb[:], A["g_ffn"][1:2].partition_broadcast(P)).then_inc(g_in, 16)
                for s in two:
                    sp.dma_start(Y[s][:], yb[s]).then_inc(y_in[s].sem, 16)
                with sp.Fori(0, LAYERS) as l:
                    t0 = l * PAIRS
                    sp.wait_ge(*ring.used(t0, ("v", M8 - 1)))
                    sp.dma_start(Wqkv[2][:], A["L1_ffn_wqkv"][l].rearrange("(k p) n -> p k n", p=P)).then_inc(win["wqkv"], 16)
                    sp.wait_ge(*ring.used(t0, ("wo", STREAMS - 1, NT // 2 - 1)))
                    sp.dma_start(Wo[2][:], A["L1_ffn_wo"][l].rearrange("(k p) n -> p k n", p=P)).then_inc(win["wo"], 16)
                    sp.wait_ge(*q_ready.prev(t0, M8))
                    sp.dma_start(At[:], A["cos"].rearrange("(t p) c d -> p t c d", p=P)).then_inc(win["tables"], 16)
                    sp.dma_start(Bt[:], A["sin"].rearrange("(t p) c d -> p t c d", p=P)).then_inc(win["tables"], 16)
                    for c, n in enumerate(("q", "k")):
                        sp.dma_start(qks[:, c, :], A[f"L1_ffn_{n}_scale"][l].partition_broadcast(P)).then_inc(win["tables"], 16)
                    sp.wait_ge(*ring.moved_before(t0, ("a", STREAMS - 1, MH - 1)))
                    sp.dma_start(W1[2][:], A["L1_ffn_w1"][l].rearrange("(k p) n -> p k n", p=P)).then_inc(win["w1"], 16)
                    sp.dma_start(b2[:], A["L1_ffn_b2"][l].partition_broadcast(P)).then_inc(win["small"], 16)
                    for tile, name in ((lng, "g"), (lnb, "b")):
                        sp.dma_start(tile[:], A[f"L1_ffn_ln_{name}"][l].rearrange("(k p) -> p k", p=P), allow_slow_non_contiguous=True).then_inc(win["small"], 16)
                    for tile, half in ((ba, 0), (bg, 1)):
                        b1 = A["L1_ffn_b1"][l][half * HID:(half + 1) * HID]
                        sp.dma_start(tile[:, 0:MH - 1], b1[0:(MH - 1) * P].rearrange("(m p) -> p m", p=P), allow_slow_non_contiguous=True).then_inc(win["small"], 16)
                        sp.dma_start(tile[0:TAIL, MH - 1:MH], b1[(MH - 1) * P:HID].rearrange("(p m) -> p m", m=1), allow_slow_non_contiguous=True).then_inc(win["small"], 16)
                    sp.wait_ge(*ring.used(t0, ("w2", STREAMS - 1, NT // 2 - 1)))
                    w2 = A["L1_ffn_w2"][l]
                    sp.dma_start(W2[2][:, 0:MH - 1, :], w2[0:(MH - 1) * P].rearrange("(k p) n -> p k n", p=P)).then_inc(win["w2"], 16)
                    sp.dma_start(W2[2][0:TAIL, MH - 1, :], w2[(MH - 1) * P:HID]).then_inc(win["w2"], 16)
                    with sp.Fori(0, PAIRS) as p:
                        t = t0 + p
                        sp.wait_ge(*ring.ready(t, ("qkT", M8 - 1, 1)))
                        for s in two:
                            sp.dma_start(X3[s], x3b[p * STREAMS + s]).then_inc(x3_in[s].sem, 16)
                        for s in two:
                            hold(sp, K.sp_passed, *ring.moved(t, ("late", s)))
                            sp.wait_ge(*yb2.at(t, s + 1))
                            hold(sp, K.sp_passed, *stored[s].at(t, 0))
                            sp.dma_start(Y[s][:], yb[(t + 1) * STREAMS + s]).then_inc(y_in[s].sem, 16)

            @block.gpsimd
            def _(pool):
                for s in two:
                    nc.gpsimd.memset(V[s][:, :, :, LD:V1], 1.0).then_inc(vones, 1)
                    nc.gpsimd.memset(plain(HT[s][:, 1, 0:1]), 0.0).then_inc(vones, 1)
                    nc.gpsimd.memset(plain(OB[s][:, 0:1]), 0.0).then_inc(vones, 1)
                for x in (mask, shift, carry):
                    nc.gpsimd.memset(x[:], 0.0).then_inc(mset, 1)
                pool.wait_ge(mset, 3)
                nc.gpsimd.affine_select(out=mask[:, 0, :], in_=mask[:, 0, :], compare_op=ALU.is_ge, fill=FAR, base=0,
                                        pattern=[[1, P]], channel_multiplier=-1).then_inc(consts, 1)
                nc.gpsimd.affine_select(out=mask[:, 1, :], in_=mask[:, 1, :], compare_op=ALU.is_ge, fill=FAR, base=0,
                                        pattern=[[-1, P]], channel_multiplier=1).then_inc(consts, 1)
                nc.gpsimd.affine_select(out=shift[:], in_=shift[:], compare_op=ALU.not_equal, fill=1.0, base=1,
                                        pattern=[[-1, P]], channel_multiplier=1).then_inc(consts, 1)
                nc.gpsimd.affine_select(out=carry[:], in_=carry[:], compare_op=ALU.not_equal, fill=1.0, base=1 - P,
                                        pattern=[[P, P]], channel_multiplier=1).then_inc(consts, 1)
                with pool.Fori(0, LAYERS) as l:
                    pool.wait_ge(win["tables"], l * TABLES + TABLES)
                    half = LD // 2
                    tab = lambda x: x.unsqueeze(1).broadcast_to([P, NT, LD])
                    for c in range(2):
                        nc.gpsimd.tensor_tensor(At[:, :, c, :], At[:, :, c, :], tab(qks[:, c, :]), ALU.mult).then_inc(*tabs.up())
                        for a, b in ((0, half), (half, 0)):
                            ins = nc.gpsimd.tensor_tensor(Bt[:, :, c, a:a + half], Bt[:, :, c, a:a + half],
                                                          qks[:, c, b:b + half].unsqueeze(1).broadcast_to([P, NT, half]), ALU.mult)
                        ins.then_inc(*tabs.up())
                    tabs.close()
                    pool.wait_ge(win["small"], l * SMALL + SMALL)
                    hold(pool, K.pool_passed, win["w2"], l * 32 + 32)
                    parts = (slice(0, P), slice(0, MH - 1)), (slice(0, TAIL), slice(MH - 1, MH))
                    for rows2, m in parts:
                        nc.gpsimd.tensor_copy(W2[0][rows2, m, :], W2[2][rows2, m, :]).then_inc(*w2_split.up())
                    pool.wait_ge(*w2_split.now(l))
                    for rows2, m in parts:
                        nc.gpsimd.tensor_tensor(W2[1][rows2, m, :], W2[2][rows2, m, :], plain(W2[0][rows2, m, :]), ALU.subtract).then_inc(*w2_split.up())
                    w2_split.close()
                    with pool.Fori(0, PAIRS) as p:
                        t = l * PAIRS + p
                        for m in range(M8):
                            i = m % TB
                            pool.wait_ge(*ring.moved(t, ("k", m)))
                            nc.gpsimd.tensor_tensor(T1[i][:], T1[i][:], T2[i], ALU.add).then_inc(*roped.up())
                            pool.wait_ge(*roped.now(t))
                            pool.wait_ge(*rnorm.at(t, m + 1))
                            keys = T1[i][:, LH:2 * LH, :]
                            nc.gpsimd.tensor_tensor(keys, keys, rn[i][:, LH:2 * LH].unsqueeze(2).broadcast_to([P, LH, LD]), ALU.mult).then_inc(*k_ready.up())
                        for s in two:
                            pool.wait_ge(*ring.moved(t, ("wo", s, NT // 2 - 1)))
                            nc.gpsimd.tensor_tensor(O[s][:, :, D:2 * D], Y[s][:], b2[:].unsqueeze(1).broadcast_to([P, NT, D]), ALU.add).then_inc(*yb2.up())
                            hold(pool, K.pool_passed, *stat.at(t, (s + 1) * NT))
                            nc.gpsimd.tensor_scalar(vare[s][:], stats[s][:, :, 1], 1e-5, None, ALU.add).then_inc(*pstep.up())
                            pool.wait_ge(*pstep.now(t))
                            nc.gpsimd.tensor_tensor(rstd[s][:], vare[s][:], K.half[:, 0:NT], ALU.pow).then_inc(*rs.up())
                        for x in (pstep, k_ready, roped, yb2, rs):
                            x.close()

            @block.vector
            def _(v):
                def low_hT(t):
                    for s in two:
                        for k in range(KD):
                            name = ("hT", s, k)
                            v.wait_ge(*h_high.at(t, s * KD + k + 1))
                            high, low = hT(s, k)
                            nc.vector.tensor_tensor(low, ring.bank(name)[:], plain(high), ALU.subtract).then_inc(*ring.out(name))

                v.wait_ge(consts, 4)
                v.wait_ge(tgs, 1)
                credit(v, q_ready, ring.emptied["late"])
                start_ring(v, ring.emptied["V"], ring.rank[("hT", 0, 0)] - 1, lambda: low_hT(-1))
                wide = lambda x, shape: x.broadcast_to(shape)
                hf = LD // 2
                with v.Fori(0, LAYERS) as l:
                    for name, W in weights:
                        v.wait_ge(*w_high.at(l, w_split.n + 1))
                        nc.vector.tensor_tensor(W[1][:], W[2][:], plain(W[0][:]), ALU.subtract).then_inc(*w_split.up())
                    w_split.close()
                    hold(v, K.v_passed, *tabs.at(l, 4))
                    with v.Fori(0, PAIRS) as p:
                        t = l * PAIRS + p

                        def rotate(m, c):
                            (i, s), b, name = TILE_UNITS[m], m % TB, (("q", "k")[c], m)
                            v.wait_ge(*ring.ready(t, name))
                            x = ring.bank(name)[:].rearrange("p (h d) -> p h d", h=LH)
                            heads = slice(c * LH, (c + 1) * LH)
                            nc.vector.tensor_tensor(T1[b][:, heads, :], x, wide(At[:, i, c, :].unsqueeze(1), [P, LH, LD]), ALU.mult)
                            nc.vector.tensor_tensor(T2[b][:, heads, 0:hf], x[:, :, hf:LD], wide(Bt[:, i, c, 0:hf].unsqueeze(1), [P, LH, hf]), ALU.mult)
                            nc.vector.tensor_tensor(T2[b][:, heads, hf:LD], x[:, :, 0:hf], wide(Bt[:, i, c, hf:LD].unsqueeze(1), [P, LH, hf]), ALU.mult)\
                                .then_inc(*ring.out(name))

                        def invert(m):
                            b = m % TB
                            v.wait_ge(*root.at(t, m + 1))
                            nc.vector.tensor_scalar(norm[b][:], norm[b][:], 1.0e-12, None, ALU.max).then_inc(*clipped.up())
                            v.wait_ge(*clipped.now(t))
                            nc.vector.reciprocal(rn[b][:], norm[b][:]).then_inc(*rnorm.up())

                        def scale_queries(m):
                            b = m % TB
                            queries = T1[b][:, 0:LH, :]
                            v.wait_ge(*rnorm.at(t, m + 1))
                            v.wait_ge(*roped.at(t, m + 1))
                            nc.vector.tensor_tensor(queries, queries, wide(rn[b][:, 0:LH].unsqueeze(2), [P, LH, LD]), ALU.mult).then_inc(*q_ready.up())

                        for m in range(M8):
                            b = m % TB
                            if m >= TB:
                                v.wait_ge(*ring.ready(t, ("qkT", m - TB, 1)))
                            else:
                                v.wait_ge(*stored[b].at(t, 0))
                            v.wait_ge(*sq.at(t, m + 1))
                            rotate(m, 0)
                            if m >= 1:
                                invert(m - 1)
                            rotate(m, 1)
                            if m >= 1:
                                scale_queries(m - 1)
                            nc.vector.tensor_reduce(ss[b][:], SQ[b], AX, ALU.add).then_inc(*ssum.up())
                        invert(M8 - 1)

                        def low_oT(s):
                            for k in range(PAIRS_H):
                                name = ("oT", s, k)
                                v.wait_ge(*o_high.at(t, s * PAIRS_H + k + 1))
                                nc.vector.tensor_tensor(OTL[s][:, k, :], ring.bank(name)[:], plain(OT[s][:, k, :]), ALU.subtract).then_inc(*ring.out(name))

                        def add_wo(s):
                            for g in range(NT // 2):
                                name = ("wo", s, g)
                                v.wait_ge(*ring.ready(t, name))
                                part = Y[s][:, 2 * g:2 * g + 2, :]
                                nc.vector.tensor_tensor(part, ring.bank(name)[:].rearrange("p (t d) -> p t d", t=2), part, ALU.add).then_inc(*ring.out(name))

                        def later(s):
                            return ring.bank(("late", s))[:].rearrange("p (t d) -> p t d", t=NT)

                        def stats_of(s):
                            v.wait_ge(*ring.ready(t, ("late", s)))
                            first = step.n
                            for i in range(NT):
                                nc.vector.bn_stats(halves[s][:, i, 0, :], Y[s][:, i, 0:P]).then_inc(*step.up())
                                nc.vector.bn_stats(halves[s][:, i, 1, :], later(s)[:, i, :]).then_inc(*step.up())
                            hold(v, K.v_passed, *step.at(t, first + 2 * NT))
                            for i in range(NT):
                                nc.vector.bn_aggr(stats[s][:, i, :], halves[s][:, i].rearrange("p a b -> p (a b)")).then_inc(*stat.up())

                        def normalize(s):
                            v.wait_ge(*rs.at(t, s + 1))
                            for i in range(NT):
                                nc.vector.tensor_scalar(O[s][:, i, 0:P], Y[s][:, i, 0:P], stats[s][:, i, 0:1], rstd[s][:, i:i + 1], ALU.subtract, ALU.mult)
                                ins = nc.vector.tensor_scalar(O[s][:, i, P:D], later(s)[:, i, :], stats[s][:, i, 0:1], rstd[s][:, i:i + 1], ALU.subtract, ALU.mult)
                            ins.then_inc(*ring.out(("late", s)))

                        def affine(s):
                            for k in range(KD):
                                name = ("nT", s, k)
                                v.wait_ge(*ring.ready(t, name))
                                nc.vector.tensor_scalar(AFF(s, k), ring.bank(name)[:], lng[:, k:k + 1], lnb[:, k:k + 1], ALU.mult, ALU.add).then_inc(*ring.out(name))

                        def low_nT(s):
                            for k in range(KD):
                                high, low = hT(s, k)
                                v.wait_ge(*n_high.at(t, s * KD + k + 1))
                                nc.vector.tensor_tensor(low, AFF(s, k), plain(high), ALU.subtract).then_inc(*n_low.up())

                        hold(v, K.v_passed, *ssum.at(t, M8))
                        for k in range(U + VLAG):
                            if k < U:
                                for w in range(NT):
                                    name, c = ("sim", k, w // 2), w % 2
                                    if c == 0:
                                        hold(v, K.v_passed, *ring.ready(t, name))
                                    own = slice(1 if w == 0 else 0, 2)
                                    psum = ring.bank(name)[:, c * 2 * P:(c + 1) * 2 * P].rearrange("p (b j) -> p b j", b=2)
                                    ins = nc.vector.tensor_tensor_reduce(SM[k % RB][:, w, own, :], psum[:, own, :], mask[:, own, :], -1.0, 3.0e38,
                                                                         ALU.add, ALU.min, nmax[k % RB][:, w:w + 1])
                                    if c == 1:
                                        ins.then_inc(*ring.out(name))
                            if PLAG <= k < U + PLAG:
                                name = ("pT", k - PLAG, 1)
                                v.wait_ge(*ring.ready(t, name))
                                nc.vector.tensor_copy(PT[(k - PLAG) % TR][:, 2:4], ring.bank(name)[:].rearrange("p (w b j) -> p w b j", w=2, b=2)).then_inc(*ring.out(name))
                            if k >= VLAG:
                                u = k - VLAG
                                h, s = HEAD_UNITS[u]
                                v.wait_ge(*ring.ready(t, ("o", u)))
                                sums = ring.bank(("o", u))[:, 0:NT * V1].rearrange("p (w d) -> p w d", w=NT)
                                nc.vector.reciprocal(rden[u % RB][:], sums[:, :, LD]).then_inc(*rd.up())
                                v.wait_ge(*rd.now(t))
                                nc.vector.tensor_tensor(O[s][:, :, h * LD:(h + 1) * LD], sums[:, :, 0:LD], wide(rden[u % RB][:].unsqueeze(2), [P, NT, LD]), ALU.mult)\
                                    .then_inc(*ring.out(("o", u)))
                            if k == 0:
                                scale_queries(M8 - 1)
                            if k == OT_AT:
                                low_oT(0)
                            if k == WO_AT:
                                add_wo(0)
                            if k == LATE_AT:
                                stats_of(0)
                            if k == NORM_AT:
                                normalize(0)
                            if k == NT_AT:
                                affine(0)
                        low_nT(0)
                        low_oT(1)

                        def hidden_low(n):
                            s, m = n // MH, n % MH
                            r = P if m < MH - 1 else TAIL
                            v.wait_ge(*hid_high.at(t, n + 1))
                            nc.vector.tensor_tensor(hidden(s, m, True)[0:r, :], hidden(s, m)[0:r, :], plain(HH[s][0:r, m, :]), ALU.subtract).then_inc(*hid_low.up())

                        def hidden_whole(n):
                            s, m = n // MH, n % MH
                            r = P if m < MH - 1 else TAIL
                            v.wait_ge(*ring.ready(t, ("a", s, m)))
                            v.wait_ge(*ring.moved(t, ("g", s, m)))
                            nc.vector.scalar_tensor_tensor(out=hidden(s, m)[0:r, :], in0=ring.bank(("a", s, m))[0:r, :], scalar=ba[0:r, m:m + 1],
                                                           in1=GL[n % RB][0:r, :], op0=ALU.add, op1=ALU.mult).then_inc(*ring.out(("a", s, m)))
                            if n % MH:
                                hidden_low(n - 1)

                        def new_y(s):
                            v.wait_ge(*yb2.at(t, s + 1))
                            for g in range(NT // 2):
                                name, part = ("w2", s, g), slice(2 * g, 2 * g + 2)
                                v.wait_ge(*ring.ready(t, name))
                                nc.vector.tensor_tensor(Z[s][:, part, :], ring.bank(name)[:].rearrange("p (t d) -> p t d", t=2), O[s][:, part, D:2 * D], ALU.add)\
                                    .then_inc(*ring.out(name))
                            v.wait_ge(*x3_in[s].at(t, 16))
                            v.wait_ge(*ring.moved(t, ("w2", s, NT // 2 - 1)))
                            nc.vector.scalar_tensor_tensor(out=X3[s], in0=Z[s], scalar=tg[:, 0:1], in1=X3[s], op0=ALU.mult, op1=ALU.add).then_inc(*fin.up())

                        for m in HIDDEN_PARTS[0]:
                            hidden_whole(m)
                        add_wo(1)
                        for m in HIDDEN_PARTS[1]:
                            hidden_whole(m)
                        stats_of(1)
                        for m in HIDDEN_PARTS[2]:
                            hidden_whole(m)
                        normalize(1)
                        for m in HIDDEN_PARTS[3]:
                            hidden_whole(m)
                        hidden_low(MH - 1)
                        affine(1)
                        low_nT(1)
                        new_y(0)
                        for m in range(MH):
                            hidden_whole(MH + m)
                        hidden_low(STREAMS * MH - 1)
                        low_hT(t)
                        new_y(1)
                        for x in (ssum, clipped, rnorm, q_ready, rd, stat, step, fin, n_low, hid_low, ring.emptied["V"], ring.emptied["late"]):
                            x.close()

            @block.scalar
            def _(act):
                act.wait_ge(g_in, 16)
                nc.scalar.activation(tg[:], gb[:], ACT.Tanh).then_inc(tgs, 1)
                act.wait_ge(vones, 3 * STREAMS)
                credit(act, ring.emptied["S"], *stored)

                def high_hT(t):
                    for s in two:
                        for k in range(KD):
                            act.wait_ge(*ring.ready(t, ("hT", s, k)))
                            nc.scalar.activation(hT(s, k)[0], ring.bank(("hT", s, k))[:], ACT.Copy).then_inc(*h_high.up())
                    h_high.close()

                high_hT(-1)
                with act.Fori(0, LAYERS) as l:
                    for name, W in weights:
                        act.wait_ge(win[name], l * 16 + 16)
                        nc.scalar.activation(W[0][:], W[2][:], ACT.Copy).then_inc(*w_high.up())
                    w_high.close()
                    act.wait_ge(win["small"], l * SMALL + SMALL)
                    with act.Fori(0, PAIRS) as p:
                        t = l * PAIRS + p

                        def roots(m):
                            act.wait_ge(*ssum.at(t, m + 1))
                            nc.scalar.activation(norm[m % TB][:], ss[m % TB][:], ACT.Sqrt).then_inc(*root.up())

                        def turned_heads(u):
                            i, s = TILE_UNITS[u]
                            for c in range(2):
                                name = ("qkT", u, c)
                                act.wait_ge(*ring.ready(t, name))
                                nc.scalar.activation(QKT[s][:, c * PAIRS_H:(c + 1) * PAIRS_H, i * P:(i + 1) * P],
                                                     ring.bank(name)[:].rearrange("p (h j) -> p h j", h=PAIRS_H), ACT.Copy).then_inc(*ring.out(name))

                        def high_oT(s):
                            for k in range(PAIRS_H):
                                act.wait_ge(*ring.ready(t, ("oT", s, k)))
                                nc.scalar.activation(OT[s][:, k, :], ring.bank(("oT", s, k))[:], ACT.Copy).then_inc(*o_high.up())

                        def high_nT(s):
                            for k in range(KD):
                                act.wait_ge(*ring.moved(t, ("nT", s, k)))
                                nc.scalar.activation(hT(s, k)[0], AFF(s, k), ACT.Copy).then_inc(*n_high.up())

                        for m in range(M8):
                            i, s = TILE_UNITS[m]
                            if m >= TB:
                                act.wait_ge(*ssum.at(t, m - TB + 1))
                            for c, name in enumerate(("q", "k")):
                                act.wait_ge(*ring.ready(t, (name, m)))
                                ins = nc.scalar.activation(SQ[m % TB][:, c * LH:(c + 1) * LH, :].rearrange("p h d -> p (h d)"), ring.bank((name, m))[:], ACT.Square)
                            ins.then_inc(*sq.up())
                            if m >= 1:
                                roots(m - 1)
                            act.wait_ge(*ring.ready(t, ("v", m)))
                            nc.scalar.activation(V[s][:, i, :, 0:LD], ring.bank(("v", m))[:].rearrange("p (h d) -> p h d", h=LH), ACT.Copy).then_inc(*ring.out(("v", m)))
                            if m >= TLAG:
                                turned_heads(m - TLAG)
                        roots(M8 - 1)
                        for k in range(U + PLAG):
                            if k < U:
                                for w in range(NT):
                                    if w % 2 == 0:
                                        act.wait_ge(*ring.moved(t, ("sim", k, w // 2)))
                                    own = slice(1 if w == 0 else 0, 2)
                                    x = SM[k % RB][:, w, own, :]
                                    ins = nc.scalar.activation(x, x, ACT.Exp, bias=nmax[k % RB][:, w:w + 1], scale=-1.0)
                                ins.then_inc(*probs.up())
                            if k in TURN_AT:
                                turned_heads(TURN_AT[k])
                            if k >= PLAG:
                                name = ("pT", k - PLAG, 0)
                                act.wait_ge(*ring.ready(t, name))
                                part = ring.bank(name)[:, P:4 * P]
                                nc.scalar.activation(PT[(k - PLAG) % TR][:].rearrange("p w b j -> p (w b j)")[:, P:4 * P], part, ACT.Copy).then_inc(*ring.out(name))
                            if k == OT_AT:
                                high_oT(0)
                        high_nT(0)
                        high_oT(1)

                        def hidden_high(n):
                            s, m = n // MH, n % MH
                            r = P if m < MH - 1 else TAIL
                            act.wait_ge(*ring.moved(t, ("a", s, m)))
                            nc.scalar.activation(HH[s][0:r, m, :], hidden(s, m)[0:r, :], ACT.Copy).then_inc(*hid_high.up())

                        for n in range(STREAMS * MH):
                            s, m = n // MH, n % MH
                            r = P if m < MH - 1 else TAIL
                            if n == MH:
                                hidden_high(MH - 1)
                                high_nT(1)
                            act.wait_ge(*ring.ready(t, ("g", s, m)))
                            if n >= RB:
                                act.wait_ge(*ring.moved(t, ("a", (n - RB) // MH, (n - RB) % MH)))
                            nc.scalar.activation(GL[n % RB][0:r, :], ring.bank(("g", s, m))[0:r, :], ACT.Gelu, bias=bg[0:r, m:m + 1])\
                                .then_inc(*ring.out(("g", s, m)))
                            if n % MH:
                                hidden_high(n - 1)
                        hidden_high(STREAMS * MH - 1)
                        high_hT(t)
                        for s in two:
                            act.wait_ge(*ring.moved(t, ("w2", s, NT // 2 - 1)))
                            act.dma_start(yb[(t + PAIRS) * STREAMS + s], Z[s]).then_inc(stored[s].sem, 16)
                            act.wait_ge(*fin.at(t, s + 1))
                            act.dma_start(ob[p * STREAMS + s], X3[s]).then_inc(stored[s].sem, 16)
                        for x in (sq, root, probs, o_high, n_high, hid_high, ring.emptied["S"]):
                            x.close()
                for s in two:
                    act.wait_ge(*stored[s].at(LAYERS * PAIRS, 0))

            @block.tensor
            def _(pe):
                pe.wait_ge(consts, 4)
                pe.wait_ge(vones, 3 * STREAMS)

                def turn_y(t, fresh):
                    for s in two:
                        pe.wait_ge(*y_in[s].at(t + 1, 16))
                        for k in range(KD):
                            bank = ring.bank(("hT", s, k)) if fresh else ring.take(pe, t, ("hT", s, k))
                            for i in range(NT):
                                mm = nc.tensor.transpose(bank[:, i * P:(i + 1) * P], Y[s][:, i, k * P:(k + 1) * P], K.ident[:])
                            mm.then_inc(*ring.full.up())

                start_ring(pe, ring.full, hT_first, lambda: turn_y(-1, True))
                with pe.Fori(0, LAYERS) as l:
                    hold(pe, K.pe_passed, *w_split.at(l, 1))
                    with pe.Fori(0, PAIRS) as p:
                        t = l * PAIRS + p
                        full = lambda: ring.full.up()

                        def turn_heads(u):
                            for c in range(2):
                                pe.wait_ge(*(q_ready, k_ready)[c].at(t, u + 1))
                                bank = ring.take(pe, t, ("qkT", u, c))
                                src = T1[u % TB][:, c * LH:(c + 1) * LH, :].rearrange("p h d -> p (h d)")
                                for g in range(PAIRS_H):
                                    mm = nc.tensor.transpose(bank[:, g * P:(g + 1) * P], src[:, g * P:(g + 1) * P], K.ident[:])
                                mm.then_inc(*full())

                        def turn_o(s):
                            pe.wait_ge(*ring.moved(t, ("o", (s + 1) * LH - 1)))
                            for k in range(PAIRS_H):
                                bank = ring.take(pe, t, ("oT", s, k))
                                for i in range(NT):
                                    mm = nc.tensor.transpose(bank[:, i * P:(i + 1) * P], O[s][:, i, k * P:(k + 1) * P], K.ident[:])
                                mm.then_inc(*full())

                        def times_wo(s):
                            pe.wait_ge(*ring.moved(t, ("oT", s, PAIRS_H - 1)))
                            for g in range(NT // 2):
                                bank = ring.take(pe, t, ("wo", s, g))
                                for i in (2 * g, 2 * g + 1):
                                    for k in range(PAIRS_H):
                                        mm = split_matmul(nc, bank[:, i % 2 * D:(i % 2 + 1) * D], [x[s][:, k, i * P:(i + 1) * P] for x in (OT, OTL)],
                                                          [x[:, k, :] for x in Wo[0:2]], start=(k == 0), stop=(k == PAIRS_H - 1))
                                mm.then_inc(*full())

                        def shift_late(s):
                            pe.wait_ge(*ring.moved(t, ("wo", s, NT // 2 - 1)))
                            bank = ring.take(pe, t, ("late", s))
                            for i in range(NT):
                                mm = nc.tensor.matmul(bank[:, i * P:(i + 1) * P], shift[:], Y[s][:, i, P:D], start=True, stop=(i == 0))
                                if i:
                                    mm = nc.tensor.matmul(bank[:, i * P:(i + 1) * P], carry[:], Y[s][:, i - 1, P:D], start=False, stop=True)
                            mm.then_inc(*full())

                        def turn_normed(s):
                            pe.wait_ge(*ring.moved(t, ("late", s)))
                            for k in range(KD):
                                bank = ring.take(pe, t, ("nT", s, k))
                                for i in range(NT):
                                    mm = nc.tensor.transpose(bank[:, i * P:(i + 1) * P], O[s][:, i, k * P:(k + 1) * P], K.ident[:])
                                mm.then_inc(*full())

                        def times_w1(s, ms):
                            pe.wait_ge(*n_low.at(t, (s + 1) * KD))
                            for m in ms:
                                r = P if m < MH - 1 else TAIL
                                for name, at in (("g", HID), ("a", 0)):
                                    bank = ring.take(pe, t, (name, s, m))
                                    for k in range(KD):
                                        mm = split_matmul(nc, bank[0:r, :], [x[:, k, at + m * P:at + m * P + r] for x in W1[0:2]], hT(s, k),
                                                          start=(k == 0), stop=(k == KD - 1))
                                    mm.then_inc(*full())

                        def times_w2(s):
                            pe.wait_ge(*hid_low.at(t, (s + 1) * MH))
                            for g in range(NT // 2):
                                bank = ring.take(pe, t, ("w2", s, g))
                                for i in (2 * g, 2 * g + 1):
                                    for m in range(MH):
                                        r = P if m < MH - 1 else TAIL
                                        mm = split_matmul(nc, bank[:, i % 2 * D:(i % 2 + 1) * D],
                                                          (HH[s][0:r, m, i * P:(i + 1) * P], hidden(s, m, True)[0:r, i * P:(i + 1) * P]),
                                                          [x[0:r, m, :] for x in W2[0:2]], start=(m == 0), stop=(m == MH - 1))
                                mm.then_inc(*full())

                        for m in range(M8):
                            i, s = TILE_UNITS[m]
                            if i == 0:
                                pe.wait_ge(*ring.moved_before(t, ("hT", s, KD - 1)))
                            for c, name in enumerate("qkv"):
                                bank = ring.take(pe, t, (name, m))
                                for k in range(KD):
                                    mm = split_matmul(nc, bank[:], late(s, k, i), [x[:, k, c * INNER:(c + 1) * INNER] for x in Wqkv[0:2]],
                                                      start=(k == 0), stop=(k == KD - 1))
                                mm.then_inc(*full())
                            if m >= TLAG:
                                turn_heads(m - TLAG)
                        for k in range(U + VLAG):
                            if k < U:
                                h, s = HEAD_UNITS[k]
                                if h == 0:
                                    pe.wait_ge(*ring.moved(t, ("qkT", (s + 1) * NT - 1, 1)))
                                part, g = slice(h % 2 * LD, h % 2 * LD + LD), h // 2
                                for w in range(NT):
                                    if w % 2 == 0:
                                        bank = ring.take(pe, t, ("sim", k, w // 2))
                                    a = 1 if w == 0 else 0
                                    mm = nc.tensor.matmul(bank[:, (w % 2 * 2 + a) * P:(w % 2 * 2 + 2) * P], QKT[s][part, g, w * P:(w + 1) * P],
                                                          QKT[s][part, PAIRS_H + g, (w - 1 + a) * P:(w + 1) * P], start=True, stop=True)
                                    if w % 2:
                                        mm.then_inc(*full())
                            if k in TURN_AT:
                                turn_heads(TURN_AT[k])
                            if PLAG <= k < U + PLAG:
                                u = k - PLAG
                                pe.wait_ge(*probs.at(t, u + 1))
                                for w in range(NT):
                                    if w % 2 == 0:
                                        bank = ring.take(pe, t, ("pT", u, w // 2))
                                    for a in range(1 if w == 0 else 0, 2):
                                        c = w % 2 * 2 + a
                                        mm = nc.tensor.transpose(bank[:, c * P:(c + 1) * P], SM[u % RB][:, w, a, :], K.ident[:])
                                    if w % 2:
                                        mm.then_inc(*full())
                            if k >= VLAG:
                                u = k - VLAG
                                h, s = HEAD_UNITS[u]
                                pe.wait_ge(*ring.moved(t, ("pT", u, 0)))
                                pe.wait_ge(*ring.moved(t, ("pT", u, 1)))
                                bank = ring.take(pe, t, ("o", u))
                                for w in range(NT):
                                    for a in range(1 if w == 0 else 0, 2):
                                        mm = nc.tensor.matmul(bank[:, w * V1:(w + 1) * V1], PT[u % TR][:, w, a, :], V[s][:, w - 1 + a, h, :],
                                                              start=(a == 0 or w == 0), stop=(a == 1))
                                mm.then_inc(*full())
                            if k == OT_AT:
                                turn_o(0)
                            if k == WO_AT:
                                pe.wait_ge(*w_split.at(l, 2))
                                times_wo(0)
                            if k == LATE_AT:
                                shift_late(0)
                            if k == NT_AT:
                                turn_normed(0)
                        turn_o(1)
                        pe.wait_ge(*w_split.at(l, 3))
                        times_w1(0, HIDDEN_PARTS[0])
                        times_wo(1)
                        times_w1(0, HIDDEN_PARTS[1])
                        shift_late(1)
                        times_w1(0, HIDDEN_PARTS[2] + HIDDEN_PARTS[3])
                        turn_normed(1)
                        pe.wait_ge(*w2_split.at(l, 4))
                        times_w2(0)
                        times_w1(1, range(MH))
                        turn_y(t, False)
                        times_w2(1)
                        ring.close_pe()


def program(nc, A):

    class K:
        keep = Store(nc, "keep")

    def scratch(name, shape, dt=FP):
        return nc.dram_tensor(name, shape, dt, kind="Internal").ap()

    K.xnT_d, K.ctxT_d = scratch("xnT", (B, P, KD, S)), scratch("ctxT", (B, P, KD, S))
    K.m_d = scratch("running_max", (B * H, S))
    K.x2_d, K.x3_d = scratch("x2", (N + CAP, D)), scratch("x3", (N, D))
    K.y_d = scratch("y", ((LAYERS + 1) * N, D))
    K.xg_d, K.slots_d = scratch("expert_rows", (N + CAP, ROW)), scratch("slots", (E_, CAP), I32)
    with K.keep.stack:
        setup(nc, A, K)
        first = Store(nc, "first")
        with nc.cleanup_on_exit(), first.stack:
            K.gates = first.sb("gates", [2, NT, B, H])
            K.acol, K.nlcol = first.sb("a_columns", [NT, B, H]), first.sb("exp_columns", [NT, B, H])
            normalize_phase(nc, A, K)
            scan_phase(nc, A, K)
            mlstm_phase(nc, A, K)
        second = Store(nc, "second")
        with second.stack:
            K.R = second.sb("priorities", [E_, B, NT])
            K.idx = second.sb("slot_tokens", [E_, SLOTS], I32)
            router_phase(nc, A, K)
            routing_phase(nc, A, K)
            expert_phase(nc, A, K)
        retrieval_phase(nc, A, K)
        layer_phase(nc, A, K)


_INS = ["x", "ctx_1024", "g_xattn", "g_ffn", "L0_xattn_ig_kernel", "L0_xattn_ig_bias", "L0_xattn_fg_kernel",
        "L0_xattn_fg_bias", "L0_xattn_outnorm_weight", "L1_ffn_wqkv", "L1_ffn_q_scale", "L1_ffn_k_scale",
        "L1_ffn_wo", "L1_ffn_ln_g", "L1_ffn_ln_b", "L1_ffn_w1", "L1_ffn_b1", "L1_ffn_w2", "L1_ffn_b2"]


def position_tables():
    f = np.float32
    half = np.arange(0, LD, 2).astype(f)
    inv_freq = f(1) / f(10000.0) ** (half / f(LD))
    pos = np.arange(S).astype(f)
    freqs = pos[:, None] * inv_freq[None]
    freqs = np.concatenate([freqs, freqs], -1)
    base = (half + f(0.4 * LD)) / f(1.4 * LD)
    scale = base[None] ** ((pos - f(S // 2)) / f(64))[:, None]
    scale = np.concatenate([scale, scale], -1)
    sign = np.where(np.arange(LD) < LD // 2, -1, 1).astype(f)
    c, s = np.cos(freqs), np.sin(freqs) * sign
    return np.stack([c * scale * f(8), c / scale], 1).astype(f), np.stack([s * scale * f(8), s / scale], 1).astype(f)


def kernel(**inputs):
    import numpy as _np
    import concourse.bacc as _bacc
    from concourse.bass_utils import run_bass_kernel_spmd as _run

    nc = _bacc.Bacc("TRN2", target_bir_lowering=False, num_devices=1)
    arrays = {name: _np.ascontiguousarray(inputs[name]) for name in _INS}
    arrays["gate_wT"] = _np.ascontiguousarray(inputs["L0_ffn_gate_w"].T)
    arrays["w1T"] = _np.ascontiguousarray(inputs["L0_ffn_w1"].transpose(0, 2, 1))
    arrays["w2T"] = _np.ascontiguousarray(inputs["L0_ffn_w2"].transpose(0, 2, 1))
    arrays["cos"], arrays["sin"] = position_tables()
    A = {n: nc.dram_tensor(n, a.shape, mybir.dt.from_np(a.dtype), kind="ExternalInput").ap() for n, a in arrays.items()}
    A["out"] = nc.dram_tensor("out", (B, S, D), FP, kind="ExternalOutput").ap()
    program(nc, A)
    return _run(nc, [arrays], core_ids=[0]).results[0]["out"]
```
